# Optimizing a Trainium2 kernel written in Bass

```python
import numpy as np
import jax
import jax.numpy as jnp

def _softmax(x, axis=-1):
    return jax.nn.softmax(x, axis=axis)

def _gelu(x):
    return jax.nn.gelu(x, approximate=True)

def _silu(x):
    return jax.nn.silu(x)

def _sigmoid(x):
    return jax.nn.sigmoid(x)

def _layernorm(x, axis=-1, eps=1e-05):
    m = jnp.mean(x, axis=axis, keepdims=True)
    v = jnp.var(x, axis=axis, keepdims=True)
    return (x - m) / jnp.sqrt(v + eps)

def _scatter_add(tgt, idx, src, axis=0):
    return tgt.at[idx].add(src)

def _segment_sum(src, seg, n):
    return jax.ops.segment_sum(src, seg, n)
kernel_name = 'mk_flamingo_gated_d1_seqx_r8_ae7838'

def setup_inputs(seed: int=0):
    np.random.seed(seed)
    _w = jnp.asarray

    def _rec_inputs():
        import jax
        import jax.numpy as jnp
        _rk = jax.random.key(seed)
        x = 7.22e-05 + 1 * jax.random.normal(jax.random.fold_in(_rk, 1), (1, 1024, 128), jnp.float32)
        _lenS = 1024 - jax.random.randint(jax.random.fold_in(_rk, 7), (1,), 0, max(1, 1024 // 4) + 1, jnp.int32)
        _lenS2 = 6404 - jax.random.randint(jax.random.fold_in(_rk, 8), (1,), 0, max(1, 6404 // 4) + 1, jnp.int32)
        _ctx_1024P = jax.random.normal(jax.random.fold_in(_rk, 11), (1, 16, 128), jnp.float32)
        _ctx_1024c = jax.random.dirichlet(jax.random.fold_in(_rk, 511), 0.3 * jnp.ones((16,), jnp.float32), (1, 6404))
        _ctx_1024t = jnp.einsum('bsk,bkd->bsd', _ctx_1024c, _ctx_1024P)
        _ctx_1024t = _ctx_1024t * jax.lax.rsqrt(jnp.mean(jnp.square(_ctx_1024t)) + 1e-12) * 0.953939
        ctx_1024 = 4.13588e-05 + 0.999923 * (_ctx_1024t + 0.3 * jax.random.normal(jax.random.fold_in(_rk, 611), (1, 6404, 128), jnp.float32))
        _g = jax.random.normal(jax.random.fold_in(_rk, 9001), (2, 1), jnp.float32)
        _g = jnp.sign(_g) * jnp.maximum(jnp.abs(_g), 1.0) + (_g == 0) * 1.0
        g_xattn = _g[0]
        g_ffn = _g[1]
        return (x, ctx_1024, g_xattn, g_ffn)
    x, ctx_1024, g_xattn, g_ffn = _rec_inputs()

    def _L0_xattn_setup():
        import jax, jax.numpy as jnp
        import numpy as np
        N_HEAD = 16
        key = jax.random.key(seed)
        ks = jax.random.split(key, 5)
        b, l, d = (4, 256, 128)
        dh = d // N_HEAD
        return {'q': jax.random.normal(ks[0], (b, l, d), dtype=jnp.float32), 'kv': jax.random.normal(ks[1], (b, l, d), dtype=jnp.float32), 'Wq': jax.random.normal(ks[2], (d, d), dtype=jnp.float32) * 0.02, 'Wkv': jax.random.normal(ks[3], (2 * dh, d), dtype=jnp.float32) * 0.02, 'Wc': jax.random.normal(ks[4], (d, d), dtype=jnp.float32) * 0.02}
    _L0_xattn_all = _L0_xattn_setup()
    _L0_xattn_in = {k: v for k, v in _L0_xattn_all.items() if k in ('Wq', 'Wkv', 'Wc')}
    del _L0_xattn_all

    def _L0_ffn_setup():
        import jax, jax.numpy as jnp
        import numpy as np
        N_EMBD = 128
        N_EXPERTS = 8
        TOP_K = 2
        CAPACITY_FACTOR = 1.25
        key = jax.random.key(seed)
        ks = jax.random.split(key, 8)
        B, T, C, E, H = (8, 256, N_EMBD, N_EXPERTS, 4 * N_EMBD)
        w = lambda k, shape: jax.random.normal(k, shape, jnp.float32) * 0.02
        return {'x': jax.random.normal(ks[0], (B, T, C), jnp.float32), 'rW1': w(ks[1], (C, H)), 'rb1': jnp.zeros((H,), jnp.float32), 'rW2': w(ks[2], (H, H)), 'rb2': jnp.zeros((H,), jnp.float32), 'rW3': w(ks[3], (H, E)), 'rb3': jnp.zeros((E,), jnp.float32), 'eW1': w(ks[4], (E, C, H)), 'eb1': jnp.zeros((E, H), jnp.float32), 'eW2': w(ks[5], (E, H, C)), 'eb2': jnp.zeros((E, C), jnp.float32)}
    _L0_ffn_all = _L0_ffn_setup()
    _L0_ffn_in = {k: v for k, v in _L0_ffn_all.items() if k in ('rW1', 'rb1', 'rW2', 'rb2', 'rW3', 'rb3', 'eW1', 'eb1', 'eW2', 'eb2')}
    del _L0_ffn_all
    return {'x': x, 'ctx_1024': ctx_1024, 'g_xattn': g_xattn, 'g_ffn': g_ffn, 'L0_xattn_Wq': _L0_xattn_in['Wq'], 'L0_xattn_Wkv': _L0_xattn_in['Wkv'], 'L0_xattn_Wc': _L0_xattn_in['Wc'], 'L0_ffn_rW1': _L0_ffn_in['rW1'], 'L0_ffn_rb1': _L0_ffn_in['rb1'], 'L0_ffn_rW2': _L0_ffn_in['rW2'], 'L0_ffn_rb2': _L0_ffn_in['rb2'], 'L0_ffn_rW3': _L0_ffn_in['rW3'], 'L0_ffn_rb3': _L0_ffn_in['rb3'], 'L0_ffn_eW1': _L0_ffn_in['eW1'], 'L0_ffn_eb1': _L0_ffn_in['eb1'], 'L0_ffn_eW2': _L0_ffn_in['eW2'], 'L0_ffn_eb2': _L0_ffn_in['eb2']}

def reference(x, ctx_1024, g_xattn, g_ffn, L0_xattn_Wq, L0_xattn_Wkv, L0_xattn_Wc, L0_ffn_rW1, L0_ffn_rb1, L0_ffn_rW2, L0_ffn_rb2, L0_ffn_rW3, L0_ffn_rb3, L0_ffn_eW1, L0_ffn_eb1, L0_ffn_eW2, L0_ffn_eb2):
    import jax
    import jax.numpy as jnp

    def _L0_xattn_ref(q, kv, Wq, Wkv, Wc):
        import jax, jax.numpy as jnp
        import numpy as np
        N_HEAD = 16
        b, l, d = q.shape
        h = N_HEAD
        dh = d // h
        qp = jnp.einsum('bld,ed->ble', q, Wq)
        scores = jnp.einsum('bld,bmd->blm', qp, kv)
        idx = jnp.argmax(scores, axis=-1)
        mem = jnp.take_along_axis(kv, idx[..., None], axis=1)
        mkv = jnp.einsum('bld,ed->ble', mem, Wkv)
        mk, mv = jnp.split(mkv, 2, axis=-1)
        qh = qp.reshape(b, l, h, dh).transpose(0, 2, 1, 3)
        scale = 1.0 / np.sqrt(dh).astype(np.float32)
        logits = jnp.einsum('bhld,bmd->bhlm', qh, mk) * scale
        attn = jax.nn.softmax(logits, axis=-1)
        out = jnp.einsum('bhlm,bmd->bhld', attn, mv)
        out = out.transpose(0, 2, 1, 3).reshape(b, l, d)
        return jnp.einsum('bld,ed->ble', out, Wc)

    def _L0_ffn_ref(x, rW1, rb1, rW2, rb2, rW3, rb3, eW1, eb1, eW2, eb2):
        import jax, jax.numpy as jnp
        import numpy as np
        N_EMBD = 128
        N_EXPERTS = 8
        TOP_K = 2
        CAPACITY_FACTOR = 1.25
        B, T, C = x.shape
        E = rb3.shape[0]
        k = TOP_K
        capacity = int(T / E * CAPACITY_FACTOR)
        h = jax.nn.relu(x @ rW1 + rb1)
        h = jax.nn.relu(h @ rW2 + rb2)
        scales = jax.nn.softmax(h @ rW3 + rb3, axis=-1)
        topk_scales, topk_experts = jax.lax.top_k(scales, k)
        e_flat = topk_experts.reshape(B, T * k)
        onehot = jax.nn.one_hot(e_flat, E, dtype=jnp.int32)
        pos_excl = jnp.cumsum(onehot, axis=1) - onehot
        pos = jnp.take_along_axis(pos_excl, e_flat[..., None], axis=-1)[..., 0]
        keep = pos < capacity
        pos_c = jnp.where(keep, pos, capacity)
        b_idx = jnp.broadcast_to(jnp.arange(B)[:, None], (B, T * k))
        x_rep = jnp.repeat(x, k, axis=1)
        dispatched = jnp.zeros((E, B, capacity, C), x.dtype)
        dispatched = dispatched.at[e_flat, b_idx, pos_c].set(jnp.where(keep[..., None], x_rep, 0.0), mode='drop')
        hh = jax.nn.relu(jnp.einsum('ebnc,ech->ebnh', dispatched, eW1) + eb1[:, None, None, :])
        eout = jnp.einsum('ebnh,ehc->ebnc', hh, eW2) + eb2[:, None, None, :]
        gathered = eout[e_flat, b_idx, pos_c]
        gathered = jnp.where(keep[..., None], gathered, 0.0).reshape(B, T, k, C)
        out = jnp.sum(topk_scales[..., None] * gathered, axis=2)
        return out
    x = x + jnp.tanh(g_xattn[0]) * _L0_xattn_ref(_layernorm(x, axis=-1), ctx_1024, L0_xattn_Wq, L0_xattn_Wkv, L0_xattn_Wc)
    x = x + jnp.tanh(g_ffn[0]) * _L0_ffn_ref(_layernorm(x, axis=-1), L0_ffn_rW1, L0_ffn_rb1, L0_ffn_rW2, L0_ffn_rb2, L0_ffn_rW3, L0_ffn_rb3, L0_ffn_eW1, L0_ffn_eb1, L0_ffn_eW2, L0_ffn_eb2)
    return x

_drawn_inputs = setup_inputs


def setup_inputs(seed=0):
    import zlib

    import numpy as np

    out = dict(_drawn_inputs(seed))
    spreads = {'L0_ffn_rb1': (0.0, 0.8),
     'L0_ffn_rb2': (0.0, 0.744),
     'L0_ffn_rb3': (0.0, 0.539),
     'L0_ffn_eb1': (0.0, 0.8),
     'L0_ffn_eb2': (0.0, 0.8)}
    factors = {'ctx_1024': 2.842,
     'L0_xattn_Wq': 8.0,
     'L0_xattn_Wkv': 3.074,
     'L0_ffn_rW1': 7.707,
     'L0_ffn_rW2': 8.0,
     'L0_ffn_rW3': 6.71,
     'L0_ffn_eW1': 8.0,
     'L0_ffn_eW2': 7.899}
    for name, (base, spread) in spreads.items():
        noise = np.random.default_rng([zlib.crc32(name.encode()), seed]).standard_normal(out[name].shape)
        drawn = base * np.exp(spread * noise) if base else spread * noise
        out[name] = jnp.asarray(drawn.astype(out[name].dtype))
    for name, factor in factors.items():
        out[name] = (out[name] * factor).astype(out[name].dtype)
    return out
```

```python
from contextlib import ExitStack

import concourse.bass as bass
from concourse import mybir

F32 = mybir.dt.float32
F32R = mybir.dt.float32r
U32 = mybir.dt.uint32
ALU = mybir.AluOpType
ACT = mybir.ActivationFunctionType
AX = mybir.AxisListType

P = 128
D = 128
TOK = 1024
NT = TOK // P
M = 6404
NKV = -(-M // P)
TAIL = M - (NKV - 1) * P
H, DH = 16, 8
HALF = 512
NL = TOK // HALF
SCALE = 1.0 / (DH ** 0.5)
EPS = 1e-5
HID = 4 * D
KH = HID // P
E, TOPK = 8, 2
CAP = int(TOK / E * 1.25)
SLOTS = E * CAP
NS = SLOTS // P
NG = 4

CHUNK = 3 * HALF
CHUNKS = [(c, min(CHUNK, M - c)) for c in range(0, M, CHUNK)]
NCH = len(CHUNKS)
IDX_TOP = 8192.0


def program(nc, x, ctx_mem, g_xattn, g_ffn, Wq, Wkv, Wc, rW1, rb1, rW2, rb2, rW3, rb3, eW1, eb1, eW2, eb2, out):
    T = NT
    dispatched = nc.dram_tensor("dispatched", (SLOTS, D), F32).ap()
    expert_out = nc.dram_tensor("expert_out", (SLOTS, D), F32).ap()
    kv = ctx_mem.rearrange("a m d -> (a m) d")
    xf = x.rearrange("a l d -> (a l) d")
    outf = out.rearrange("a l d -> (a l) d")

    with ExitStack() as stack:
        def sb(name, shape, dt=F32):
            return stack.enter_context(nc.sbuf_tensor(name, shape, dt))

        def sem(name):
            return stack.enter_context(nc.semaphore(name))

        ps = stack.enter_context(nc.psum_tensor("ps", [P, 8 * HALF], F32))

        def bank(b, n=1):
            return ps[:, b * HALF:(b + n) * HALF]

        ident = sb("ident", [P, P])
        ones = sb("ones", [P, P])
        below = sb("below", [P, P])
        x_sb = sb("x_sb", [P, NT, D])
        consts = sb("consts", [P, HALF])
        C_WQ, C_WC, C_WKV, C_B, C_ROW = 0, 128, 256, 272, 320
        gates = sb("gates", [P, 2])
        eb2_row = sb("eb2_row", [1, E, D])
        xn = sb("xn", [P, NT, D])
        xnT = sb("xnT", [P, TOK])
        x1 = sb("x1", [P, NT, D])
        stats = sb("stats", [P, NT, 6])
        mv = sb("mv", [P, NT, 2])
        var_eps = sb("var_eps", [P, NT])
        rstd = sb("rstd", [P, NT])
        minus_half = sb("minus_half", [P, NT])
        iota8 = sb("iota8", [P, E])
        iota8_i = sb("iota8_i", [P, E], mybir.dt.int32)
        rw1_sb = sb("rw1_sb", [P, HID])
        rw2_sb = sb("rw2_sb", [P, KH, HID])
        rw3_sb = sb("rw3_sb", [P, KH, E])
        ew1_sb = sb("ew1_sb", [P, E, HID])
        ew2_sb = sb("ew2_sb", [P, E, KH, D])
        zero = sb("zero", [P, NS, D])
        disp = zero

        attention = ExitStack()

        def sba(name, shape, dt=F32):
            return attention.enter_context(nc.sbuf_tensor(name, shape, dt))

        kv_nat = sba("kv_nat", [P, NKV, D])
        shared = sba("shared", [P, H * TOK], F32R)
        kvt_hi = shared[:, 0:M]
        kvt_lo = shared[:, M:2 * M]
        q_rows = shared[0:34, :].rearrange("r (h l) -> r h l", h=H)
        wq_nat = sba("wq_nat", [P, D])
        wkv_nat = sba("wkv_nat", [2 * DH, D])
        wc_nat = sba("wc_nat", [P, D])
        bias_nat = sba("bias_nat", [E * KH + 2 * KH, P])
        row10 = sba("row10", [1, E + 2])
        wk4 = sba("wk4", [P, 4 * DH])
        q_hi = sba("q_hi", [P, TOK], F32R)
        q_lo = sba("q_lo", [P, TOK], F32R)
        offs = sba("offs", [P, NCH])
        offs_i = sba("offs_i", [P, NCH], mybir.dt.int32)
        part_i = sba("part_i", [P, 1], mybir.dt.int32)
        part_f = sba("part_f", [P, 1])
        best8 = sba("best8", [P, 2, NCH, 8])
        at8 = sba("at8", [P, 2, NCH, 8], U32)
        cand = sba("cand", [P, 2, NCH])
        cand2 = sba("cand2", [P, 2, NCH])
        top = sba("top", [P, 2])
        low = sba("low", [P, 2])
        idx = sba("idx", [P, NT], U32)
        mem = sba("mem", [P, 2, D])
        memT = sba("memT", [P, 2, P])
        sgn = sba("sgn", [32, 1])
        lo_rows = sba("lo_rows", [32, 1])
        k_a = sba("k_a", [32, P], F32R)
        k_b = sba("k_b", [32, P])
        k_rows = sba("k_rows", [34, TOK], F32R)
        v_ext = sba("v_ext", [P, NT, 32])
        mx = sba("mx", [P, NT, H])
        nm_hi = sba("nm_hi", [H, TOK], F32R)
        nm_lo = sba("nm_lo", [H, TOK], F32R)
        kv_flat = kv_nat[:, :, :].rearrange("p t d -> p (t d)")
        probs = kv_flat[:, 0:8 * HALF].rearrange("p (a j l) -> p a j l", a=2, j=4)
        av = kv_flat[:, 8 * HALF:(8 + NG) * HALF].rearrange("p (g l) -> p g l", g=NG)
        rden = sba("rden", [P, H])
        att = sba("att", [P, D])
        attT = sba("attT", [P, P])
        attention.close()

        h1 = sb("h1", [P, KH, TOK])
        h2 = sb("h2", [P, KH, TOK])
        r8 = sb("r8", [P, NT, E])
        m8 = sb("m8", [P, NT, 8])
        i8 = sb("i8", [P, NT, 8], U32)
        i8f = sb("i8f", [P, NT, TOPK])
        e8 = sb("e8", [P, NT, 8])
        nm8 = sb("nm8", [P, NT])
        sum8 = sb("sum8", [P, NT])
        rs8 = sb("rs8", [P, NT])
        pick = sb("pick", [P, TOPK, NT, E])
        mask = sb("mask", [P, NT, E])
        seen = sb("seen", [P, NT, E])
        pos = sb("pos", [P, NT, E])
        scr = sb("scr", [P, TOPK, NT, E])
        place = sb("place", [P, TOPK, NT])
        keep = sb("keep", [P, TOPK, NT])
        lost = sb("lost", [P, TOPK, NT])
        dest = sb("dest", [P, TOPK, NT])
        dest_put = sb("dest_put", [P, TOPK, NT], U32)
        dest_get = sb("dest_get", [P, TOPK, NT], U32)
        tmpw = sb("tmpw", [P, TOPK, NT])
        weight = sb("weight", [P, TOPK, NT])
        dT = sb("dT", [P, SLOTS])
        hh = sb("hh", [P, 2, KH, CAP])
        eo = sb("eo", [P, SLOTS // 80, D])
        got = sb("got", [P, TOPK, NT, D])
        acc = sb("acc", [P, NT, D])
        fin = sb("fin", [P, NT, D])

        s_x = sem("x_loaded"); s_kv = [sem(f"kv_loaded{j}") for j in range(6)]
        s_small = sem("small_loaded"); s_w = sem("weights_loaded")
        s_const = sem("pool_consts"); s_zero = sem("zero_written")
        s_cT = sem("consts_transposed"); s_cs = sem("consts_copied")
        s_ve = sem("variance_ready"); s_rstd = sem("rstd_ready"); s_xn = sem("xn_ready")
        s_xT = sem("xn_transposed"); s_xTs = sem("xnT_copied"); s_qp = sem("q_projected")
        s_qhi = sem("q_hi_ready"); s_qlo = sem("q_lo_ready")
        s_kvT = sem("kv_transposed"); s_khi = sem("kvt_hi_ready"); s_klo = sem("kvt_lo_ready")
        s_sc = sem("scores_ready"); s_scu = sem("scores_used"); s_idx = sem("idx_ready")
        s_mem = [sem("mem0_gathered"), sem("mem1_gathered")]
        s_mT = sem("mem_transposed"); s_mTs = sem("memT_copied"); s_mkv = sem("mkv_ready"); s_mkvu = sem("mkv_copied")
        s_qrows = sem("q_rows_loaded"); s_p1 = sem("logits_for_max_ready"); s_p1u = sem("logits_for_max_used")
        s_mxT = sem("max_transposed"); s_nm = sem("minus_max_ready"); s_nmrow = [sem(f"minus_max_row{L}") for L in range(NL)]
        s_lg = sem("logits_ready"); s_ex = sem("probs_ready"); s_avd = sem("av_done"); s_avc = sem("av_copied")
        s_avT = sem("av_transposed"); s_att = sem("att_ready"); s_attT = sem("att_transposed"); s_attTs = sem("attT_copied")
        s_wc = sem("projected"); s_x1 = sem("x1_ready")
        s_dve = sem("dve_step"); s_act = sem("act_step"); s_pool = sem("pool_step")
        s_h1 = sem("h1_products"); s_h1s = sem("h1_ready"); s_h2 = sem("h2_products"); s_h2s = sem("h2_ready")
        s_r = sem("router_logits"); s_rs = sem("router_logits_copied"); s_m8 = sem("router_sorted"); s_e8 = sem("router_exp")
        s_mask = sem("mask_ready"); s_pos = sem("positions_ready"); s_dest = sem("dest_ready")
        s_put = sem("tokens_put"); s_disp = sem("dispatched_loaded")
        s_dT = sem("dispatched_transposed"); s_dTs = sem("dT_copied")
        s_e1 = sem("expert_hidden_products"); s_e1s = sem("expert_hidden_ready")
        s_e2 = sem("expert_out_products"); s_e2s = sem("expert_out_ready"); s_eo = sem("expert_out_stored")
        s_got = sem("expert_rows_got"); s_fin = sem("rows_ready"); s_out = sem("out_stored")
        block = stack.enter_context(nc.Block())

        KV_PIECE = 10
        n_scores = NT * NCH

        @block.sync
        def _(sp):
            sp.dma_start(x_sb[:], xf.rearrange("(t p) d -> p t d", p=P)).then_inc(s_x, 16)
            for j in range(5):
                rows = kv[j * KV_PIECE * P:(j + 1) * KV_PIECE * P, :]
                sp.dma_start(kv_nat[:, j * KV_PIECE:(j + 1) * KV_PIECE, :],
                             rows.rearrange("(t p) d -> p t d", p=P)).then_inc(s_kv[j], 16)
            sp.dma_start(kv_nat[0:TAIL, NKV - 1, :], kv[(NKV - 1) * P:M, :]).then_inc(s_kv[5], 16)
            sp.dma_start(rw1_sb[:], rW1).then_inc(s_w, 16)
            sp.dma_start(rw2_sb[:], rW2.rearrange("(k p) n -> p k n", p=P)).then_inc(s_w, 16)
            sp.dma_start(rw3_sb[:], rW3.rearrange("(k p) n -> p k n", p=P)).then_inc(s_w, 16)
            sp.dma_start(ew1_sb[:], eW1.rearrange("e c h -> c e h")).then_inc(s_w, 16)
            sp.dma_start(ew2_sb[:], eW2.rearrange("e (k p) c -> p e k c", p=P)).then_inc(s_w, 16)
            sp.wait_ge(s_qlo, NL)
            sp.wait_ge(s_sc, n_scores)
            for r, src in enumerate((q_hi, q_lo, q_hi, q_lo)):
                for h in range(H):
                    sp.dma_start(q_rows[r * DH:(r + 1) * DH, h, :].bitcast(F32), src[h * DH:(h + 1) * DH, :].bitcast(F32)).then_inc(s_qrows, 16)
            for L in range(NL):
                sp.wait_ge(s_nm, 4 * (L + 1))
                cols = slice(L * HALF, (L + 1) * HALF)
                sp.dma_start(q_rows[32:33, :, cols].bitcast(F32), nm_hi[:, cols].bitcast(F32)).then_inc(s_nmrow[L], 16)
                sp.dma_start(q_rows[33:34, :, cols].bitcast(F32), nm_lo[:, cols].bitcast(F32)).then_inc(s_nmrow[L], 16)
            sp.wait_ge(s_put, 16 * TOPK * NT)
            sp.dma_start(disp[:], dispatched.rearrange("(t p) d -> p t d", p=P)).then_inc(s_disp, 16)
            for e in range(E):
                sp.wait_ge(s_e2s, e + 1)
                sp.dma_start(expert_out[e * CAP:(e + 1) * CAP, :].rearrange("(t p) d -> p t d", p=80),
                             eo[0:80, 2 * e:2 * e + 2, :]).then_inc(s_eo, 16)
            sp.wait_ge(s_fin, NT)
            sp.dma_start(outf.rearrange("(t p) d -> p t d", p=P), fin[:]).then_inc(s_out, 16)
            sp.wait_ge(s_out, 16)

        @block.gpsimd
        def _(pool):
            n = [0]

            def link(ins):
                n[0] += 1
                ins.then_inc(s_pool, 1)
                pool.wait_ge(s_pool, n[0])

            link(pool.memset(ident[:], 0.0))
            pool.affine_select(out=ident[:], in_=ident[:], compare_op=ALU.not_equal, fill=1.0, base=0,
                               pattern=[[-1, P]], channel_multiplier=1).then_inc(s_const, 1)
            link(pool.memset(ones[:], 1.0))
            pool.affine_select(out=below[:], in_=ones[:], compare_op=ALU.is_gt, fill=0.0, base=0,
                               pattern=[[1, P]], channel_multiplier=-1).then_inc(s_const, 1)
            link(pool.memset(minus_half[:], -0.5))
            link(pool.iota(offs_i[:], pattern=[[CHUNK, NCH]], base=-int(IDX_TOP), channel_multiplier=0))
            pool.tensor_copy(offs[:], offs_i[:]).then_inc(s_const, 1)
            link(pool.iota(iota8_i[:], pattern=[[1, E]], base=0, channel_multiplier=0))
            pool.tensor_copy(iota8[:], iota8_i[:]).then_inc(s_const, 1)
            link(pool.iota(part_i[:], pattern=[[0, 1]], base=0, channel_multiplier=1))
            link(pool.tensor_copy(part_f[:], part_i[:]))
            link(pool.tensor_scalar(lo_rows[:], part_f[0:32, :], float(2 * DH), None, ALU.is_ge))
            pool.tensor_scalar(sgn[:], lo_rows[:], -2.0, 1.0, ALU.mult, ALU.add).then_inc(s_const, 1)
            link(pool.memset(v_ext[:], 0.0))
            pool.memset(v_ext[:, :, DH:DH + 1], 1.0).then_inc(s_const, 1)
            link(pool.memset(zero[:], 0.0))
            pool.dma_start(dispatched.rearrange("(t p) d -> p t d", p=P), zero[:]).then_inc(s_zero, 16)
            pool.wait_ge(s_ve, 1)
            pool.tensor_tensor(rstd[:], var_eps[:], minus_half[:], ALU.pow).then_inc(s_rstd, 1)
            for i in range(NT):
                pool.wait_ge(s_idx, i + 1)
                if i >= 2:
                    pool.wait_ge(s_mT, i - 1)
                pool.indirect_dma_start(out=mem[:, i % 2, :], out_offset=None, in_=kv,
                                        in_offset=bass.IndirectOffsetOnAxis(ap=idx[:, i:i + 1], axis=0)
                                        ).then_inc(s_mem[i % 2], 16)
            pool.wait_ge(s_ve, 2)
            pool.tensor_tensor(rstd[:], var_eps[:], minus_half[:], ALU.pow).then_inc(s_rstd, 1)
            pool.wait_ge(s_dest, 1)
            pool.wait_ge(s_zero, 16)
            for k in range(TOPK):
                for i in range(NT):
                    pool.indirect_dma_start(out=dispatched, out_offset=bass.IndirectOffsetOnAxis(
                        ap=dest_put[:, k, i:i + 1], axis=0), in_=xn[:, i, :], in_offset=None,
                        bounds_check=SLOTS - 1, oob_is_err=False).then_inc(s_put, 16)
            pool.wait_ge(s_eo, 16 * E)
            for k in range(TOPK):
                for i in range(NT):
                    pool.indirect_dma_start(out=got[:, k, i, :], out_offset=None, in_=expert_out,
                                            in_offset=bass.IndirectOffsetOnAxis(ap=dest_get[:, k, i:i + 1], axis=0)
                                            ).then_inc(s_got, 16)

        @block.scalar
        def _(act):
            act.dma_start(wq_nat[:], Wq).then_inc(s_small, 16)
            act.dma_start(wkv_nat[:], Wkv).then_inc(s_small, 16)
            act.dma_start(wc_nat[:], Wc).then_inc(s_small, 16)
            act.dma_start(bias_nat[0:E * KH, :], eb1.rearrange("e (k p) -> (e k) p", p=P)).then_inc(s_small, 16)
            act.dma_start(bias_nat[E * KH:E * KH + KH, :], rb1.rearrange("(k p) -> k p", p=P)).then_inc(s_small, 16)
            act.dma_start(bias_nat[E * KH + KH:, :], rb2.rearrange("(k p) -> k p", p=P)).then_inc(s_small, 16)
            act.dma_start(row10[0:1, 0:E], rb3.rearrange("(a e) -> a e", a=1)).then_inc(s_small, 16)
            act.dma_start(row10[0:1, E:E + 1], g_xattn.rearrange("(a e) -> a e", a=1)).then_inc(s_small, 16)
            act.dma_start(row10[0:1, E + 1:E + 2], g_ffn.rearrange("(a e) -> a e", a=1)).then_inc(s_small, 16)
            act.dma_start(eb2_row[:], eb2.rearrange("(a e) d -> a e d", a=1)).then_inc(s_small, 16)
            act.wait_ge(s_cT, 1)
            act.copy(consts[:, 0:C_ROW + 10], ps[:, 7 * HALF:7 * HALF + C_ROW + 10]).then_inc(s_cs, 1)
            act.wait_ge(s_cs, 1)
            act.activation(gates[:], consts[:, C_ROW + E:C_ROW + E + 2], ACT.Tanh).then_inc(s_cs, 1)
            act.copy(wk4[:, :].rearrange("p (r d) -> p r d", r=4),
                     consts[:, C_WKV:C_WKV + DH].unsqueeze(1).broadcast_to([P, 4, DH])).then_inc(s_cs, 1)
            for n in range(NL):
                act.wait_ge(s_xT, n + 1)
                act.copy(xnT[:, n * HALF:(n + 1) * HALF], bank(6 + n)).then_inc(s_xTs, 1)
            for n in range(NL):
                act.wait_ge(s_qp, n + 1)
                act.copy(q_hi[:, n * HALF:(n + 1) * HALF], bank(6 + n)).then_inc(s_qhi, 1)
            for g in range(13):
                act.wait_ge(s_kvT, g + 1)
                w = min(HALF, M - g * HALF)
                act.copy(kvt_hi[:, g * HALF:g * HALF + w], ps[:, (g % 6) * HALF:(g % 6) * HALF + w]).then_inc(s_khi, 1)
            for i in range(NT):
                act.wait_ge(s_mT, i + 1)
                act.copy(memT[:, i % 2, :], ps[:, 6 * HALF:6 * HALF + P]).then_inc(s_mTs, 1)
            n = 0

            def copy_av(L, g):
                act.wait_ge(s_avd, (L * NG + g + 1) * T)
                if L and g == 0:
                    act.wait_ge(s_avT, 4 * L)
                act.copy(av[:, g, :], bank(6)).then_inc(s_avc, 1)

            for L in range(NL):
                for g in range(NG):
                    for t in range(T):
                        u = (L * NG + g) * T + t
                        if u >= 2:
                            act.wait_ge(s_avd, u - 1)
                        for j in range(4):
                            act.wait_ge(s_lg, n + 1)
                            act.activation(probs[:, u % 2, j, :], bank(4 + n % 2), ACT.Exp, scale=SCALE).then_inc(s_ex, 1)
                            n += 1
                        if t == 0 and g:
                            copy_av(L, g - 1)
                copy_av(L, NG - 1)
                for i in range(4 * L, 4 * L + 4):
                    act.wait_ge(s_attT, i + 1)
                    act.copy(attT[:], ps[:, 7 * HALF:7 * HALF + P]).then_inc(s_attTs, 1)
            for n in range(NL):
                act.wait_ge(s_xT, NL + n + 1)
                act.copy(xnT[:, n * HALF:(n + 1) * HALF], bank(6 + n)).then_inc(s_xTs, 1)
            n = 0
            for L in range(NL):
                for k in range(KH):
                    act.wait_ge(s_h1, n + 1)
                    act.activation(h1[:, k, L * HALF:(L + 1) * HALF], bank(n % 4), ACT.Relu,
                                   bias=consts[:, C_B + E * KH + k:C_B + E * KH + k + 1]).then_inc(s_h1s, 1)
                    n += 1
            n = 0
            for L in range(NL):
                for k in range(KH):
                    act.wait_ge(s_h2, n + 1)
                    act.activation(h2[:, k, L * HALF:(L + 1) * HALF], bank(n % 4), ACT.Relu,
                                   bias=consts[:, C_B + E * KH + KH + k:C_B + E * KH + KH + k + 1]).then_inc(s_h2s, 1)
                    n += 1
            for i in range(NT):
                act.wait_ge(s_m8, i + 1)
                act.activation(e8[:, i, :], m8[:, i, :], ACT.Exp, bias=nm8[:, i:i + 1],
                               accum_out=sum8[:, i:i + 1]).then_inc(s_e8, 1)
            for g in range(3):
                w = min(4, NS - 4 * g) * P
                act.wait_ge(s_dT, g + 1)
                act.copy(dT[:, g * HALF:g * HALF + w], ps[:, g * HALF:g * HALF + w]).then_inc(s_dTs, 1)
            for e in range(E):
                for k in range(KH):
                    if k == 0 and e >= 2:
                        act.wait_ge(s_e2, e - 1)
                    act.wait_ge(s_e1, KH * e + k + 1)
                    b = 3 + (KH * e + k) % 2
                    act.activation(hh[:, e % 2, k, :], ps[:, b * HALF:b * HALF + CAP], ACT.Relu,
                                   bias=consts[:, C_B + KH * e + k:C_B + KH * e + k + 1]).then_inc(s_e1s, 1)

        @block.vector
        def _(dve):
            n = [0]

            def link(ins):
                n[0] += 1
                ins.then_inc(s_dve, 1)
                dve.wait_ge(s_dve, n[0])

            def layernorm(src, phase):
                for i in range(NT):
                    if phase:
                        dve.wait_ge(s_x1, i + 1)
                    ins = dve.bn_stats(stats[:, i, :], src[:, i, :])
                    n[0] += 1
                    ins.then_inc(s_dve, 1)
                dve.wait_ge(s_dve, n[0])
                for i in range(NT):
                    ins = dve.bn_aggr(mv[:, i, :], stats[:, i, :])
                    n[0] += 1
                    ins.then_inc(s_dve, 1)
                dve.wait_ge(s_dve, n[0])
                dve.tensor_scalar(var_eps[:], mv[:, :, 1], EPS, None, ALU.add).then_inc(s_ve, 1)
                dve.wait_ge(s_rstd, phase + 1)
                for i in range(NT):
                    dve.tensor_scalar(xn[:, i, :], src[:, i, :], mv[:, i, 0:1], rstd[:, i:i + 1],
                                      ALU.subtract, ALU.mult).then_inc(s_xn, 1)

            dve.wait_ge(s_x, 16)
            dve.wait_ge(s_const, 1)
            layernorm(x_sb, 0)
            for h in range(NL):
                dve.wait_ge(s_qhi, h + 1)
                dve.tensor_tensor(q_lo[:, h * HALF:(h + 1) * HALF], bank(6 + h), q_hi[:, h * HALF:(h + 1) * HALF],
                                  ALU.subtract).then_inc(s_qlo, 1)
            dve.wait_ge(s_const, 6)
            dve.tensor_copy(k_rows[32:34, :].rearrange("r (t p) -> r t p", t=NT),
                            ones[32:34, :].unsqueeze(1).broadcast_to([2, NT, P])).then_inc(s_mkvu, 2)
            for g in range(13):
                dve.wait_ge(s_khi, g + 1)
                w = min(HALF, M - g * HALF)
                dve.tensor_tensor(kvt_lo[:, g * HALF:g * HALF + w], ps[:, (g % 6) * HALF:(g % 6) * HALF + w],
                                  kvt_hi[:, g * HALF:g * HALF + w], ALU.subtract).then_inc(s_klo, 1)

            def mkv_out(i):
                dve.wait_ge(s_mkv, i + 1)
                c = slice(i * P, (i + 1) * P)
                mk = ps[0:32, 6 * HALF + P:6 * HALF + 2 * P]
                link(dve.tensor_copy(k_a[:], mk))
                link(dve.tensor_scalar(k_b[:], k_a[:].bitcast(F32), sgn[:, 0:1], None, ALU.mult))
                dve.scalar_tensor_tensor(out=k_rows[0:32, c], in0=mk, scalar=lo_rows[:, 0:1], in1=k_b[:],
                                         op0=ALU.mult, op1=ALU.add).then_inc(s_mkvu, 1)
                dve.tensor_copy(v_ext[:, i, 0:DH], ps[:, 6 * HALF + 2 * P:6 * HALF + 2 * P + DH]).then_inc(s_mkvu, 1)

            for i in range(NT):
                b2 = i % 2
                for c, (_, w) in enumerate(CHUNKS):
                    m = i * NCH + c
                    sc = ps[:, (m % 2) * CHUNK:(m % 2) * CHUNK + w]
                    dve.wait_ge(s_sc, m + 1)
                    link(dve.max(best8[:, b2, c, :], sc))
                    dve.max_index(at8[:, b2, c, :], best8[:, b2, c, :], sc).then_inc(s_scu, 1)
                    if c == 1 and i >= 1:
                        mkv_out(i - 1)
                link(dve.tensor_reduce(top[:, b2:b2 + 1], best8[:, b2, :, 0], AX.X, ALU.max))
                dve.wait_ge(s_scu, (i + 1) * NCH)
                link(dve.tensor_tensor(cand[:, b2, :], at8[:, b2, :, 0], offs[:], ALU.add))
                link(dve.scalar_tensor_tensor(out=cand2[:, b2, :], in0=best8[:, b2, :, 0], scalar=top[:, b2:b2 + 1],
                                              in1=cand[:, b2, :], op0=ALU.is_equal, op1=ALU.mult))
                link(dve.tensor_reduce(low[:, b2:b2 + 1], cand2[:, b2, :], AX.X, ALU.min))
                dve.tensor_scalar(idx[:, i:i + 1], low[:, b2:b2 + 1], IDX_TOP, None, ALU.add).then_inc(s_idx, 1)
            mkv_out(NT - 1)

            for i in range(NT):
                for h in range(H):
                    m = i * H + h
                    dve.wait_ge(s_p1, m + 1)
                    dve.tensor_reduce(mx[:, i, h:h + 1], bank(2 * (m % 2), 2), AX.X, ALU.max).then_inc(s_p1u, 1)
                c = slice(i * P, (i + 1) * P)
                dve.wait_ge(s_mxT, i + 1)
                mt = ps[0:H, 7 * HALF:7 * HALF + P]
                link(dve.tensor_scalar(nm_hi[:, c], mt, -1.0, None, ALU.mult))
                dve.scalar_tensor_tensor(out=nm_lo[:, c], in0=mt, scalar=-1.0, in1=nm_hi[:, c].bitcast(F32),
                                         op0=ALU.mult, op1=ALU.subtract).then_inc(s_nm, 1)
            for i in range(NT):
                dve.wait_ge(s_avT, i + 1)
                a = bank(7).rearrange("p (h d) -> p h d", h=H)
                link(dve.reciprocal(rden[:], a[:, :, DH]))
                dve.tensor_tensor(att[:].rearrange("p (h d) -> p h d", h=H), a[:, :, 0:DH],
                                  rden[:].unsqueeze(2).broadcast_to([P, H, DH]), ALU.mult).then_inc(s_att, 1)
                dve.wait_ge(s_wc, i + 1)
                dve.scalar_tensor_tensor(out=x1[:, i, :], in0=ps[:, 7 * HALF:7 * HALF + D], scalar=gates[:, 0:1],
                                         in1=x_sb[:, i, :], op0=ALU.mult, op1=ALU.add).then_inc(s_x1, 1)
            layernorm(x1, 1)
            for i in range(NT):
                dve.wait_ge(s_r, NT)
                link(dve.tensor_tensor(r8[:, i, :], ps[:, 4 * HALF + i * E:4 * HALF + (i + 1) * E],
                                       consts[:, C_ROW:C_ROW + E], ALU.add))
                link(dve.max(m8[:, i, :], r8[:, i, :]))
                link(dve.max_index(i8[:, i, :], m8[:, i, :], r8[:, i, :]))
                dve.tensor_scalar(nm8[:, i:i + 1], m8[:, i, 0:1], -1.0, None, ALU.mult).then_inc(s_m8, 1)
            link(dve.tensor_copy(i8f[:], i8[:, :, 0:TOPK]))
            for k in range(TOPK):
                link(dve.tensor_tensor(pick[:, k], iota8[:].unsqueeze(1).broadcast_to([P, NT, E]),
                                       i8f[:, :, k:k + 1].broadcast_to([P, NT, E]), ALU.is_equal))
            link(dve.tensor_tensor(mask[:], pick[:, 0], pick[:, 1], ALU.add))
            link(dve.memset(seen[:, 0, :], 0.0))
            for i in range(1, NT):
                link(dve.tensor_tensor(seen[:, i, :], seen[:, i - 1, :], mask[:, i - 1, :], ALU.add))
            dve.sem_inc(s_mask, 1)
            dve.wait_ge(s_pos, 1)
            link(dve.tensor_copy(pos[:], ps[:, 5 * HALF:5 * HALF + NT * E].rearrange("p (t e) -> p t e", t=NT)))
            for k in range(TOPK):
                link(dve.tensor_tensor(scr[:, k], pick[:, k], pos[:], ALU.mult))
            link(dve.tensor_reduce(place[:], scr[:], AX.X, ALU.add))
            link(dve.tensor_scalar(keep[:], place[:], float(CAP), None, ALU.is_lt))
            link(dve.tensor_scalar(lost[:], keep[:], -float(SLOTS), float(SLOTS), ALU.mult, ALU.add))
            for k in range(TOPK):
                link(dve.scalar_tensor_tensor(out=dest[:, k, :], in0=i8f[:, :, k], scalar=float(CAP),
                                              in1=place[:, k, :], op0=ALU.mult, op1=ALU.add))
            link(dve.tensor_tensor(dest_put[:], dest[:], lost[:], ALU.add))
            dve.sem_inc(s_dest, 1)
            link(dve.tensor_tensor(dest_get[:], dest[:], keep[:], ALU.mult))
            dve.wait_ge(s_e8, NT)
            link(dve.reciprocal(rs8[:], sum8[:]))
            link(dve.tensor_scalar(rs8[:], rs8[:], gates[:, 1:2], None, ALU.mult))
            for k in range(TOPK):
                link(dve.tensor_tensor(tmpw[:, k, :], e8[:, :, k], rs8[:], ALU.mult))
            link(dve.tensor_tensor(weight[:], tmpw[:], keep[:], ALU.mult))
            dve.sem_inc(s_dest, 1)
            for e in range(E):
                dve.wait_ge(s_e2, e + 1)
                b = 5 + e % 2
                dve.tensor_copy(eo[0:80, 2 * e:2 * e + 2, :], ps[0:80, b * HALF:b * HALF + 2 * D]).then_inc(s_e2s, 1)
            dve.wait_ge(s_got, 16 * TOPK * NT)
            for i in range(NT):
                link(dve.scalar_tensor_tensor(out=acc[:, i, :], in0=got[:, 0, i, :], scalar=weight[:, 0, i:i + 1],
                                              in1=x1[:, i, :], op0=ALU.mult, op1=ALU.add))
                dve.scalar_tensor_tensor(out=fin[:, i, :], in0=got[:, 1, i, :], scalar=weight[:, 1, i:i + 1],
                                         in1=acc[:, i, :], op0=ALU.mult, op1=ALU.add).then_inc(s_fin, 1)

        @block.tensor
        def _(pe):
            b7 = 7 * HALF
            pe.wait_ge(s_const, 2)
            pe.wait_ge(s_small, 16 * 10)
            pe.transpose(ps[:, b7 + C_WQ:b7 + C_WQ + D], wq_nat[:], ident[:])
            pe.transpose(ps[:, b7 + C_WC:b7 + C_WC + D], wc_nat[:], ident[:])
            pe.transpose(ps[:, b7 + C_WKV:b7 + C_WKV + 2 * DH], wkv_nat[:], ident[0:2 * DH, 0:2 * DH])
            nb = E * KH + 2 * KH
            pe.transpose(ps[:, b7 + C_B:b7 + C_B + nb], bias_nat[:], ident[0:nb, 0:nb])
            pe.matmul(ps[:, b7 + C_B + nb:b7 + C_ROW], ones[0:1, :], ones[0:1, 0:C_ROW - C_B - nb], start=True, stop=True)
            pe.matmul(ps[:, b7 + C_ROW:b7 + C_ROW + 10], ones[0:1, :], row10[:], start=True, stop=True).then_inc(s_cT, 1)
            pe.wait_ge(s_cs, 1)
            for half in range(NL):
                pe.wait_ge(s_xn, 4 * (half + 1))
                for t in range(4):
                    last = pe.transpose(ps[:, (6 + half) * HALF + t * P:(6 + half) * HALF + (t + 1) * P],
                                        xn[:, 4 * half + t, :], ident[:])
                last.then_inc(s_xT, 1)
            for half in range(NL):
                pe.wait_ge(s_xTs, half + 1)
                pe.matmul(bank(6 + half), consts[:, C_WQ:C_WQ + D], xnT[:, half * HALF:(half + 1) * HALF],
                          start=True, stop=True).then_inc(s_qp, 1)
            for g in range(13):
                if g >= 6:
                    pe.wait_ge(s_klo, g - 5)
                for t in range(4 * g, min(4 * g + 4, NKV)):
                    pe.wait_ge(s_kv[t // KV_PIECE], 16)
                    r = P if t < NKV - 1 else TAIL
                    col = (g % 6) * HALF + (t - 4 * g) * P
                    last = pe.transpose(ps[:, col:col + r], kv_nat[0:r, t, :], ident[0:r, 0:r])
                last.then_inc(s_kvT, 1)

            def lookup(i):
                pe.wait_ge(s_mem[i % 2], 16 * (i // 2 + 1))
                if i >= 1:
                    pe.wait_ge(s_mkvu, 2 + 2 * i)
                pe.transpose(ps[:, 6 * HALF:6 * HALF + P], mem[:, i % 2, :], ident[:]).then_inc(s_mT, 1)
                pe.wait_ge(s_mTs, i + 1)
                pe.wait_ge(s_cs, 3)
                pe.matmul(ps[0:32, 6 * HALF + P:6 * HALF + 2 * P], wk4[:], memT[:, i % 2, :], start=True, stop=True)
                pe.matmul(ps[:, 6 * HALF + 2 * P:6 * HALF + 2 * P + DH], memT[:, i % 2, :],
                          consts[:, C_WKV + DH:C_WKV + 2 * DH], start=True, stop=True).then_inc(s_mkv, 1)

            pe.wait_ge(s_klo, 13)
            pe.wait_ge(s_qlo, NL)
            for i in range(NT):
                q_h, q_l = q_hi[:, i * P:(i + 1) * P], q_lo[:, i * P:(i + 1) * P]
                for c, (start, w) in enumerate(CHUNKS):
                    m = i * NCH + c
                    if m >= 2:
                        pe.wait_ge(s_scu, m - 1)
                    for s in range(0, w, HALF):
                        k = min(HALF, w - s)
                        o = ps[:, (m % 2) * CHUNK + s:(m % 2) * CHUNK + s + k]
                        hi, lo = kvt_hi[:, start + s:start + s + k], kvt_lo[:, start + s:start + s + k]
                        pe.matmul(o, q_h, hi, start=True, stop=False)
                        pe.matmul(o, q_h, lo, start=False, stop=False)
                        last = pe.matmul(o, q_l, hi, start=False, stop=True)
                    last.then_inc(s_sc, 1)
                    if c == 1 and i >= 1:
                        lookup(i - 1)
            lookup(NT - 1)

            pe.wait_ge(s_qrows, 16 * 4 * H)
            pe.wait_ge(s_mkvu, 2 + 2 * NT)
            for i in range(NT):
                for h in range(H):
                    m = i * H + h
                    if m >= 2:
                        pe.wait_ge(s_p1u, m - 1)
                    for c in range(2):
                        last = pe.matmul(bank(2 * (m % 2) + c), q_rows[0:32, h, i * P:(i + 1) * P],
                                         k_rows[0:32, c * HALF:(c + 1) * HALF], start=True, stop=True)
                    last.then_inc(s_p1, 1)
                pe.wait_ge(s_p1u, (i + 1) * H)
                if i:
                    pe.wait_ge(s_nm, i)
                pe.transpose(ps[0:H, b7:b7 + P], mx[:, i, :], ident[:]).then_inc(s_mxT, 1)
            pe.wait_ge(s_nm, NT)
            n = 0
            for L in range(NL):
                pe.wait_ge(s_nmrow[L], 32)
                cols = slice(L * HALF, (L + 1) * HALF)
                units = [(g, t) for g in range(NG) for t in range(T)]

                def weigh(g, t):
                    u = (L * NG + g) * T + t
                    pe.wait_ge(s_ex, 4 * (u + 1))
                    if t == 0 and L * NG + g:
                        pe.wait_ge(s_avc, L * NG + g)
                    for j in range(4):
                        last = pe.matmul(ps[32 * j:32 * j + 32, 6 * HALF:7 * HALF], v_ext[:, t, :], probs[:, u % 2, j, :],
                                         start=(t == 0), stop=(t == T - 1), skip_group_check=True)
                    last.then_inc(s_avd, 1)

                for k, (g, t) in enumerate(units):
                    for j in range(4):
                        if n >= 2:
                            pe.wait_ge(s_ex, n - 1)
                        pe.matmul(bank(4 + n % 2), k_rows[0:34, t * P:(t + 1) * P], q_rows[0:34, 4 * g + j, cols],
                                  start=True, stop=True).then_inc(s_lg, 1)
                        n += 1
                    if k:
                        weigh(*units[k - 1])
                weigh(*units[-1])
                pe.wait_ge(s_avc, NG * (L + 1))
                for i in range(4 * L, 4 * L + 4):
                    if i:
                        pe.wait_ge(s_x1, i)
                    for g in range(NG):
                        last = pe.transpose(ps[:, b7 + g * P:b7 + (g + 1) * P], av[:, g, (i % 4) * P:(i % 4 + 1) * P], ident[:])
                    last.then_inc(s_avT, 1)
                    pe.wait_ge(s_att, i + 1)
                    pe.transpose(ps[:, b7:b7 + P], att[:], ident[:]).then_inc(s_attT, 1)
                    pe.wait_ge(s_attTs, i + 1)
                    pe.matmul(ps[:, b7:b7 + D], attT[:], consts[:, C_WC:C_WC + D], start=True, stop=True).then_inc(s_wc, 1)

            for half in range(NL):
                pe.wait_ge(s_xn, NT + 4 * (half + 1))
                for t in range(4):
                    last = pe.transpose(ps[:, (6 + half) * HALF + t * P:(6 + half) * HALF + (t + 1) * P],
                                        xn[:, 4 * half + t, :], ident[:])
                last.then_inc(s_xT, 1)
            pe.wait_ge(s_w, 16 * 5)
            n = 0
            for L in range(NL):
                pe.wait_ge(s_xTs, NL + L + 1)
                for k in range(KH):
                    if n >= 4:
                        pe.wait_ge(s_h1s, n - 3)
                    pe.matmul(bank(n % 4), rw1_sb[:, k * P:(k + 1) * P], xnT[:, L * HALF:(L + 1) * HALF],
                              start=True, stop=True).then_inc(s_h1, 1)
                    n += 1
            n = 0
            for L in range(NL):
                for k in range(KH):
                    pe.wait_ge(s_h1s, NL * KH if n >= 4 else KH + max(0, n + 1))
                    if n >= 4:
                        pe.wait_ge(s_h2s, n - 3)
                    for c in range(KH):
                        last = pe.matmul(bank(n % 4), rw2_sb[:, c, k * P:(k + 1) * P], h1[:, c, L * HALF:(L + 1) * HALF],
                                         start=(c == 0), stop=(c == KH - 1))
                    last.then_inc(s_h2, 1)
                    n += 1
            for i in range(NT):
                pe.wait_ge(s_h2s, KH * (i // 4 + 1))
                for c in range(KH):
                    last = pe.matmul(ps[:, 4 * HALF + i * E:4 * HALF + (i + 1) * E], h2[:, c, i * P:(i + 1) * P],
                                     rw3_sb[:, c, :], start=(c == 0), stop=(c == KH - 1))
                last.then_inc(s_r, 1)
            pe.wait_ge(s_mask, 1)
            pe.matmul(ps[:, 5 * HALF:5 * HALF + NT * E], below[:], mask[:].rearrange("p t e -> p (t e)"),
                      start=True, stop=False)
            pe.matmul(ps[:, 5 * HALF:5 * HALF + NT * E], ones[:], seen[:].rearrange("p t e -> p (t e)"),
                      start=False, stop=True).then_inc(s_pos, 1)
            pe.wait_ge(s_disp, 16)
            for g in range(3):
                for t in range(4 * g, min(4 * g + 4, NS)):
                    last = pe.transpose(ps[:, t * P:(t + 1) * P], disp[:, t, :], ident[:])
                last.then_inc(s_dT, 1)
            pe.wait_ge(s_dTs, 3)

            def expert_out_rows(e):
                for half in range(2):
                    b = 5 + e % 2
                    o = ps[0:80, b * HALF + half * D:b * HALF + (half + 1) * D]
                    if half == 0:
                        pe.wait_ge(s_e1s, KH * (e + 1))
                        if e >= 2:
                            pe.wait_ge(s_e2s, e - 1)
                    for k in range(KH):
                        pe.matmul(o, hh[:, e % 2, k, half * 80:half * 80 + 80], ew2_sb[:, e, k, :],
                                  start=(k == 0), stop=False)
                    last = pe.matmul(o, ones[0:1, 0:80], eb2_row[0:1, e, :], start=False, stop=True)
                last.then_inc(s_e2, 1)

            for e in range(E):
                for k in range(KH):
                    m = KH * e + k
                    if m >= 2:
                        pe.wait_ge(s_e1s, m - 1)
                    b = 3 + m % 2
                    pe.matmul(ps[:, b * HALF:b * HALF + CAP], ew1_sb[:, e, k * P:(k + 1) * P], dT[:, e * CAP:(e + 1) * CAP],
                              start=True, stop=True).then_inc(s_e1, 1)
                if e:
                    expert_out_rows(e - 1)
            expert_out_rows(E - 1)


_INS = ['x', 'ctx_1024', 'g_xattn', 'g_ffn', 'L0_xattn_Wq', 'L0_xattn_Wkv', 'L0_xattn_Wc', 'L0_ffn_rW1', 'L0_ffn_rb1',
        'L0_ffn_rW2', 'L0_ffn_rb2', 'L0_ffn_rW3', 'L0_ffn_rb3', 'L0_ffn_eW1', 'L0_ffn_eb1', 'L0_ffn_eW2', 'L0_ffn_eb2']


def kernel(**inputs):
    import numpy as _np
    import concourse.bacc as _bacc
    from concourse import mybir as _mybir
    from concourse.bass_utils import run_bass_kernel_spmd as _run

    nc = _bacc.Bacc("TRN2", target_bir_lowering=False, num_devices=1)
    arrays, args = {}, []
    for name in _INS:
        a = _np.ascontiguousarray(inputs[name])
        arrays[f"in_{name}_dram"] = a
        args.append(nc.dram_tensor(f"in_{name}_dram", a.shape, _mybir.dt.from_np(a.dtype), kind="ExternalInput").ap())
    args.append(nc.dram_tensor("out_0_dram", (1, TOK, D), _mybir.dt.float32, kind="ExternalOutput").ap())
    program(nc, *args)
    r = _run(nc, [arrays], core_ids=[0])
    return r.results[0]["out_0_dram"]
```

```python
from contextlib import ExitStack

import concourse.bass as bass
from concourse import mybir

F32 = mybir.dt.float32
F32R = mybir.dt.float32r
U32 = mybir.dt.uint32
ALU = mybir.AluOpType
ACT = mybir.ActivationFunctionType
AX = mybir.AxisListType

P = 128
D = 128
TOK = 1024
NT = TOK // P
M = 6404
NKV = -(-M // P)
TAIL = M - (NKV - 1) * P
H, DH = 16, 8
HALF = 512
NL = TOK // HALF
SCALE = 1.0 / (DH ** 0.5)
EPS = 1e-5
HID = 4 * D
KH = HID // P
E, TOPK = 8, 2
CAP = int(TOK / E * 1.25)
SLOTS = E * CAP
NS = SLOTS // P
NG, GH = 4, 4
RS = 32
W = 256
NQ = TOK // W
TQ = W // P
HB = HALF // W

CHUNK = 3 * HALF
CHUNKS = [(c, min(CHUNK, M - c)) for c in range(0, M, CHUNK)]
NCH = len(CHUNKS)
NKG = -(-M // HALF)
IDX_TOP = 8192.0


def program(nc, x, ctx_mem, g_xattn, g_ffn, Wq, Wkv, Wc, rW1, rb1, rW2, rb2, rW3, rb3, eW1, eb1, eW2, eb2, out):
    dispatched = nc.dram_tensor("dispatched", (SLOTS, D), F32).ap()
    expert_out = nc.dram_tensor("expert_out", (SLOTS, D), F32).ap()
    kv = ctx_mem.rearrange("a m d -> (a m) d")
    xf = x.rearrange("a l d -> (a l) d")
    outf = out.rearrange("a l d -> (a l) d")

    with ExitStack() as stack:
        def sb(name, shape, dt=F32):
            return stack.enter_context(nc.sbuf_tensor(name, shape, dt))

        def sem(name):
            return stack.enter_context(nc.semaphore(name))

        ps = stack.enter_context(nc.psum_tensor("ps", [P, 8 * HALF], F32))

        def bank(b, n=1):
            return ps[:, b * HALF:(b + n) * HALF]

        ident = sb("ident", [P, P])
        ones = sb("ones", [P, P])
        below = sb("below", [P, P])
        x_sb = sb("x_sb", [P, NT, D])
        consts = sb("consts", [P, HALF])
        C_WQ, C_WC, C_WKV, C_B, C_ROW = 0, 128, 256, 272, 320
        gates = sb("gates", [P, 2])
        eb2_row = sb("eb2_row", [1, E, D])
        xn = sb("xn", [P, NT, D])
        xnT = sb("xnT", [P, TOK])
        x1 = sb("x1", [P, NT, D])
        stats = sb("stats", [P, NT, 6])
        mv = sb("mv", [P, NT, 2])
        var_eps = sb("var_eps", [P, NT])
        rstd = sb("rstd", [P, NT])
        minus_half = sb("minus_half", [P, NT])
        iota8 = sb("iota8", [P, E])
        iota8_i = sb("iota8_i", [P, E], mybir.dt.int32)
        rw1_sb = sb("rw1_sb", [P, HID])
        rw2_sb = sb("rw2_sb", [P, KH, HID])
        rw3_sb = sb("rw3_sb", [P, KH, E])
        ew1_sb = sb("ew1_sb", [P, E, HID])
        ew2_sb = sb("ew2_sb", [P, E, KH, D])
        zero = sb("zero", [P, NS, D])
        disp = zero

        attention = ExitStack()

        def sba(name, shape, dt=F32):
            return attention.enter_context(nc.sbuf_tensor(name, shape, dt))

        kv_nat = sba("kv_nat", [P, NKV, D])
        shared = sba("shared", [P, 2 * M], F32R)
        kvt_hi = shared[:, 0:M]
        kvt_lo = shared[:, M:2 * M]
        wq_nat = sba("wq_nat", [P, D])
        wkv_nat = sba("wkv_nat", [2 * DH, D])
        wc_nat = sba("wc_nat", [P, D])
        bias_nat = sba("bias_nat", [E * KH + 2 * KH, P])
        row10 = sba("row10", [1, E + 2])
        wq_rep = sba("wq_rep", [P, H, RS])
        wk_rep = sba("wk_rep", [P, GH, RS])
        q_rows = sba("q_rows", [P, NG, TOK], F32R)
        k_blk = sba("k_blk", [P, GH, TOK], F32R)
        q_hi = sba("q_hi", [P, TOK], F32R)
        q_lo = sba("q_lo", [P, TOK], F32R)
        offs = sba("offs", [P, NCH])
        offs_i = sba("offs_i", [P, NCH], mybir.dt.int32)
        part_i = sba("part_i", [P, 1], mybir.dt.int32)
        part_f = sba("part_f", [P, 1])
        best8 = sba("best8", [P, 2, NCH, 8])
        at8 = sba("at8", [P, 2, NCH, 8], U32)
        cand = sba("cand", [P, 2, NCH])
        cand2 = sba("cand2", [P, 2, NCH])
        top = sba("top", [P, 2])
        low = sba("low", [P, 2])
        idx = sba("idx", [P, NT], U32)
        idxf = sba("idxf", [P, NT])
        diag = sba("diag", [P, P])
        id_row = sba("id_row", [P, TOK])
        own = sba("own", [P, P])
        not_earlier = sba("not_earlier", [P, P])
        junk = sba("junk", [P, TOK], mybir.dt.bfloat16)
        hits_a = sba("hits_a", [P, NT])
        hits_b = sba("hits_b", [P, NT])
        first = sba("first", [P, NT + 1])
        seen_f = sba("seen_f", [P, NT + 1])
        n_rows = sba("n_rows", [1, 1], mybir.dt.int32)
        slot = sba("slot", [P, NT])
        above = sba("above", [P, NT, NT])
        slot_t = sba("slot_t", [P, NT])
        slot_p = sba("slot_p", [P, NT])
        iota_i = sba("iota_i", [P, P], mybir.dt.int32)
        iota1 = sba("iota1", [P, P])
        thr = sba("thr", [P, NT])
        pick_t = sba("pick_t", [P, NT, 2, NT])
        pad = sba("pad", [P, NT])
        valid = sba("valid", [P, NT])
        row_f = sba("row_f", [P, NT])
        row_u = sba("row_u", [P, NT], U32)
        uses = sba("uses", [P, NT])
        weight_v = sba("weight_v", [P, NT])
        q_a = sba("q_a", [P, HALF], F32R)
        k_a = sba("k_a", [P, 2, P], F32R)
        rr = sba("rr", [P, 1])
        ge = sba("ge", [P, 8])
        q_low = sba("q_low", [P, 1])
        q_sgn = sba("q_sgn", [P, 1])
        k_low = sba("k_low", [P, 1])
        k_sgn = sba("k_sgn", [P, 1])
        k_one = sba("k_one", [P, 1])
        v_ext = sba("v_ext", [P, NT, RS])
        mx = sba("mx", [P, NT, H])
        nm_hi = shared[0:H, 0:TOK]
        nm_lo = shared[0:H, TOK:2 * TOK]
        kv_flat = kv_nat[:, :, :].rearrange("p t d -> p (t d)")
        probs = kv_flat[:, 0:8 * W].rearrange("p (a j l) -> p a j l", a=2, j=GH)
        av = kv_flat[:, 8 * W:16 * W].rearrange("p (a g l) -> p a g l", a=2, g=NG)
        pick_p = kv_flat[:, 0:NT * P].rearrange("p (t k) -> p t k", t=NT)
        mem = kv_flat[:, 16 * W:16 * W + TOK].rearrange("p (t d) -> p t d", t=NT)
        memT = kv_flat[:, 16 * W + TOK:16 * W + 2 * TOK]
        rden = sba("rden", [P, H])
        att = sba("att", [P, D])
        attT = sba("attT", [P, P])
        attention.close()

        h1 = sb("h1", [P, KH, TOK])
        h2 = sb("h2", [P, KH, TOK])
        r8 = sb("r8", [P, NT, E])
        m8 = sb("m8", [P, NT, 8])
        i8 = sb("i8", [P, NT, 8], U32)
        i8f = sb("i8f", [P, NT, TOPK])
        e8 = sb("e8", [P, NT, 8])
        nm8 = sb("nm8", [P, NT])
        sum8 = sb("sum8", [P, NT])
        rs8 = sb("rs8", [P, NT])
        pick = sb("pick", [P, TOPK, NT, E])
        mask = sb("mask", [P, NT, E])
        seen = sb("seen", [P, NT, E])
        pos = sb("pos", [P, NT, E])
        scr = sb("scr", [P, TOPK, NT, E])
        place = sb("place", [P, TOPK, NT])
        keep = sb("keep", [P, TOPK, NT])
        lost = sb("lost", [P, TOPK, NT])
        dest = sb("dest", [P, TOPK, NT])
        dest_put = sb("dest_put", [P, TOPK, NT], U32)
        dest_get = sb("dest_get", [P, TOPK, NT], U32)
        tmpw = sb("tmpw", [P, TOPK, NT])
        weight = sb("weight", [P, TOPK, NT])
        dT = sb("dT", [P, SLOTS])
        hh = sb("hh", [P, 2, KH, CAP])
        eo = sb("eo", [P, SLOTS // 80, D])
        got = sb("got", [P, TOPK, NT, D])
        acc = sb("acc", [P, NT, D])
        fin = sb("fin", [P, NT, D])

        s_x = sem("x_loaded"); s_kv = [sem(f"kv_loaded{j}") for j in range(6)]
        s_small = sem("small_loaded"); s_wql = sem("wq_loaded"); s_w = sem("weights_loaded")
        s_const = sem("pool_consts"); s_zero = sem("zero_written")
        s_cT = sem("consts_transposed"); s_cs = sem("consts_copied")
        s_ve = sem("variance_ready"); s_rstd = sem("rstd_ready"); s_xn = sem("xn_ready")
        s_xT = sem("xn_transposed"); s_xTs = sem("xnT_copied"); s_qp = sem("q_projected")
        s_qhi = sem("q_hi_ready"); s_qlo = sem("q_lo_ready")
        s_kvT = sem("kv_transposed"); s_khi = sem("kvt_hi_ready"); s_klo = sem("kvt_lo_ready")
        s_sc = sem("scores_ready"); s_scu = sem("scores_used"); s_idx = sem("idx_ready")
        s_diag = sem("diag_ready"); s_row = sem("id_row_product"); s_rowc = sem("id_row_copied")
        s_q4 = sem("q_rows_product"); s_qa = sem("q_rows_rounded"); s_q4u = sem("q_rows_ready")
        s_first = sem("first_ready"); s_slot = sem("slots_product"); s_pk = sem("picks_ready")
        s_rows = sem("rows_product"); s_count = sem("row_count_ready"); s_idxc = sem("row_list_ready")
        s_mem = [sem(f"mem_gathered{j}") for j in range(4)]
        s_mT = sem("mem_transposed"); s_mTs = sem("memT_copied"); s_mkv = sem("mkv_product")
        s_ka = sem("keys_rounded"); s_kb = sem("mkv_ready")
        s_p1 = sem("logits_for_max_ready"); s_p1u = sem("logits_for_max_used")
        s_nmrow = [sem(f"minus_max_row{L}") for L in range(NQ)]
        s_lg = sem("logits_ready"); s_ex = sem("probs_ready"); s_avd = sem("av_done"); s_avc = sem("av_copied")
        s_avT = sem("av_transposed"); s_att = sem("att_ready"); s_attT = sem("att_transposed"); s_attTs = sem("attT_copied")
        s_wc = sem("projected"); s_x1 = sem("x1_ready")
        s_dve = sem("dve_step"); s_dveb = sem("dve_attention_step"); s_act = sem("act_step"); s_pool = sem("pool_step")
        s_h1 = sem("h1_products"); s_h1s = sem("h1_ready"); s_h2 = sem("h2_products"); s_h2s = sem("h2_ready")
        s_r = sem("router_logits"); s_rs = sem("router_logits_copied"); s_m8 = sem("router_sorted"); s_e8 = sem("router_exp")
        s_mask = sem("mask_ready"); s_pos = sem("positions_ready"); s_dest = sem("dest_ready")
        s_put = sem("tokens_put"); s_disp = sem("dispatched_loaded")
        s_dT = sem("dispatched_transposed"); s_dTs = sem("dT_copied")
        s_e1 = sem("expert_hidden_products"); s_e1s = sem("expert_hidden_ready")
        s_e2 = sem("expert_out_products"); s_e2s = sem("expert_out_ready"); s_eo = sem("expert_out_stored")
        s_got = sem("expert_rows_got"); s_fin = sem("rows_ready"); s_out = sem("out_stored")
        block = stack.enter_context(nc.Block())

        KV_PIECE = 10

        def ring_jobs(T):
            units = H // (2 if T <= 4 else 1)
            jobs = [(a, u) for a in range(TQ) for u in range(units)]
            for a in range(TQ - 1):
                jobs.insert((a + 1) * units + 1 + a, (a, None))
            return jobs + [(TQ - 1, None)]

        def ring_span(T, s):
            n, steps = len(ring_jobs(T)), NG * T
            return range(min(n, s * n // (steps - 2)), min(n, (s + 1) * n // (steps - 2)))

        def by_count(eng, emit):
            with eng.register("rows_" + str(eng.engine).split(".")[-1]) as reg:
                eng.wait_ge(s_count, 1)
                eng.reg_load(reg, n_rows[0:1, 0:1])
                n = eng.snap(reg, min_val=1, max_val=TOK)
                with eng.If(n <= 3 * P):
                    emit(3)
                with eng.Else():
                    with eng.If(n <= 4 * P):
                        emit(4)
                    with eng.Else():
                        emit(NT)
        n_scores = NT * NCH

        @block.sync
        def _(sp):
            sp.dma_start(x_sb[:], xf.rearrange("(t p) d -> p t d", p=P)).then_inc(s_x, 16)
            for j in range(5):
                rows = kv[j * KV_PIECE * P:(j + 1) * KV_PIECE * P, :]
                sp.dma_start(kv_nat[:, j * KV_PIECE:(j + 1) * KV_PIECE, :],
                             rows.rearrange("(t p) d -> p t d", p=P)).then_inc(s_kv[j], 16)
            sp.dma_start(kv_nat[0:TAIL, NKV - 1, :], kv[(NKV - 1) * P:M, :]).then_inc(s_kv[5], 16)
            sp.dma_start(rw1_sb[:], rW1).then_inc(s_w, 16)
            sp.dma_start(rw2_sb[:], rW2.rearrange("(k p) n -> p k n", p=P)).then_inc(s_w, 16)
            sp.dma_start(rw3_sb[:], rW3.rearrange("(k p) n -> p k n", p=P)).then_inc(s_w, 16)
            sp.dma_start(ew1_sb[:], eW1.rearrange("e c h -> c e h")).then_inc(s_w, 16)
            sp.dma_start(ew2_sb[:], eW2.rearrange("e (k p) c -> p e k c", p=P)).then_inc(s_w, 16)

            def minus_max_rows(T):
                per_q = len(ring_jobs(T))
                for q in range(NQ):
                    sp.wait_ge(s_p1u, (q + 1) * per_q)
                    cols = slice(q * W, (q + 1) * W)
                    for r, src in ((3 * DH, nm_hi), (3 * DH + 1, nm_lo)):
                        sp.dma_start(q_rows[r:P:RS, :, cols].bitcast(F32), src[:, cols].bitcast(F32)
                                     ).then_inc(s_nmrow[q], 16)

            by_count(sp, minus_max_rows)
            sp.wait_ge(s_put, 16 * TOPK * NT)
            sp.dma_start(disp[:], dispatched.rearrange("(t p) d -> p t d", p=P)).then_inc(s_disp, 16)
            for e in range(E):
                sp.wait_ge(s_e2s, e + 1)
                sp.dma_start(expert_out[e * CAP:(e + 1) * CAP, :].rearrange("(t p) d -> p t d", p=80),
                             eo[0:80, 2 * e:2 * e + 2, :]).then_inc(s_eo, 16)
            sp.wait_ge(s_fin, NT)
            sp.dma_start(outf.rearrange("(t p) d -> p t d", p=P), fin[:]).then_inc(s_out, 16)
            sp.wait_ge(s_out, 16)

        @block.gpsimd
        def _(pool):
            n = [0]

            def link(ins):
                n[0] += 1
                ins.then_inc(s_pool, 1)
                pool.wait_ge(s_pool, n[0])

            link(pool.memset(ident[:], 0.0))
            pool.affine_select(out=ident[:], in_=ident[:], compare_op=ALU.not_equal, fill=1.0, base=0,
                               pattern=[[-1, P]], channel_multiplier=1).then_inc(s_const, 1)
            link(pool.memset(ones[:], 1.0))
            pool.affine_select(out=below[:], in_=ones[:], compare_op=ALU.is_gt, fill=0.0, base=0,
                               pattern=[[1, P]], channel_multiplier=-1).then_inc(s_const, 1)
            link(pool.memset(minus_half[:], -0.5))
            pool.wait_ge(s_ve, 1)
            pool.tensor_tensor(rstd[:], var_eps[:], minus_half[:], ALU.pow).then_inc(s_rstd, 1)
            link(pool.iota(offs_i[:], pattern=[[CHUNK, NCH]], base=-int(IDX_TOP), channel_multiplier=0))
            pool.tensor_copy(offs[:], offs_i[:]).then_inc(s_const, 1)
            link(pool.iota(iota8_i[:], pattern=[[1, E]], base=0, channel_multiplier=0))
            pool.tensor_copy(iota8[:], iota8_i[:]).then_inc(s_const, 1)
            link(pool.memset(not_earlier[:], 0.0))
            link(pool.affine_select(out=not_earlier[:], in_=not_earlier[:], compare_op=ALU.is_gt, fill=-2 * IDX_TOP,
                                    base=0, pattern=[[-1, P]], channel_multiplier=1))
            link(pool.iota(iota_i[:], pattern=[[1, P]], base=1, channel_multiplier=0))
            link(pool.tensor_copy(iota1[:], iota_i[:]))
            link(pool.tensor_scalar(thr[:], iota1[:, 0:NT], float(P), -float(P), ALU.mult, ALU.add))
            link(pool.iota(part_i[:], pattern=[[0, 1]], base=0, channel_multiplier=1))
            link(pool.tensor_copy(rr[:], part_i[:]))
            for j in range(1, GH):
                link(pool.tensor_scalar(ge[:, j:j + 1], rr[:], float(RS), -float(RS), ALU.is_ge, ALU.mult))
                link(pool.tensor_tensor(rr[:], rr[:], ge[:, j:j + 1], ALU.add))
            for k, r in enumerate((DH, 2 * DH, 3 * DH, 3 * DH + 2)):
                link(pool.tensor_scalar(ge[:, 4 + k:5 + k], rr[:], float(r), None, ALU.is_ge))
            link(pool.tensor_tensor(q_low[:], ge[:, 4:5], ge[:, 5:6], ALU.subtract))
            link(pool.tensor_tensor(k_low[:], ge[:, 5:6], ge[:, 6:7], ALU.subtract))
            link(pool.tensor_tensor(k_one[:], ge[:, 6:7], ge[:, 7:8], ALU.subtract))
            link(pool.tensor_scalar(q_sgn[:], q_low[:], -2.0, 1.0, ALU.mult, ALU.add))
            link(pool.tensor_scalar(k_sgn[:], k_low[:], -2.0, 1.0, ALU.mult, ALU.add))
            link(pool.memset(wq_rep[:], 0.0))
            pool.memset(wk_rep[:], 0.0).then_inc(s_const, 1)
            link(pool.memset(first[:], 0.0))
            link(pool.memset(seen_f[:], 0.0))
            link(pool.memset(hits_a[:], 0.0))
            link(pool.memset(v_ext[:], 0.0))
            pool.memset(k_blk[:].bitcast(F32), 0.0).then_inc(s_const, 1)
            link(pool.memset(zero[:], 0.0))
            pool.dma_start(dispatched.rearrange("(t p) d -> p t d", p=P), zero[:]).then_inc(s_zero, 16)

            def gather(T):
                pool.wait_ge(s_idxc, 1)
                for t in range(T):
                    if t >= 4:
                        pool.wait_ge(s_mT, t - 3)
                    pool.indirect_dma_start(out=mem[:, t, :], out_offset=None, in_=kv,
                                            in_offset=bass.IndirectOffsetOnAxis(ap=row_u[:, t:t + 1], axis=0)
                                            ).then_inc(s_mem[t % 4], 16)

            by_count(pool, gather)
            pool.wait_ge(s_ve, 2)
            pool.tensor_tensor(rstd[:], var_eps[:], minus_half[:], ALU.pow).then_inc(s_rstd, 1)
            pool.wait_ge(s_dest, 1)
            pool.wait_ge(s_zero, 16)
            for k in range(TOPK):
                for i in range(NT):
                    pool.indirect_dma_start(out=dispatched, out_offset=bass.IndirectOffsetOnAxis(
                        ap=dest_put[:, k, i:i + 1], axis=0), in_=xn[:, i, :], in_offset=None,
                        bounds_check=SLOTS - 1, oob_is_err=False).then_inc(s_put, 16)
            pool.wait_ge(s_eo, 16 * E)
            for k in range(TOPK):
                for i in range(NT):
                    pool.indirect_dma_start(out=got[:, k, i, :], out_offset=None, in_=expert_out,
                                            in_offset=bass.IndirectOffsetOnAxis(ap=dest_get[:, k, i:i + 1], axis=0)
                                            ).then_inc(s_got, 16)

        @block.scalar
        def _(act):
            act.dma_start(wq_nat[:], Wq).then_inc(s_wql, 16)
            act.dma_start(wkv_nat[:], Wkv).then_inc(s_small, 16)
            act.dma_start(wc_nat[:], Wc).then_inc(s_small, 16)
            act.dma_start(bias_nat[0:E * KH, :], eb1.rearrange("e (k p) -> (e k) p", p=P)).then_inc(s_small, 16)
            act.dma_start(bias_nat[E * KH:E * KH + KH, :], rb1.rearrange("(k p) -> k p", p=P)).then_inc(s_small, 16)
            act.dma_start(bias_nat[E * KH + KH:, :], rb2.rearrange("(k p) -> k p", p=P)).then_inc(s_small, 16)
            act.dma_start(row10[0:1, 0:E], rb3.rearrange("(a e) -> a e", a=1)).then_inc(s_small, 16)
            act.dma_start(row10[0:1, E:E + 1], g_xattn.rearrange("(a e) -> a e", a=1)).then_inc(s_small, 16)
            act.dma_start(row10[0:1, E + 1:E + 2], g_ffn.rearrange("(a e) -> a e", a=1)).then_inc(s_small, 16)
            act.dma_start(eb2_row[:], eb2.rearrange("(a e) d -> a e d", a=1)).then_inc(s_small, 16)
            act.wait_ge(s_cT, 1)
            act.copy(consts[:, 0:D], ps[:, 5 * HALF:5 * HALF + D]).then_inc(s_cs, 1)
            for n in range(NL):
                act.wait_ge(s_xT, n + 1)
                act.copy(xnT[:, n * HALF:(n + 1) * HALF], bank(6 + n)).then_inc(s_xTs, 1)
            for n in range(NL):
                act.wait_ge(s_qp, n + 1)
                act.copy(q_hi[:, n * HALF:(n + 1) * HALF], bank(6 + n)).then_inc(s_qhi, 1)
            act.wait_ge(s_cT, 2)
            act.copy(consts[:, D:C_ROW + 10], ps[:, 5 * HALF + D:5 * HALF + C_ROW + 10]).then_inc(s_cs, 1)
            act.wait_ge(s_cs, 2)
            act.activation(gates[:], consts[:, C_ROW + E:C_ROW + E + 2], ACT.Tanh).then_inc(s_cs, 1)
            act.wait_ge(s_const, 5)
            act.copy(wk_rep[:, :, 0:3 * DH].rearrange("p j (r d) -> p j r d", r=3),
                     consts[:, C_WKV:C_WKV + DH].unsqueeze(1).unsqueeze(1).broadcast_to([P, GH, 3, DH])).then_inc(s_cs, 1)
            act.copy(wq_rep[:, :, 0:3 * DH].rearrange("p h (r d) -> p h r d", r=3),
                     consts[:, C_WQ:C_WQ + D].rearrange("p (h d) -> p h d", h=H).unsqueeze(2).broadcast_to([P, H, 3, DH])
                     ).then_inc(s_cs, 1)
            for g in range(NKG):
                act.wait_ge(s_kvT, g + 1)
                w = min(HALF, M - g * HALF)
                act.copy(kvt_hi[:, g * HALF:g * HALF + w], ps[:, (6 + g % 2) * HALF:(6 + g % 2) * HALF + w]).then_inc(s_khi, 1)
            for i in range(NT):
                if i:
                    act.wait_ge(s_row, i)
                    act.copy(id_row[:, (i - 1) * P:i * P], ps[:, 6 * HALF:6 * HALF + P]).then_inc(s_rowc, 1)
                act.wait_ge(s_q4, i + 1)
                if i:
                    act.wait_ge(s_q4u, i)
                act.activation(q_a[:], bank(7), ACT.Identity, scale=q_sgn[:, 0:1]).then_inc(s_qa, 1)
            act.wait_ge(s_row, NT)
            act.copy(id_row[:, (NT - 1) * P:], ps[:, 6 * HALF:6 * HALF + P]).then_inc(s_rowc, 1)

            def attention_act(T):
                for t in range(T + 1):
                    if t < T:
                        act.wait_ge(s_mT, t + 1)
                        act.copy(memT[:, t * P:(t + 1) * P], ps[:, (t % 2) * HALF:(t % 2) * HALF + P]).then_inc(s_mTs, 1)
                    if t:
                        act.wait_ge(s_mkv, t)
                        if t >= 3:
                            act.wait_ge(s_kb, t - 2)
                        b = 2 + (t - 1) % 2
                        act.activation(k_a[:, (t - 1) % 2, :], ps[:, b * HALF:b * HALF + P], ACT.Identity,
                                       scale=k_sgn[:, 0:1], bias=k_one[:, 0:1]).then_inc(s_ka, 1)
                steps, n = NG * T, 0

                def copy_av(group):
                    q, g = divmod(group, NG)
                    act.wait_ge(s_avd, (group + 1) * T)
                    if q >= 2:
                        act.wait_ge(s_avT, TQ * (q - 1))
                    act.copy(av[:, q % 2, g, :], ps[:, 6 * HALF:6 * HALF + W]).then_inc(s_avc, 1)

                for period in range(1, NQ + 2):
                    for s in range(steps):
                        if period >= 2 and s >= 3 and (s - 3) % 4 == 0 and (s - 3) // 4 < TQ:
                            act.wait_ge(s_attT, TQ * (period - 2) + (s - 3) // 4 + 1)
                            act.copy(attT[:], ps[:, 7 * HALF:7 * HALF + P]).then_inc(s_attTs, 1)
                        if period <= NQ:
                            u = (period - 1) * steps + s
                            if u >= 2:
                                act.wait_ge(s_avd, u - 1)
                            for b in range(GH // HB):
                                act.wait_ge(s_lg, n + 1)
                                act.activation(probs[:, u % 2, b * HB:(b + 1) * HB, :], bank(4 + n % 2), ACT.Exp,
                                               scale=SCALE).then_inc(s_ex, 1)
                                n += 1
                        u = (period - 1) * steps + s
                        if u and s % T == 0 and u // T <= NQ * NG:
                            copy_av(u // T - 1)

            by_count(act, attention_act)
            for n in range(NL):
                act.wait_ge(s_xT, NL + n + 1)
                act.copy(xnT[:, n * HALF:(n + 1) * HALF], bank(6 + n)).then_inc(s_xTs, 1)
            n = 0
            for L in range(NL):
                for k in range(KH):
                    act.wait_ge(s_h1, n + 1)
                    act.activation(h1[:, k, L * HALF:(L + 1) * HALF], bank(n % 4), ACT.Relu,
                                   bias=consts[:, C_B + E * KH + k:C_B + E * KH + k + 1]).then_inc(s_h1s, 1)
                    n += 1
            n = 0
            for L in range(NL):
                for k in range(KH):
                    act.wait_ge(s_h2, n + 1)
                    act.activation(h2[:, k, L * HALF:(L + 1) * HALF], bank(n % 4), ACT.Relu,
                                   bias=consts[:, C_B + E * KH + KH + k:C_B + E * KH + KH + k + 1]).then_inc(s_h2s, 1)
                    n += 1
            for i in range(NT):
                act.wait_ge(s_m8, i + 1)
                act.activation(e8[:, i, :], m8[:, i, :], ACT.Exp, bias=nm8[:, i:i + 1],
                               accum_out=sum8[:, i:i + 1]).then_inc(s_e8, 1)
            for g in range(3):
                w = min(4, NS - 4 * g) * P
                act.wait_ge(s_dT, g + 1)
                act.copy(dT[:, g * HALF:g * HALF + w], ps[:, g * HALF:g * HALF + w]).then_inc(s_dTs, 1)
            for e in range(E):
                for k in range(KH):
                    if k == 0 and e >= 2:
                        act.wait_ge(s_e2, e - 1)
                    act.wait_ge(s_e1, KH * e + k + 1)
                    b = 3 + (KH * e + k) % 2
                    act.activation(hh[:, e % 2, k, :], ps[:, b * HALF:b * HALF + CAP], ACT.Relu,
                                   bias=consts[:, C_B + KH * e + k:C_B + KH * e + k + 1]).then_inc(s_e1s, 1)

        @block.vector
        def _(dve):
            n = [0]

            def link(ins):
                n[0] += 1
                ins.then_inc(s_dve, 1)
                dve.wait_ge(s_dve, n[0])

            def layernorm(src, phase):
                if phase == 0:
                    for i in range(NT):
                        n[0] += 1
                        dve.bn_stats(stats[:, i, :], src[:, i, :]).then_inc(s_dve, 1)
                    dve.wait_ge(s_dve, n[0])
                    for i in range(NT):
                        n[0] += 1
                        dve.bn_aggr(mv[:, i, :], stats[:, i, :]).then_inc(s_dve, 1)
                    dve.wait_ge(s_dve, n[0])
                dve.tensor_scalar(var_eps[:], mv[:, :, 1], EPS, None, ALU.add).then_inc(s_ve, 1)
                dve.wait_ge(s_rstd, phase + 1)
                for i in range(NT):
                    dve.tensor_scalar(xn[:, i, :], src[:, i, :], mv[:, i, 0:1], rstd[:, i:i + 1],
                                      ALU.subtract, ALU.mult).then_inc(s_xn, 1)

            dve.wait_ge(s_x, 16)
            dve.wait_ge(s_const, 1)
            layernorm(x_sb, 0)
            for h in range(NL):
                dve.wait_ge(s_qhi, h + 1)
                dve.tensor_tensor(q_lo[:, h * HALF:(h + 1) * HALF], bank(6 + h), q_hi[:, h * HALF:(h + 1) * HALF],
                                  ALU.subtract).then_inc(s_qlo, 1)

            def kvt_lows(groups):
                for g in groups:
                    dve.wait_ge(s_khi, g + 1)
                    w = min(HALF, M - g * HALF)
                    dve.tensor_tensor(kvt_lo[:, g * HALF:g * HALF + w], ps[:, (6 + g % 2) * HALF:(6 + g % 2) * HALF + w],
                                      kvt_hi[:, g * HALF:g * HALF + w], ALU.subtract).then_inc(s_klo, 1)

            def first_of(i):
                dve.wait_ge(s_rowc, i + 1)
                link(dve.tensor_tensor(own[:], id_row[:, i * P:(i + 1) * P], not_earlier[:], ALU.add))
                link(dve.tensor_scalar(junk[:, 0:P], own[:], idxf[:, i:i + 1], 0.0, ALU.is_equal, ALU.add,
                                       accum_out=hits_b[:, i:i + 1]))
                if i:
                    link(dve.tensor_scalar(junk[:, 0:i * P], id_row[:, 0:i * P], idxf[:, i:i + 1], 0.0, ALU.is_equal,
                                           ALU.add, accum_out=hits_a[:, i:i + 1]))
                link(dve.tensor_scalar(first[:, i:i + 1], hits_b[:, i:i + 1], hits_a[:, i:i + 1], 0.0, ALU.add,
                                       ALU.is_equal))
                link(dve.tensor_tensor(seen_f[:, i + 1:i + 2], seen_f[:, i:i + 1], first[:, i:i + 1], ALU.add))

            dve.wait_ge(s_const, 6)
            kvt_lows(range(0, 3))
            for i in range(NT):
                b2 = i % 2
                for c, (_, w) in enumerate(CHUNKS):
                    if i == 0:
                        kvt_lows(range(3 * c + 3, min(3 * c + 6, NKG)))
                    m = i * NCH + c
                    sc = ps[:, (m % 2) * CHUNK:(m % 2) * CHUNK + w]
                    dve.wait_ge(s_sc, m + 1)
                    link(dve.max(best8[:, b2, c, :], sc))
                    dve.max_index(at8[:, b2, c, :], best8[:, b2, c, :], sc).then_inc(s_scu, 1)
                    if c == 1 and i >= 1:
                        first_of(i - 1)
                    if c == (NCH - 1 if i == 0 else 2):
                        g, half = i // NL, i % NL
                        dve.wait_ge(s_qa, i + 1)
                        dve.scalar_tensor_tensor(out=q_rows[:, g, half * HALF:(half + 1) * HALF], in0=bank(7),
                                                 scalar=q_low[:, 0:1], in1=q_a[:].bitcast(F32),
                                                 op0=ALU.mult, op1=ALU.add).then_inc(s_q4u, 1)
                link(dve.tensor_reduce(top[:, b2:b2 + 1], best8[:, b2, :, 0], AX.X, ALU.max))
                dve.wait_ge(s_scu, (i + 1) * NCH)
                link(dve.tensor_tensor(cand[:, b2, :], at8[:, b2, :, 0], offs[:], ALU.add))
                link(dve.scalar_tensor_tensor(out=cand2[:, b2, :], in0=best8[:, b2, :, 0], scalar=top[:, b2:b2 + 1],
                                              in1=cand[:, b2, :], op0=ALU.is_equal, op1=ALU.mult))
                link(dve.tensor_reduce(low[:, b2:b2 + 1], cand2[:, b2, :], AX.X, ALU.min))
                link(dve.tensor_scalar(idxf[:, i:i + 1], low[:, b2:b2 + 1], IDX_TOP, None, ALU.add))
                if i:
                    dve.wait_ge(s_row, i)
                dve.tensor_scalar(diag[:], ident[:], idxf[:, i:i + 1], None, ALU.mult).then_inc(s_diag, 1)
            first_of(NT - 1)
            dve.sem_inc(s_first, 1)
            dve.wait_ge(s_slot, 1)
            sl = ps[:, 6 * HALF + P:6 * HALF + P + NT + 1]
            dve.tensor_copy(n_rows[:], sl[0:1, NT:NT + 1]).then_inc(s_count, 1)
            link(dve.scalar_tensor_tensor(out=slot[:], in0=sl[:, 0:NT], scalar=1.0, in1=first[:, 0:NT],
                                          op0=ALU.add, op1=ALU.mult))
            link(dve.tensor_tensor(above[:], thr[:].unsqueeze(1).broadcast_to([P, NT, NT]),
                                   slot[:].unsqueeze(2).broadcast_to([P, NT, NT]), ALU.is_lt))
            link(dve.tensor_reduce(slot_t[:], above[:], AX.X, ALU.add))
            link(dve.scalar_tensor_tensor(out=slot_p[:], in0=slot_t[:], scalar=-float(P), in1=slot[:],
                                          op0=ALU.mult, op1=ALU.add))
            link(dve.tensor_scalar(slot_p[:], slot_p[:], float(P), None, ALU.add))
            link(dve.tensor_tensor(pick_t[:, :, 1, :], iota1[:, 0:NT].unsqueeze(1).broadcast_to([P, NT, NT]),
                                   slot_t[:].unsqueeze(2).broadcast_to([P, NT, NT]), ALU.is_equal))
            link(dve.tensor_tensor(pick_t[:, :, 0, :], pick_t[:, :, 1, :],
                                   idxf[:].unsqueeze(2).broadcast_to([P, NT, NT]), ALU.mult))
            for i in range(NT):
                dve.tensor_scalar(pick_p[:, i, :], iota1[:], slot_p[:, i:i + 1], None, ALU.is_equal).then_inc(s_pk, 1)
            dve.wait_ge(s_rows, 1)
            got_rows = ps[:, 5 * HALF:5 * HALF + 2 * NT]
            link(dve.tensor_copy(valid[:], got_rows[:, NT:2 * NT]))
            link(dve.tensor_scalar(pad[:], valid[:], -1.0, 1.0, ALU.mult, ALU.add))
            link(dve.scalar_tensor_tensor(out=row_f[:], in0=pad[:], scalar=id_row[:, 0:1], in1=got_rows[:, 0:NT],
                                          op0=ALU.mult, op1=ALU.add))
            link(dve.tensor_copy(row_u[:], row_f[:]))
            dve.sem_inc(s_idxc, 1)

            def attention_dve(T):
                n = [0]

                def link(ins):
                    n[0] += 1
                    ins.then_inc(s_dveb, 1)
                    dve.wait_ge(s_dveb, n[0])

                for t in range(T):
                    n[0] += 1
                    if t:
                        dve.wait_ge(s_dveb, n[0] - 1)
                    dve.tensor_scalar(junk[:], id_row[:], row_f[:, t:t + 1], 0.0, ALU.is_equal, ALU.add,
                                      accum_out=uses[:, t:t + 1]).then_inc(s_dveb, 1)
                dve.wait_ge(s_dveb, n[0])
                link(dve.tensor_tensor(weight_v[:, 0:T], uses[:, 0:T], valid[:, 0:T], ALU.mult))
                for t in range(T):
                    dve.wait_ge(s_ka, t + 1)
                    c, b, bv = slice(t * P, (t + 1) * P), (2 + t % 2) * HALF, (4 + t % 2) * HALF
                    for j in range(GH):
                        r = slice(RS * j, RS * (j + 1))
                        dve.scalar_tensor_tensor(out=k_blk[r, j, c], in0=ps[r, b:b + P], scalar=k_low[r, 0:1],
                                                 in1=k_a[r, t % 2, :].bitcast(F32), op0=ALU.mult, op1=ALU.add)
                    dve.tensor_copy(v_ext[:, t, DH:DH + 1], weight_v[:, t:t + 1])
                    dve.tensor_scalar(v_ext[:, t, 0:DH], ps[:, bv:bv + DH], weight_v[:, t:t + 1], None, ALU.mult
                                      ).then_inc(s_kb, 1)
                jobs, steps, m = ring_jobs(T), NG * T, 0
                hu = 2 if T <= 4 else 1
                for period in range(NQ + 2):
                    for s in range(steps):
                        if period >= 2 and s >= 2 and s % 2 == 0 and (s - 2) // 4 < TQ:
                            i = TQ * (period - 2) + (s - 2) // 4
                            if (s - 2) % 4 == 0:
                                dve.wait_ge(s_avT, i + 1)
                                a = bank(7).rearrange("p (h d) -> p h d", h=H)
                                link(dve.reciprocal(rden[:], a[:, :, DH]))
                                dve.tensor_tensor(att[:].rearrange("p (h d) -> p h d", h=H), a[:, :, 0:DH],
                                                  rden[:].unsqueeze(2).broadcast_to([P, H, DH]), ALU.mult
                                                  ).then_inc(s_att, 1)
                            else:
                                dve.wait_ge(s_wc, i + 1)
                                dve.scalar_tensor_tensor(out=x1[:, i, :], in0=ps[:, 7 * HALF:7 * HALF + D],
                                                         scalar=gates[:, 0:1], in1=x_sb[:, i, :],
                                                         op0=ALU.mult, op1=ALU.add).then_inc(s_x1, 1)
                                dve.wait_ge(s_x1, i + 1)
                                link(dve.bn_stats(stats[:, i, :], x1[:, i, :]))
                                link(dve.bn_aggr(mv[:, i, :], stats[:, i, :]))
                        for k in (ring_span(T, s) if period < NQ else ()):
                            a, unit = jobs[k]
                            i = TQ * period + a
                            dve.wait_ge(s_p1, m + 1)
                            if unit is not None:
                                sc = bank(2 * (m % 2), 2)
                                if hu == 2:
                                    sc = sc.rearrange("p (h k) -> p h k", h=2)[:, :, 0:T * P]
                                dve.tensor_reduce(mx[:, i, unit * hu:(unit + 1) * hu], sc, AX.X, ALU.max).then_inc(s_p1u, 1)
                            else:
                                c = slice(i * P, (i + 1) * P)
                                mt = ps[0:H, 2 * (m % 2) * HALF:2 * (m % 2) * HALF + P]
                                link(dve.tensor_scalar(nm_hi[:, c], mt, -1.0, None, ALU.mult))
                                dve.scalar_tensor_tensor(out=nm_lo[:, c], in0=mt, scalar=-1.0,
                                                         in1=nm_hi[:, c].bitcast(F32),
                                                         op0=ALU.mult, op1=ALU.subtract).then_inc(s_p1u, 1)
                            m += 1

            by_count(dve, attention_dve)
            layernorm(x1, 1)
            for i in range(NT):
                dve.wait_ge(s_r, NT)
                link(dve.tensor_tensor(r8[:, i, :], ps[:, 4 * HALF + i * E:4 * HALF + (i + 1) * E],
                                       consts[:, C_ROW:C_ROW + E], ALU.add))
                link(dve.max(m8[:, i, :], r8[:, i, :]))
                link(dve.max_index(i8[:, i, :], m8[:, i, :], r8[:, i, :]))
                dve.tensor_scalar(nm8[:, i:i + 1], m8[:, i, 0:1], -1.0, None, ALU.mult).then_inc(s_m8, 1)
            link(dve.tensor_copy(i8f[:], i8[:, :, 0:TOPK]))
            for k in range(TOPK):
                link(dve.tensor_tensor(pick[:, k], iota8[:].unsqueeze(1).broadcast_to([P, NT, E]),
                                       i8f[:, :, k:k + 1].broadcast_to([P, NT, E]), ALU.is_equal))
            link(dve.tensor_tensor(mask[:], pick[:, 0], pick[:, 1], ALU.add))
            link(dve.memset(seen[:, 0, :], 0.0))
            for i in range(1, NT):
                link(dve.tensor_tensor(seen[:, i, :], seen[:, i - 1, :], mask[:, i - 1, :], ALU.add))
            dve.sem_inc(s_mask, 1)
            dve.wait_ge(s_pos, 1)
            link(dve.tensor_copy(pos[:], ps[:, 5 * HALF:5 * HALF + NT * E].rearrange("p (t e) -> p t e", t=NT)))
            for k in range(TOPK):
                link(dve.tensor_tensor(scr[:, k], pick[:, k], pos[:], ALU.mult))
            link(dve.tensor_reduce(place[:], scr[:], AX.X, ALU.add))
            link(dve.tensor_scalar(keep[:], place[:], float(CAP), None, ALU.is_lt))
            link(dve.tensor_scalar(lost[:], keep[:], -float(SLOTS), float(SLOTS), ALU.mult, ALU.add))
            for k in range(TOPK):
                link(dve.scalar_tensor_tensor(out=dest[:, k, :], in0=i8f[:, :, k], scalar=float(CAP),
                                              in1=place[:, k, :], op0=ALU.mult, op1=ALU.add))
            link(dve.tensor_tensor(dest_put[:], dest[:], lost[:], ALU.add))
            dve.sem_inc(s_dest, 1)
            link(dve.tensor_tensor(dest_get[:], dest[:], keep[:], ALU.mult))
            dve.wait_ge(s_e8, NT)
            link(dve.reciprocal(rs8[:], sum8[:]))
            link(dve.tensor_scalar(rs8[:], rs8[:], gates[:, 1:2], None, ALU.mult))
            for k in range(TOPK):
                link(dve.tensor_tensor(tmpw[:, k, :], e8[:, :, k], rs8[:], ALU.mult))
            link(dve.tensor_tensor(weight[:], tmpw[:], keep[:], ALU.mult))
            dve.sem_inc(s_dest, 1)
            for e in range(E):
                dve.wait_ge(s_e2, e + 1)
                b = 5 + e % 2
                dve.tensor_copy(eo[0:80, 2 * e:2 * e + 2, :], ps[0:80, b * HALF:b * HALF + 2 * D]).then_inc(s_e2s, 1)
            dve.wait_ge(s_got, 16 * TOPK * NT)
            for i in range(NT):
                link(dve.scalar_tensor_tensor(out=acc[:, i, :], in0=got[:, 0, i, :], scalar=weight[:, 0, i:i + 1],
                                              in1=x1[:, i, :], op0=ALU.mult, op1=ALU.add))
                dve.scalar_tensor_tensor(out=fin[:, i, :], in0=got[:, 1, i, :], scalar=weight[:, 1, i:i + 1],
                                         in1=acc[:, i, :], op0=ALU.mult, op1=ALU.add).then_inc(s_fin, 1)

        @block.tensor
        def _(pe):
            b5, b7 = 5 * HALF, 7 * HALF
            pe.wait_ge(s_const, 1)
            pe.wait_ge(s_wql, 16)
            pe.transpose(ps[:, b5 + C_WQ:b5 + C_WQ + D], wq_nat[:], ident[:]).then_inc(s_cT, 1)
            for half in range(NL):
                pe.wait_ge(s_xn, 4 * (half + 1))
                for t in range(4):
                    last = pe.transpose(ps[:, (6 + half) * HALF + t * P:(6 + half) * HALF + (t + 1) * P],
                                        xn[:, 4 * half + t, :], ident[:])
                last.then_inc(s_xT, 1)
            pe.wait_ge(s_cs, 1)
            for half in range(NL):
                pe.wait_ge(s_xTs, half + 1)
                pe.matmul(bank(6 + half), consts[:, C_WQ:C_WQ + D], xnT[:, half * HALF:(half + 1) * HALF],
                          start=True, stop=True).then_inc(s_qp, 1)
            pe.wait_ge(s_const, 2)
            pe.wait_ge(s_small, 16 * 9)
            pe.transpose(ps[:, b5 + C_WC:b5 + C_WC + D], wc_nat[:], ident[:])
            pe.transpose(ps[:, b5 + C_WKV:b5 + C_WKV + 2 * DH], wkv_nat[:], ident[0:2 * DH, 0:2 * DH])
            nb = E * KH + 2 * KH
            pe.transpose(ps[:, b5 + C_B:b5 + C_B + nb], bias_nat[:], ident[0:nb, 0:nb])
            pe.matmul(ps[:, b5 + C_B + nb:b5 + C_ROW], ones[0:1, :], ones[0:1, 0:C_ROW - C_B - nb], start=True, stop=True)
            pe.matmul(ps[:, b5 + C_ROW:b5 + C_ROW + 10], ones[0:1, :], row10[:], start=True, stop=True).then_inc(s_cT, 1)

            def turn_kv(groups):
                for g in groups:
                    if g < 2:
                        pe.wait_ge(s_qlo, g + 1)
                    else:
                        pe.wait_ge(s_klo, g - 1)
                    for t in range(4 * g, min(4 * g + 4, NKV)):
                        pe.wait_ge(s_kv[t // KV_PIECE], 16)
                        r = P if t < NKV - 1 else TAIL
                        col = (6 + g % 2) * HALF + (t - 4 * g) * P
                        last = pe.transpose(ps[:, col:col + r], kv_nat[0:r, t, :], ident[0:r, 0:r])
                    last.then_inc(s_kvT, 1)

            def index_row(i):
                pe.wait_ge(s_diag, i + 1)
                pe.wait_ge(s_rowc if i else s_klo, i if i else NKG)
                pe.matmul(ps[:, 6 * HALF:6 * HALF + P], ones[:], diag[:], start=True, stop=True).then_inc(s_row, 1)

            turn_kv(range(0, 3))
            for i in range(NT):
                q_h, q_l = q_hi[:, i * P:(i + 1) * P], q_lo[:, i * P:(i + 1) * P]
                for c, (start, w) in enumerate(CHUNKS):
                    if i == 0:
                        turn_kv(range(3 * c + 3, min(3 * c + 6, NKG)))
                        pe.wait_ge(s_klo, min(3 * c + 3, NKG))
                        pe.wait_ge(s_cs, 2)
                    m = i * NCH + c
                    if m >= 2:
                        pe.wait_ge(s_scu, m - 1)
                    for s in range(0, w, HALF):
                        k = min(HALF, w - s)
                        o = ps[:, (m % 2) * CHUNK + s:(m % 2) * CHUNK + s + k]
                        hi, lo = kvt_hi[:, start + s:start + s + k], kvt_lo[:, start + s:start + s + k]
                        pe.matmul(o, q_h, hi, start=True, stop=False)
                        pe.matmul(o, q_h, lo, start=False, stop=False)
                        last = pe.matmul(o, q_l, hi, start=False, stop=True)
                    last.then_inc(s_sc, 1)
                    if c == 0 and i >= 1:
                        index_row(i - 1)
                    if c == (NCH - 1 if i == 0 else 1):
                        g, half = i // NL, i % NL
                        pe.wait_ge(s_cs, 5)
                        pe.wait_ge(s_q4u if i else s_klo, i if i else NKG)
                        pe.matmul(bank(7), wq_rep[:, GH * g:GH * (g + 1), :].rearrange("p j r -> p (j r)"),
                                  xnT[:, half * HALF:(half + 1) * HALF], start=True, stop=True).then_inc(s_q4, 1)
            index_row(NT - 1)

            pe.wait_ge(s_first, 1)
            pe.wait_ge(s_rowc, NT)
            sl = ps[:, 6 * HALF + P:6 * HALF + P + NT + 1]
            pe.matmul(sl, below[:], first[:], start=True, stop=False)
            pe.matmul(sl, ones[:], seen_f[:], start=False, stop=True).then_inc(s_slot, 1)
            pe.wait_ge(s_scu, NT * NCH)
            for i in range(NT):
                pe.wait_ge(s_pk, i + 1)
                last = pe.matmul(ps[:, 5 * HALF:5 * HALF + 2 * NT], pick_p[:, i, :],
                                 pick_t[:, i].rearrange("p k t -> p (k t)"), start=(i == 0), stop=(i == NT - 1))
            last.then_inc(s_rows, 1)

            def attention_pe(T):
                for t in range(T + 1):
                    if t < T:
                        pe.wait_ge(s_mem[t % 4], 16 * (t // 4 + 1))
                        if t >= 2:
                            pe.wait_ge(s_mTs, t - 1)
                        pe.transpose(ps[:, (t % 2) * HALF:(t % 2) * HALF + P], mem[:, t, :], ident[:]).then_inc(s_mT, 1)
                    if t:
                        k = t - 1
                        pe.wait_ge(s_mTs, t)
                        if k >= 2:
                            pe.wait_ge(s_kb, k - 1)
                        else:
                            pe.wait_ge(s_idxc, 1)
                        b, bv = (2 + k % 2) * HALF, (4 + k % 2) * HALF
                        pe.matmul(ps[:, b:b + P], wk_rep[:].rearrange("p j r -> p (j r)"), memT[:, k * P:(k + 1) * P],
                                  start=True, stop=True)
                        pe.matmul(ps[:, bv:bv + DH], memT[:, k * P:(k + 1) * P], consts[:, C_WKV + DH:C_WKV + 2 * DH],
                                  start=True, stop=True).then_inc(s_mkv, 1)
                pe.wait_ge(s_kb, T)
                pe.wait_ge(s_q4u, NT)
                jobs, steps, m, n = ring_jobs(T), NG * T, 0, 0
                hu = 2 if T <= 4 else 1

                def weigh(u):
                    group, t = divmod(u, T)
                    pe.wait_ge(s_ex, (GH // HB) * (u + 1))
                    if t == 0 and group:
                        pe.wait_ge(s_avc, group)
                    for j in range(GH):
                        last = pe.matmul(ps[RS * j:RS * (j + 1), 6 * HALF:6 * HALF + W], v_ext[:, t, :],
                                         probs[:, u % 2, j, :], start=(t == 0), stop=(t == T - 1),
                                         skip_group_check=True)
                    last.then_inc(s_avd, 1)

                for period in range(NQ + 2):
                    for s in range(steps):
                        for k in (ring_span(T, s) if period < NQ else ()):
                            a, unit = jobs[k]
                            i = TQ * period + a
                            if m >= 2:
                                pe.wait_ge(s_p1u, m - 1)
                            if unit is None:
                                pe.wait_ge(s_p1u, m if a == TQ - 1 else m - 1)
                                pe.transpose(ps[0:H, 2 * (m % 2) * HALF:2 * (m % 2) * HALF + P], mx[:, i, :], ident[:]
                                             ).then_inc(s_p1, 1)
                            else:
                                for h in range(unit * hu, (unit + 1) * hu):
                                    for c in range(0, T * P, HALF):
                                        w = min(HALF, T * P - c)
                                        b = 2 * (m % 2) + h - unit * hu + c // HALF
                                        last = pe.matmul(ps[:, b * HALF:b * HALF + w],
                                                         q_rows[:, h % NG, i * P:(i + 1) * P],
                                                         k_blk[:, h // NG, c:c + w], start=True, stop=True)
                                last.then_inc(s_p1, 1)
                            m += 1
                        if 1 <= period <= NQ:
                            q = period - 1
                            g, t = divmod(s, T)
                            if s == 0:
                                pe.wait_ge(s_nmrow[q], 32)
                            for b in range(GH // HB):
                                if n >= 2:
                                    pe.wait_ge(s_ex, n - 1)
                                for j in range(b * HB, (b + 1) * HB):
                                    col = (4 + n % 2) * HALF + (j - b * HB) * W
                                    last = pe.matmul(ps[:, col:col + W], k_blk[:, j, t * P:(t + 1) * P],
                                                     q_rows[:, g, q * W:(q + 1) * W], start=True, stop=True)
                                last.then_inc(s_lg, 1)
                                n += 1
                        u = (period - 1) * steps + s
                        if 1 <= u <= NQ * steps:
                            weigh(u - 1)
                        if period >= 2 and s >= 1 and (s - 1) // 4 < TQ:
                            i = TQ * (period - 2) + (s - 1) // 4
                            part = (s - 1) % 4
                            if part == 0:
                                pe.wait_ge(s_avc, NG * (period - 1))
                                if i:
                                    pe.wait_ge(s_x1, i)
                                for g in range(NG):
                                    last = pe.transpose(ps[:, b7 + g * P:b7 + (g + 1) * P],
                                                        av[:, period % 2, g, (i % TQ) * P:(i % TQ + 1) * P], ident[:])
                                last.then_inc(s_avT, 1)
                            elif part == 1:
                                pe.wait_ge(s_att, i + 1)
                                pe.transpose(ps[:, b7:b7 + P], att[:], ident[:]).then_inc(s_attT, 1)
                            elif part == 2:
                                pe.wait_ge(s_attTs, i + 1)
                                pe.matmul(ps[:, b7:b7 + D], attT[:], consts[:, C_WC:C_WC + D], start=True, stop=True
                                          ).then_inc(s_wc, 1)

            by_count(pe, attention_pe)
            pe.wait_ge(s_x1, NT)
            for half in range(NL):
                pe.wait_ge(s_xn, NT + 4 * (half + 1))
                for t in range(4):
                    last = pe.transpose(ps[:, (6 + half) * HALF + t * P:(6 + half) * HALF + (t + 1) * P],
                                        xn[:, 4 * half + t, :], ident[:])
                last.then_inc(s_xT, 1)
            pe.wait_ge(s_w, 16 * 5)
            n = 0
            for L in range(NL):
                pe.wait_ge(s_xTs, NL + L + 1)
                for k in range(KH):
                    if n >= 4:
                        pe.wait_ge(s_h1s, n - 3)
                    pe.matmul(bank(n % 4), rw1_sb[:, k * P:(k + 1) * P], xnT[:, L * HALF:(L + 1) * HALF],
                              start=True, stop=True).then_inc(s_h1, 1)
                    n += 1
            n = 0
            for L in range(NL):
                for k in range(KH):
                    pe.wait_ge(s_h1s, NL * KH if n >= 4 else KH + max(0, n + 1))
                    if n >= 4:
                        pe.wait_ge(s_h2s, n - 3)
                    for c in range(KH):
                        last = pe.matmul(bank(n % 4), rw2_sb[:, c, k * P:(k + 1) * P], h1[:, c, L * HALF:(L + 1) * HALF],
                                         start=(c == 0), stop=(c == KH - 1))
                    last.then_inc(s_h2, 1)
                    n += 1
            for i in range(NT):
                pe.wait_ge(s_h2s, KH * (i // 4 + 1))
                for c in range(KH):
                    last = pe.matmul(ps[:, 4 * HALF + i * E:4 * HALF + (i + 1) * E], h2[:, c, i * P:(i + 1) * P],
                                     rw3_sb[:, c, :], start=(c == 0), stop=(c == KH - 1))
                last.then_inc(s_r, 1)
            pe.wait_ge(s_mask, 1)
            pe.matmul(ps[:, 5 * HALF:5 * HALF + NT * E], below[:], mask[:].rearrange("p t e -> p (t e)"),
                      start=True, stop=False)
            pe.matmul(ps[:, 5 * HALF:5 * HALF + NT * E], ones[:], seen[:].rearrange("p t e -> p (t e)"),
                      start=False, stop=True).then_inc(s_pos, 1)
            pe.wait_ge(s_disp, 16)
            for g in range(3):
                for t in range(4 * g, min(4 * g + 4, NS)):
                    last = pe.transpose(ps[:, t * P:(t + 1) * P], disp[:, t, :], ident[:])
                last.then_inc(s_dT, 1)
            pe.wait_ge(s_dTs, 3)

            def expert_out_rows(e):
                for half in range(2):
                    b = 5 + e % 2
                    o = ps[0:80, b * HALF + half * D:b * HALF + (half + 1) * D]
                    if half == 0:
                        pe.wait_ge(s_e1s, KH * (e + 1))
                        if e >= 2:
                            pe.wait_ge(s_e2s, e - 1)
                    for k in range(KH):
                        pe.matmul(o, hh[:, e % 2, k, half * 80:half * 80 + 80], ew2_sb[:, e, k, :],
                                  start=(k == 0), stop=False)
                    last = pe.matmul(o, ones[0:1, 0:80], eb2_row[0:1, e, :], start=False, stop=True)
                last.then_inc(s_e2, 1)

            for e in range(E):
                for k in range(KH):
                    m = KH * e + k
                    if m >= 2:
                        pe.wait_ge(s_e1s, m - 1)
                    b = 3 + m % 2
                    pe.matmul(ps[:, b * HALF:b * HALF + CAP], ew1_sb[:, e, k * P:(k + 1) * P], dT[:, e * CAP:(e + 1) * CAP],
                              start=True, stop=True).then_inc(s_e1, 1)
                if e:
                    expert_out_rows(e - 1)
            expert_out_rows(E - 1)


_INS = ['x', 'ctx_1024', 'g_xattn', 'g_ffn', 'L0_xattn_Wq', 'L0_xattn_Wkv', 'L0_xattn_Wc', 'L0_ffn_rW1', 'L0_ffn_rb1',
        'L0_ffn_rW2', 'L0_ffn_rb2', 'L0_ffn_rW3', 'L0_ffn_rb3', 'L0_ffn_eW1', 'L0_ffn_eb1', 'L0_ffn_eW2', 'L0_ffn_eb2']


def kernel(**inputs):
    import numpy as _np
    import concourse.bacc as _bacc
    from concourse import mybir as _mybir
    from concourse.bass_utils import run_bass_kernel_spmd as _run

    nc = _bacc.Bacc("TRN2", target_bir_lowering=False, num_devices=1)
    arrays, args = {}, []
    for name in _INS:
        a = _np.ascontiguousarray(inputs[name])
        arrays[f"in_{name}_dram"] = a
        args.append(nc.dram_tensor(f"in_{name}_dram", a.shape, _mybir.dt.from_np(a.dtype), kind="ExternalInput").ap())
    args.append(nc.dram_tensor("out_0_dram", (1, TOK, D), _mybir.dt.float32, kind="ExternalOutput").ap())
    program(nc, *args)
    r = _run(nc, [arrays], core_ids=[0])
    return r.results[0]["out_0_dram"]
```

```python
from contextlib import ExitStack

import concourse.bass as bass
from concourse import mybir

F32 = mybir.dt.float32
F32R = mybir.dt.float32r
BF16 = mybir.dt.bfloat16
U32 = mybir.dt.uint32
ALU = mybir.AluOpType
ACT = mybir.ActivationFunctionType
AX = mybir.AxisListType

P = 128
D = 128
TOK = 1024
NT = TOK // P
M = 6404
PAIRS = M // 2
NKV = -(-PAIRS // P)
TAIL = PAIRS - (NKV - 1) * P
H, DH = 16, 8
HALF = 512
NL = TOK // HALF
SCALE = 1.0 / (DH ** 0.5)
EPS = 1e-5
HID = 4 * D
KH = HID // P
E, TOPK = 8, 2
CAP = int(TOK / E * 1.25)
SLOTS = E * CAP
NS = SLOTS // P
NG, GH = 4, 4
RS = 32
W = 256
NQ = TOK // W
TQ = W // P
HB = HALF // W

NCH = 8
CH_ENDS = [2 * -(-PAIRS * (c + 1) // (2 * NCH)) for c in range(NCH)]
CHUNKS = [(0 if c == 0 else CH_ENDS[c - 1], CH_ENDS[c]) for c in range(NCH)]
CHUNK = max(e - b for b, e in CHUNKS)
MID = CHUNKS[NCH // 2][0]
NKG = -(-PAIRS // HALF)
LOWEST = -3.0e38
LEAD = 5
FAR = 16384.0


def program(nc, x, ctx_mem, g_xattn, g_ffn, Wq, Wkv, Wc, rW1, rb1, rW2, rb2, rW3, rb3, eW1, eb1, eW2, eb2, out):
    kv = ctx_mem.rearrange("a m d -> (a m) d")
    kv_pairs = ctx_mem.rearrange("a (r two) d -> (a r) (two d)", two=2)
    xf = x.rearrange("a l d -> (a l) d")
    outf = out.rearrange("a l d -> (a l) d")

    with ExitStack() as stack:
        def sb(name, shape, dt=F32):
            return stack.enter_context(nc.sbuf_tensor(name, shape, dt))

        def sem(name):
            return stack.enter_context(nc.semaphore(name))

        ps = stack.enter_context(nc.psum_tensor("ps", [P, 8 * HALF], F32))

        def bank(b, n=1):
            return ps[:, b * HALF:(b + n) * HALF]

        ident = sb("ident", [P, P])
        ones = sb("ones", [P, P])
        below = sb("below", [P, P])
        x_sb = sb("x_sb", [P, NT, D])
        consts = sb("consts", [P, HALF])
        C_WQ, C_WC, C_WKV, C_B, C_ROW = 0, 128, 256, 272, 320
        gates = sb("gates", [P, 2])
        xn = sb("xn", [P, NT, D])
        xnT = sb("xnT", [P, TOK])
        x1 = sb("x1", [P, NT, D])
        stats = sb("stats", [P, NT, 6])
        mv = sb("mv", [P, NT, 2])
        var_eps = sb("var_eps", [P, NT])
        rstd = sb("rstd", [P, NT])
        minus_half = sb("minus_half", [P, NT])
        iota8 = sb("iota8", [P, E])
        iota8_i = sb("iota8_i", [P, E], mybir.dt.int32)
        rw1_sb = sb("rw1_sb", [P, HID])
        rw2_sb = sb("rw2_sb", [P, KH, HID])
        rw3_sb = sb("rw3_sb", [P, KH, E])
        ew1_sb = sb("ew1_sb", [P, E, HID])
        ew2_sb = sb("ew2_sb", [P, E, KH, D])
        iota_i = sb("iota_i", [P, P], mybir.dt.int32)
        iota1 = sb("iota1", [P, P])
        thr = sb("thr", [P, NS])

        attention = ExitStack()

        def sba(name, shape, dt=F32):
            return attention.enter_context(nc.sbuf_tensor(name, shape, dt))

        kv_nat = sba("kv_nat", [P, NKV, 2, D])
        shared = sba("shared", [P, 4 * PAIRS], F32R)
        kvt_hi = (shared[:, 0:PAIRS], shared[:, PAIRS:2 * PAIRS])
        kvt_lo = (shared[:, 2 * PAIRS:3 * PAIRS], shared[:, 3 * PAIRS:4 * PAIRS])
        wq_nat = sba("wq_nat", [P, D])
        wkv_nat = sba("wkv_nat", [2 * DH, D])
        wc_nat = sba("wc_nat", [P, D])
        bias_nat = sba("bias_nat", [E * KH + 2 * KH + E, P])
        row10 = sba("row10", [1, E + 2])
        wq_rep = sba("wq_rep", [P, H, RS])
        wk_rep = sba("wk_rep", [P, GH, RS])
        kd_blk = sba("kd_blk", [P, GH, HALF], F32R)
        q_rows = sba("q_rows", [P, NG, TOK], F32R)
        with ExitStack() as early:
            gain = early.enter_context(nc.sbuf_tensor("gain", [P, 3, CHUNK], F32))
            q_nat = early.enter_context(nc.sbuf_tensor("q_nat", [P, NT, D], F32))
            q_a = early.enter_context(nc.sbuf_tensor("q_a", [P, HALF], F32R))
            pick_p = early.enter_context(nc.sbuf_tensor("pick_p", [P, NT, P], BF16))
            q_x = early.enter_context(nc.sbuf_tensor("q_x", [P, HALF], F32))
        k_blk = sba("k_blk", [P, GH, TOK], F32R)
        q_hi = sba("q_hi", [P, TOK], F32R)
        q_lo = sba("q_lo", [P, TOK], F32R)
        part_i = sba("part_i", [P, 1], mybir.dt.int32)
        best = sba("best", [P, 2, 2, 8])
        best8 = sba("best8", [P, 2, 2, 8])
        at8 = sba("at8", [P, 2, 2, 8], U32)
        later = sba("later", [P, 1])
        apart = sba("apart", [P, 1])
        at = sba("at", [P, 2], U32)
        pair = sba("pair", [P, 2, 2 * D])
        dot = sba("dot", [P, 2])
        at_f = sba("at_f", [P, 1])
        odd = sba("odd", [P, 1])
        idxf = sba("idxf", [P, NT])
        diag = sba("diag", [P, P])
        id_row = sba("id_row", [P, TOK])
        own = sba("own", [P, P])
        not_earlier = sba("not_earlier", [P, P])
        junk = sba("junk", [P, TOK], BF16)
        hits_a = sba("hits_a", [P, NT])
        hits_b = sba("hits_b", [P, NT])
        first = sba("first", [P, NT + 1], BF16)
        seen_f = sba("seen_f", [P, NT + 1], BF16)
        below_b = sba("below_b", [P, P], BF16)
        all_b = sba("all_b", [P, P], BF16)
        n_rows = sba("n_rows", [1, 1], mybir.dt.int32)
        slot = sba("slot", [P, NT])
        above = sba("above", [P, NT, NT])
        slot_t = sba("slot_t", [P, NT])
        slot_p = sba("slot_p", [P, NT])
        pick_t = sba("pick_t", [P, NT, 3, NT], BF16)
        idx_b = sba("idx_b", [P, 2, NT], BF16)
        row_c = sba("row_c", [P, 3, NT])
        pad = sba("pad", [P, NT])
        row_s = sba("row_s", [P, NT])
        row_f = sba("row_f", [P, NT])
        row_u = sba("row_u", [P, NT], U32)
        uses = sba("uses", [P, NT])
        weight_v = sba("weight_v", [P, NT])
        k_a = sba("k_a", [P, 2, P], F32R)
        rr = sba("rr", [P, 1])
        ge = sba("ge", [P, 8])
        q_low = sba("q_low", [P, 1])
        q_sgn = sba("q_sgn", [P, 1])
        k_low = sba("k_low", [P, 1])
        k_sgn = sba("k_sgn", [P, 1])
        k_one = sba("k_one", [P, 1])
        v_ext = sba("v_ext", [P, NT, RS])
        mx = sba("mx", [P, NT, H])
        nm_hi = shared[0:H, 0:TOK]
        nm_lo = shared[0:H, TOK:2 * TOK]
        kd_a = shared[:, 2 * TOK:2 * TOK + HALF]
        kv_flat = kv_nat[:].rearrange("p t two d -> p (t two d)")
        m_all = (kv_flat[:, 0:PAIRS], kv_flat[:, PAIRS:2 * PAIRS])
        probs = kv_flat[:, 0:8 * W].rearrange("p (a j l) -> p a j l", a=2, j=GH)
        av = kv_flat[:, 8 * W:16 * W].rearrange("p (a g l) -> p a g l", a=2, g=NG)
        mem = kv_flat[:, 16 * W:16 * W + TOK].rearrange("p (t d) -> p t d", t=NT)
        memT = kv_flat[:, 16 * W + TOK:16 * W + 2 * TOK]
        memT_d = kv_flat[:, 16 * W + 2 * TOK:16 * W + 2 * TOK + HALF]
        rise = kv_flat[:, 16 * W:16 * W + 4 * HALF].rearrange("p (b k) -> p b k", b=4)
        rden = sba("rden", [P, H])
        att = sba("att", [P, D])
        attT = sba("attT", [P, P])
        attention.close()

        put = sb("put", [P, NT, HALF], F32R)
        dT = sb("dT", [P, SLOTS])
        hh = sb("hh", [P, 2, KH, CAP])
        eoT = sb("eoT", [P, SLOTS])
        info_diag = sb("info_diag", [P, 2, NS, P], BF16)
        with ExitStack() as hidden:
            h1 = hidden.enter_context(nc.sbuf_tensor("h1", [P, KH, TOK], F32))
            h2 = hidden.enter_context(nc.sbuf_tensor("h2", [P, KH, TOK], F32))
        get = sb("get", [P, NS, TOK], F32R)
        r8 = sb("r8", [P, NT, E])
        m8 = sb("m8", [P, NT, 8])
        i8 = sb("i8", [P, NT, 8], U32)
        i8f = sb("i8f", [P, TOPK, NT])
        e8 = sb("e8", [P, NT, 8])
        below_top = sb("below_top", [P, NT, 8])
        sum8 = sb("sum8", [P, NT])
        rs8 = sb("rs8", [P, NT])
        pick = sb("pick", [P, TOPK, NT, E])
        counts = [sb(f"counts{k}", [P, 4 + NT, E]) for k in range(4)]
        scr = sb("scr", [P, TOPK, NT, E])
        place = sb("place", [P, TOPK * NT])
        keep = sb("keep", [P, TOPK * NT])
        dest = sb("dest", [P, TOPK * NT])
        slot1 = sb("slot1", [P, TOPK * NT])
        above_s = sb("above_s", [P, TOPK * NT, NS])
        slot_a = sb("slot_a", [P, TOPK * NT])
        slot_b = sb("slot_b", [P, TOPK * NT])
        tmpw = sb("tmpw", [P, TOPK, NT])
        weight = sb("weight", [P, TOPK * NT])
        tok1_i = sb("tok1_i", [P, TOK], mybir.dt.int32)
        tok1_row = sb("tok1_row", [P, TOK])
        tok1_i8 = sb("tok1_i8", [P, NT], mybir.dt.int32)
        tok1 = sb("tok1", [P, NT])
        pick_a = sb("pick_a", [P, TOPK * NT, NS], BF16)
        pick_id = sb("pick_id", [P, TOPK * NT, 2, NS], BF16)
        pick_w = sb("pick_w", [P, TOPK * NT, 3, NS], BF16)
        pick_b = sb("pick_b", [P, TOPK * NT, P], BF16)
        weight_b = sb("weight_b", [P, 3, TOPK * NT], BF16)
        weight_r = sb("weight_r", [P, 2, TOPK * NT])
        tile_of = sb("tile_of", [P, TOPK * NT])
        iota1_b = sb("iota1_b", [P, P], BF16)
        ident_b = sb("ident_b", [P, P], BF16)
        ones_b = sb("ones_b", [P, 2, P], BF16)
        info_id = sb("info_id", [P, 2, NS])
        info = sb("info", [P, 2, NS])
        info_w = sb("info_w", [P, 3, NS])
        info_s = sb("info_s", [P, NS])
        tok_of = sb("tok_of", [P, SLOTS])
        xn_hi = sb("xn_hi", [P, NT, D], F32R)
        xn_lo = sb("xn_lo", [P, NT, D], F32R)
        eo = sb("eo", [P, NS, 2, D], F32R)
        acc = sb("acc", [P, NT, D])
        fin = sb("fin", [P, NT, D])

        s_x = sem("x_loaded"); s_kv = [sem(f"kv_loaded{j}") for j in range(6)]
        s_small = sem("small_loaded"); s_wql = sem("wq_loaded"); s_w = sem("weights_loaded")
        s_const = sem("pool_consts");
        s_cT = sem("consts_transposed"); s_cs = sem("consts_copied")
        s_ve = sem("variance_ready"); s_rstd = sem("rstd_ready"); s_xn = sem("xn_ready")
        s_xT = sem("xn_transposed"); s_xTs = sem("xnT_copied"); s_qp = sem("q_projected")
        s_qhi = sem("q_hi_ready"); s_qlo = sem("q_lo_ready")
        s_kvT = sem("kv_transposed"); s_khi = sem("kvt_hi_ready"); s_klo = sem("kvt_lo_ready")
        s_sc = sem("scores_ready"); s_scd = sem("score_gains_product"); s_rl = sem("gains_ready"); s_qn = sem("q_nat_ready"); s_pair = [sem("pair0_gathered"), sem("pair1_gathered")]; s_kd = sem("pairs_differenced"); s_qnp = sem("q_nat_product"); s_dots = sem("pair_products_ready"); s_kz = sem("key_blocks_zeroed"); s_scu = sem("scores_used"); s_idx = sem("idx_ready")
        s_diag = sem("diag_ready"); s_row = sem("id_row_product"); s_rowc = sem("id_row_copied")
        s_q4 = sem("q_rows_product"); s_qa = sem("q_rows_rounded"); s_q4u = sem("q_rows_ready"); s_own = sem("own_row_ready"); s_at = sem("winning_pair_ready"); s_dot = sem("dot_ready"); s_hits = sem("hits_ready")
        s_first = sem("first_ready"); s_slot = sem("slots_product"); s_pk = sem("picks_ready")
        s_rows = sem("rows_product"); s_count = sem("row_count_ready"); s_idxc = sem("row_list_ready")
        s_mem = [sem(f"mem_gathered{j}") for j in range(4)]
        s_mT = sem("mem_transposed"); s_mTs = sem("memT_copied"); s_mkv = sem("mkv_product")
        s_ka = sem("keys_rounded"); s_kb = sem("mkv_ready"); s_md = sem("memT_differences"); s_kdp = sem("key_differences_product"); s_kda = sem("key_differences_rounded"); s_kdb = sem("key_difference_blocks"); s_p1d = sem("rises_product"); s_p1r = sem("rises_ready")
        s_p1 = sem("logits_for_max_ready"); s_p1u = sem("logits_for_max_used")
        s_nmrow = [sem(f"minus_max_row{L}") for L in range(NQ)]
        s_lg = sem("logits_ready"); s_ex = sem("probs_ready"); s_avd = sem("av_done"); s_avc = sem("av_copied")
        s_avT = sem("av_transposed"); s_att = sem("att_ready"); s_attT = sem("att_transposed"); s_attTs = sem("attT_copied")
        s_wc = sem("projected"); s_x1 = sem("x1_ready")
        s_dve = sem("dve_step"); s_dveb = sem("dve_attention_step"); s_pool = sem("pool_step")
        s_h1 = sem("h1_products"); s_h1s = sem("h1_ready"); s_h2 = sem("h2_products"); s_h2s = sem("h2_ready")
        s_r = sem("router_logits"); s_m8 = sem("router_sorted"); s_e8 = sem("router_exp")
        s_mask = sem("mask_ready"); s_pos = sem("positions_ready"); s_tok = sem("token_numbers_ready")
        s_xh = sem("xn_hi_ready"); s_xl = sem("xn_lo_ready"); s_pb = sem("place_picks_ready"); s_iw = sem("info_weights_ready"); s_pw = sem("weight_picks_ready"); s_inw = sem("info_weights_product"); s_in = sem("info_product")
        s_idg = sem("info_diag_ready"); s_tr = sem("tok_of_product"); s_trc = sem("tok_of_ready")
        s_put = sem("put_ready"); s_putu = sem("put_used")
        s_dTs = sem("dT_copied")
        s_e1 = sem("expert_hidden_products"); s_e1s = sem("expert_hidden_ready")
        s_e2 = sem("expert_out_products"); s_e2s = sem("expert_out_ready")
        s_eT = sem("expert_out_turned"); s_eh = sem("expert_rows_rounded"); s_eo = sem("expert_rows_ready")
        s_cmb = sem("combined"); s_acc = sem("rows_added"); s_fin = sem("out_rows_ready"); s_out = sem("out_stored")
        block = stack.enter_context(nc.Block())

        KV_PIECE = 5
        done_with = [[t for t in range(NS) if e * CAP < (t + 1) * P <= (e + 1) * CAP] for e in range(E)]
        groups = [e for e in range(E) if done_with[e]]
        combine_at = lambda i: ((0, 1, 2, 7)[i // 2] * HALF + (i % 2) * 2 * D)

        def turns(c):
            upto = [2 * -(-e // HALF) for _, e in CHUNKS] + [2 * NKG]
            return range(0 if c < 0 else upto[c], upto[c + 1])

        def max_jobs(T):
            units = H // (2 if T <= 4 else 1)
            jobs = []
            for i in range(NT):
                jobs += [(i, u) for u in range(units)]
                if i:
                    jobs.insert(len(jobs) - units + 1, (i - 1, None))
            return jobs + [(NT - 1, None)]

        def by_rise(T, m):
            return max_jobs(T)[m][1] is not None and m in jobs_at(T, -1)

        def place_of(T, m):
            return m % (4 if m in jobs_at(T, -1) else 2)

        def rises_before(T, m):
            return sum(by_rise(T, k) for k in range(m))

        def heads_of(T, unit):
            hu = 2 if T <= 4 else 1
            g, j = divmod(unit * hu, GH)
            return g, j, j + hu

        def max_turns(T):
            jobs = max_jobs(T)
            return [jobs.index((TQ * (q + 1) - 1, None)) + 1 for q in range(NQ)]

        def jobs_at(T, step):
            n, steps = len(max_jobs(T)), NQ * NG * T

            def upto(x):
                return min(n, max_turns(T)[0] + LEAD + -(-(x + 1) * n // steps))
            return range(0 if step < 0 else upto(step - 1), upto(step))

        HIDDEN_AT = {0: [(1, 0)], 1: [(1, 1), (1, 2)], 2: [(1, 3)], 4: [(2, 0)], 6: [(2, 1)], 8: [(2, 2)]}

        def by_count(eng, emit):
            with eng.register("rows_" + str(eng.engine).split(".")[-1]) as reg:
                eng.wait_ge(s_count, 1)
                eng.reg_load(reg, n_rows[0:1, 0:1])
                n = eng.snap(reg, min_val=1, max_val=TOK)
                with eng.If(n <= 3 * P):
                    emit(3)
                with eng.Else():
                    with eng.If(n <= 4 * P):
                        emit(4)
                    with eng.Else():
                        emit(NT)

        @block.sync
        def _(sp):
            sp.dma_start(x_sb[:], xf.rearrange("(t p) d -> p t d", p=P)).then_inc(s_x, 16)
            for j in range(5):
                rows = kv_pairs[j * KV_PIECE * P:(j + 1) * KV_PIECE * P, :]
                sp.dma_start(kv_nat[:, j * KV_PIECE:(j + 1) * KV_PIECE].rearrange("p t two d -> p t (two d)"),
                             rows.rearrange("(t p) d -> p t d", p=P)).then_inc(s_kv[j], 16)
            sp.dma_start(kv_nat[0:TAIL, NKV - 1].rearrange("p two d -> p (two d)"),
                         kv_pairs[(NKV - 1) * P:PAIRS, :]).then_inc(s_kv[5], 16)
            sp.dma_start(rw1_sb[:], rW1).then_inc(s_w, 16)
            sp.dma_start(rw2_sb[:], rW2.rearrange("(k p) n -> p k n", p=P)).then_inc(s_w, 16)
            sp.dma_start(rw3_sb[:], rW3.rearrange("(k p) n -> p k n", p=P)).then_inc(s_w, 16)
            sp.dma_start(ew1_sb[:], eW1.rearrange("e c h -> c e h")).then_inc(s_w, 16)
            sp.dma_start(ew2_sb[:], eW2.rearrange("e (k p) c -> p e k c", p=P)).then_inc(s_w, 16)

            def minus_max_rows(T):
                for q, done in enumerate(max_turns(T)):
                    sp.wait_ge(s_p1u, done)
                    cols = slice(q * W, (q + 1) * W)
                    for r, src in ((3 * DH, nm_hi), (3 * DH + 1, nm_lo)):
                        sp.dma_start(q_rows[r:P:RS, :, cols].bitcast(F32), src[:, cols].bitcast(F32)
                                     ).then_inc(s_nmrow[q], 16)

            by_count(sp, minus_max_rows)
            for c in range(NT // 2):
                sp.wait_ge(s_fin, 2 * c + 2)
                sp.dma_start(outf[2 * c * P:2 * (c + 1) * P, :].rearrange("(t p) d -> p t d", p=P),
                             fin[:, 2 * c:2 * c + 2, :]).then_inc(s_out, 16)
            sp.wait_ge(s_out, 16 * NT // 2)

        @block.gpsimd
        def _(pool):
            n = [0]

            def link(ins):
                n[0] += 1
                ins.then_inc(s_pool, 1)
                pool.wait_ge(s_pool, n[0])

            link(pool.memset(ident[:], 0.0))
            pool.affine_select(out=ident[:], in_=ident[:], compare_op=ALU.not_equal, fill=1.0, base=0,
                               pattern=[[-1, P]], channel_multiplier=1).then_inc(s_const, 1)
            link(pool.memset(ones[:], 1.0))
            pool.affine_select(out=below[:], in_=ones[:], compare_op=ALU.is_gt, fill=0.0, base=0,
                               pattern=[[1, P]], channel_multiplier=-1).then_inc(s_const, 1)
            link(pool.memset(minus_half[:], -0.5))
            for j in range(6):
                pool.wait_ge(s_kv[j], 16)
                r, tiles = (P, slice(j * KV_PIECE, (j + 1) * KV_PIECE)) if j < 5 else (TAIL, slice(NKV - 1, NKV))
                pool.tensor_tensor(kv_nat[0:r, tiles, 1, :], kv_nat[0:r, tiles, 1, :], kv_nat[0:r, tiles, 0, :],
                                   ALU.subtract).then_inc(s_kd, 1)
                if j == 0:
                    pool.wait_ge(s_ve, 1)
                    pool.tensor_tensor(rstd[:], var_eps[:], minus_half[:], ALU.pow).then_inc(s_rstd, 1)
            link(pool.iota(iota8_i[:], pattern=[[1, E]], base=0, channel_multiplier=0))
            pool.tensor_copy(iota8[:], iota8_i[:]).then_inc(s_const, 1)
            link(pool.memset(not_earlier[:], 0.0))
            link(pool.affine_select(out=not_earlier[:], in_=not_earlier[:], compare_op=ALU.is_gt, fill=-FAR,
                                    base=0, pattern=[[-1, P]], channel_multiplier=1))
            link(pool.iota(iota_i[:], pattern=[[1, P]], base=1, channel_multiplier=0))
            link(pool.tensor_copy(iota1[:], iota_i[:]))
            link(pool.tensor_scalar(thr[:], iota1[:, 0:NS], float(P), -float(P), ALU.mult, ALU.add))
            link(pool.iota(part_i[:], pattern=[[0, 1]], base=0, channel_multiplier=1))
            link(pool.tensor_copy(rr[:], part_i[:]))
            for j in range(1, GH):
                link(pool.tensor_scalar(ge[:, j:j + 1], rr[:], float(RS), -float(RS), ALU.is_ge, ALU.mult))
                link(pool.tensor_tensor(rr[:], rr[:], ge[:, j:j + 1], ALU.add))
            for k, r in enumerate((DH, 2 * DH, 3 * DH, 3 * DH + 2)):
                link(pool.tensor_scalar(ge[:, 4 + k:5 + k], rr[:], float(r), None, ALU.is_ge))
            link(pool.tensor_tensor(q_low[:], ge[:, 4:5], ge[:, 5:6], ALU.subtract))
            link(pool.tensor_tensor(k_low[:], ge[:, 5:6], ge[:, 6:7], ALU.subtract))
            link(pool.tensor_tensor(k_one[:], ge[:, 6:7], ge[:, 7:8], ALU.subtract))
            link(pool.tensor_scalar(q_sgn[:], q_low[:], -2.0, 1.0, ALU.mult, ALU.add))
            link(pool.tensor_scalar(k_sgn[:], k_low[:], -2.0, 1.0, ALU.mult, ALU.add))
            link(pool.memset(wq_rep[:], 0.0))
            pool.memset(wk_rep[:], 0.0).then_inc(s_const, 1)
            link(pool.memset(all_b[:], 1.0))
            link(pool.tensor_copy(below_b[:], below[:]))
            link(pool.memset(first[:], 0.0))
            link(pool.memset(seen_f[:], 0.0))
            link(pool.memset(hits_a[:], 0.0))
            pool.memset(v_ext[:], 0.0)
            pool.memset(kd_blk[:].bitcast(F32), 0.0)
            def low_queries(k):
                g, half = k // NL, k % NL
                pool.wait_ge(s_qa, k + 1)
                pool.tensor_tensor(q_rows[:, g, half * HALF:(half + 1) * HALF], q_x[:], q_a[:].bitcast(F32), ALU.add
                                   ).then_inc(s_q4u, 1)

            def index_of(i):
                link(pool.tensor_copy(at_f[:], at[:, i % 2:i % 2 + 1]))
                pool.wait_ge(s_dot, i + 1)
                link(pool.tensor_scalar(odd[:], dot[:, i % 2:i % 2 + 1], 0.0, None, ALU.is_gt))
                link(pool.tensor_scalar(idxf[:, i:i + 1], at_f[:], 2.0, odd[:, 0:1], ALU.mult, ALU.add))
                if i:
                    pool.wait_ge(s_row, i)
                pool.tensor_scalar(diag[:], ident[:], idxf[:, i:i + 1], None, ALU.mult).then_inc(s_diag, 1)

            def own_row(i):
                pool.wait_ge(s_rowc, i + 1)
                if i:
                    pool.wait_ge(s_hits, i)
                pool.tensor_tensor(own[:], id_row[:, i * P:(i + 1) * P], not_earlier[:], ALU.add).then_inc(s_own, 1)

            def first_of(i):
                pool.wait_ge(s_hits, i + 1)
                link(pool.tensor_tensor(hits_a[:, i:i + 1], hits_a[:, i:i + 1], hits_b[:, i:i + 1], ALU.add))
                link(pool.tensor_scalar(first[:, i:i + 1], hits_a[:, i:i + 1], 0.0, None, ALU.is_equal))
                pool.tensor_tensor(seen_f[:, i + 1:i + 2], seen_f[:, i:i + 1], first[:, i:i + 1], ALU.add
                                   ).then_inc(s_first, 1)
                pool.wait_ge(s_first, i + 1)

            for i in range(NT):
                if i >= 1:
                    low_queries(i - 1)
                if i >= 2:
                    own_row(i - 2)
                if i >= 1:
                    index_of(i - 1)
                if i >= 2:
                    first_of(i - 2)
                if i == NT - 1:
                    own_row(i - 1)
                b2 = i % 2
                pool.wait_ge(s_at, i + 1)
                pool.indirect_dma_start(out=pair[:, b2, :], out_offset=None, in_=kv_pairs,
                                        in_offset=bass.IndirectOffsetOnAxis(ap=at[:, b2:b2 + 1], axis=0)
                                        ).then_inc(s_pair[b2], 16)
                if i == NT - 1:
                    low_queries(NT - 1)
                    break
                pool.wait_ge(s_pair[b2], 16 * (i // 2 + 1))
                link(pool.tensor_tensor(pair[:, b2, D:], pair[:, b2, D:], pair[:, b2, 0:D], ALU.subtract))
                pool.wait_ge(s_qn, NL)
                pool.tensor_tensor(pair[:, b2, 0:D], pair[:, b2, D:], q_nat[:, i, :], ALU.mult).then_inc(s_dots, 1)
            first_of(NT - 2)

            def gather(T):
                pool.wait_ge(s_idxc, 1)
                for t in range(T):
                    if t >= 4:
                        pool.wait_ge(s_mT, t - 3)
                    pool.indirect_dma_start(out=mem[:, t, :], out_offset=None, in_=kv,
                                            in_offset=bass.IndirectOffsetOnAxis(ap=row_u[:, t:t + 1], axis=0)
                                            ).then_inc(s_mem[t % 4], 16)
                    if t == 2:
                        pool.memset(k_blk[:].bitcast(F32)[:, :, 0:T * P], 0.0).then_inc(s_kz, 1)

            by_count(pool, gather)
            for half in range(NL):
                pool.wait_ge(s_ve, half + 2)
                t = slice(4 * half, 4 * half + 4)
                pool.tensor_tensor(rstd[:, t], var_eps[:, t], minus_half[:, t], ALU.pow).then_inc(s_rstd, 1)
            pool.wait_ge(s_x1, NT)
            link(pool.iota(tok1_i8[:], pattern=[[P, NT]], base=1, channel_multiplier=1))
            link(pool.tensor_copy(tok1[:], tok1_i8[:]))
            for k in range(4):
                link(pool.memset(counts[k][:], 0.0))
            for k in range(TOPK):
                link(pool.tensor_scalar(tile_of[:, k * NT:(k + 1) * NT], tok1[:], tok1[:, 0:1], 1.0 / P,
                                        ALU.subtract, ALU.mult))
            link(pool.tensor_copy(iota1_b[:], iota1[:]))
            link(pool.tensor_copy(ident_b[:], ident[:]))
            link(pool.memset(ones_b[:, 0, :], 1.0))
            link(pool.memset(ones_b[:, 1, :], float(P)))
            pool.sem_inc(s_tok, 1)
            pool.wait_ge(s_xh, NL)
            pool.tensor_tensor(xn_lo[:], xn[:], xn_hi[:], ALU.subtract).then_inc(s_xl, 1)
            link(pool.iota(tok1_i[:], pattern=[[1, TOK]], base=1, channel_multiplier=0))
            pool.tensor_copy(tok1_row[:], tok1_i[:]).then_inc(s_tok, 1)

        @block.scalar
        def _(act):
            act.dma_start(wq_nat[:], Wq).then_inc(s_wql, 16)
            act.dma_start(wkv_nat[:], Wkv).then_inc(s_small, 16)
            act.dma_start(wc_nat[:], Wc).then_inc(s_small, 16)
            act.dma_start(bias_nat[0:E * KH, :], eb1.rearrange("e (k p) -> (e k) p", p=P)).then_inc(s_small, 16)
            act.dma_start(bias_nat[E * KH:E * KH + KH, :], rb1.rearrange("(k p) -> k p", p=P)).then_inc(s_small, 16)
            act.dma_start(bias_nat[E * KH + KH:E * KH + 2 * KH, :], rb2.rearrange("(k p) -> k p", p=P)).then_inc(s_small, 16)
            act.dma_start(row10[0:1, 0:E], rb3.rearrange("(a e) -> a e", a=1)).then_inc(s_small, 16)
            act.dma_start(row10[0:1, E:E + 1], g_xattn.rearrange("(a e) -> a e", a=1)).then_inc(s_small, 16)
            act.dma_start(row10[0:1, E + 1:E + 2], g_ffn.rearrange("(a e) -> a e", a=1)).then_inc(s_small, 16)
            act.dma_start(bias_nat[E * KH + 2 * KH:, :], eb2).then_inc(s_small, 16)
            act.wait_ge(s_cT, 1)
            act.copy(consts[:, 0:D], ps[:, 3 * HALF:3 * HALF + D]).then_inc(s_cs, 1)
            def round_kv(jobs):
                for k in jobs:
                    g, part = divmod(k, 2)
                    act.wait_ge(s_kvT, k + 1)
                    cols = slice(g * HALF, min((g + 1) * HALF, PAIRS))
                    act.copy(kvt_hi[part][:, cols], ps[:, (6 + part) * HALF:(6 + part) * HALF + cols.stop - cols.start]
                             ).then_inc(s_khi, 1)

            round_kv(turns(-1))
            for n in range(NL):
                act.wait_ge(s_xT, n + 1)
                act.copy(xnT[:, n * HALF:(n + 1) * HALF], bank(4 + n)).then_inc(s_xTs, 1)
            for n in range(NL):
                act.wait_ge(s_qp, n + 1)
                act.copy(q_hi[:, n * HALF:(n + 1) * HALF], bank(4 + n)).then_inc(s_qhi, 1)
            round_kv(turns(0))
            for n in range(NL):
                act.wait_ge(s_qnp, n + 1)
                act.copy(q_nat[:, 4 * n:4 * n + 4, :], bank(4 + n).rearrange("p (t e) -> p t e", t=4)).then_inc(s_qn, 1)

            def index_row(i):
                act.wait_ge(s_row, i + 1)
                act.copy(id_row[:, i * P:(i + 1) * P], ps[:, 6 * HALF:6 * HALF + P]).then_inc(s_rowc, 1)

            def side_jobs(i):
                if i >= 2:
                    index_row(i - 2)
                act.wait_ge(s_q4, i)
                if i >= 2:
                    act.wait_ge(s_q4u, i - 1)
                act.activation(q_x[:], bank(7), ACT.Identity, scale=q_low[:, 0:1])
                act.activation(q_a[:], bank(7), ACT.Identity, scale=q_sgn[:, 0:1]).then_inc(s_qa, 1)

            for i in range(NT):
                for c, (start, end) in enumerate(CHUNKS):
                    if i == 0 and c:
                        round_kv(turns(c))
                    m = i * NCH + c
                    act.wait_ge(s_scd, m + 1)
                    if m >= 3:
                        act.wait_ge(s_scu, m - 2)
                    b = (2 * (m % 3) + 1) * HALF
                    act.activation(gain[:, m % 3, 0:end - start], ps[:, b:b + end - start], ACT.Relu).then_inc(s_rl, 1)
                    if c == 2 and i >= 1:
                        side_jobs(i)
                if i == 0:
                    act.wait_ge(s_cT, 2)
                    act.copy(consts[:, D:C_ROW + 10], ps[:, 7 * HALF + D:7 * HALF + C_ROW + 10]).then_inc(s_cs, 1)
                    act.wait_ge(s_cs, 2)
                    act.activation(gates[:], consts[:, C_ROW + E:C_ROW + E + 2], ACT.Tanh).then_inc(s_cs, 1)
                    act.wait_ge(s_const, 4)
                    act.copy(wk_rep[:, :, 0:3 * DH].rearrange("p j (r d) -> p j r d", r=3),
                             consts[:, C_WKV:C_WKV + DH].unsqueeze(1).unsqueeze(1).broadcast_to([P, GH, 3, DH])
                             ).then_inc(s_cs, 1)
                    act.copy(wq_rep[:, :, 0:3 * DH].rearrange("p h (r d) -> p h r d", r=3),
                             consts[:, C_WQ:C_WQ + D].rearrange("p (h d) -> p h d", h=H).unsqueeze(2)
                             .broadcast_to([P, H, 3, DH])).then_inc(s_cs, 1)
            side_jobs(NT)
            index_row(NT - 1)

            def hidden_rows(layer, half, k):
                src, done, to, c = ((s_h1, s_h1s, h1, C_B + E * KH) if layer == 1 else
                                    (s_h2, s_h2s, h2, C_B + E * KH + KH))
                n = KH * half + k
                act.wait_ge(src, n + 1)
                act.activation(to[:, k, half * HALF:(half + 1) * HALF], bank(n % 4), ACT.Relu,
                               bias=consts[:, c + k:c + k + 1]).then_inc(done, 1)

            def attention_act(T):
                for t in range(T + 1):
                    if t < T:
                        act.wait_ge(s_mT, t + 1)
                        act.copy(memT[:, t * P:(t + 1) * P], ps[:, (t % 2) * HALF:(t % 2) * HALF + P]).then_inc(s_mTs, 1)
                    if t:
                        act.wait_ge(s_mkv, t)
                        if t >= 3:
                            act.wait_ge(s_kb, t - 2)
                        b = 2 + (t - 1) % 2
                        act.activation(k_a[:, (t - 1) % 2, :], ps[:, b * HALF:b * HALF + P], ACT.Identity,
                                       scale=k_sgn[:, 0:1], bias=k_one[:, 0:1]).then_inc(s_ka, 1)
                act.wait_ge(s_kdp, 1)
                act.activation(kd_a[:, 0:T * P // 2], ps[:, 0:T * P // 2], ACT.Identity, scale=k_sgn[:, 0:1]
                               ).then_inc(s_kda, 1)
                steps, n = NG * T, 0

                def rise_of(m):
                    if by_rise(T, m):
                        act.wait_ge(s_p1d, rises_before(T, m) + 1)
                        w = (2 if T <= 4 else 1) * T * P // 2
                        b = (2 * place_of(T, m) + 1) * HALF
                        act.activation(rise[:, place_of(T, m), 0:w], ps[:, b:b + w], ACT.Relu).then_inc(s_p1r, 1)

                for m in jobs_at(T, -1):
                    rise_of(m)

                def copy_av(group):
                    q, g = divmod(group, NG)
                    act.wait_ge(s_avd, (group + 1) * T)
                    if q >= 2:
                        act.wait_ge(s_avT, TQ * (q - 1))
                    act.copy(av[:, q % 2, g, :], ps[:, 6 * HALF:6 * HALF + W]).then_inc(s_avc, 1)

                for period in range(1, NQ + 2):
                    for s in range(steps):
                        if period == NQ + 1 and s - 1 in HIDDEN_AT and s != 3:
                            for layer, k in HIDDEN_AT[s - 1]:
                                hidden_rows(layer, 0, k)
                        if period >= 2 and s >= 3 and (s - 3) % 4 == 0 and (s - 3) // 4 < TQ:
                            act.wait_ge(s_attT, TQ * (period - 2) + (s - 3) // 4 + 1)
                            act.copy(attT[:], ps[:, 7 * HALF:7 * HALF + P]).then_inc(s_attTs, 1)
                        take = jobs_at(T, (period - 1) * steps + s) if period <= NQ else ()
                        for m in take[:1]:
                            rise_of(m)
                        if period <= NQ:
                            u = (period - 1) * steps + s
                            if u >= 2:
                                act.wait_ge(s_avd, u - 1)
                            for b in range(GH // HB):
                                act.wait_ge(s_lg, n + 1)
                                act.activation(probs[:, u % 2, b * HB:(b + 1) * HB, :], bank(4 + n % 2), ACT.Exp,
                                               scale=SCALE).then_inc(s_ex, 1)
                                n += 1
                        for m in take[1:]:
                            rise_of(m)
                        u = (period - 1) * steps + s
                        if u and s % T == 0 and u // T <= NQ * NG:
                            copy_av(u // T - 1)
                        if period == NQ + 1 and s == 0:
                            act.wait_ge(s_xT, NL + 1)
                            act.copy(xnT[:, 0:HALF], bank(4)).then_inc(s_xTs, 1)
                        if period == NQ + 1 and s == 3:
                            for layer, k in HIDDEN_AT[s - 1]:
                                hidden_rows(layer, 0, k)

            by_count(act, attention_act)
            act.wait_ge(s_x1, NT)
            act.copy(xn_hi[:, 0:4, :], xn[:, 0:4, :]).then_inc(s_xh, 1)
            hidden_rows(2, 0, 3)
            act.wait_ge(s_xT, NL + 2)
            act.copy(xnT[:, HALF:], bank(5)).then_inc(s_xTs, 1)
            for k in range(KH):
                hidden_rows(1, 1, k)
            act.copy(xn_hi[:, 4:, :], xn[:, 4:, :]).then_inc(s_xh, 1)
            for k in range(KH):
                hidden_rows(2, 1, k)
            act.wait_ge(s_m8, NL)
            act.activation(e8[:], below_top[:], ACT.Exp).then_inc(s_e8, 1)
            for b in range(3):
                w = min(HALF, SLOTS - b * HALF)
                act.wait_ge(s_tr, b + 1)
                act.copy(tok_of[:, b * HALF:b * HALF + w], ps[:, b * HALF:b * HALF + w]).then_inc(s_trc, 1)
            for b in range(3):
                w = min(HALF, SLOTS - b * HALF)
                act.wait_ge(s_putu, (b + 1) * NT)
                act.copy(dT[:, b * HALF:b * HALF + w], ps[:, b * HALF:b * HALF + w]).then_inc(s_dTs, 1)
            for e in range(E + 2):
                for k in (range(KH) if e < E else ()):
                    if k == 0 and e >= 2:
                        act.wait_ge(s_e2, e - 1)
                    act.wait_ge(s_e1, KH * e + k + 1)
                    b = 3 + (KH * e + k) % 2
                    act.activation(hh[:, e % 2, k, :], ps[:, b * HALF:b * HALF + CAP], ACT.Relu,
                                   bias=consts[:, C_B + KH * e + k:C_B + KH * e + k + 1]).then_inc(s_e1s, 1)
                if e >= 2 and e - 2 in groups:
                    act.wait_ge(s_iw, 1)
                    act.wait_ge(s_eT, groups.index(e - 2) + 1)
                    for n, t in enumerate(done_with[e - 2]):
                        act.activation(eo[:, t, 0, :], ps[:, 6 * HALF + n * P:6 * HALF + (n + 1) * P], ACT.Identity,
                                       scale=info[:, 1, t:t + 1]).then_inc(s_eh, 1)

        @block.vector
        def _(dve):
            n = [0]

            def link(ins):
                n[0] += 1
                ins.then_inc(s_dve, 1)
                dve.wait_ge(s_dve, n[0])

            def normalise(src, tiles, phase):
                dve.wait_ge(s_rstd, phase)
                for i in tiles:
                    dve.tensor_scalar(xn[:, i, :], src[:, i, :], mv[:, i, 0:1], rstd[:, i:i + 1],
                                      ALU.subtract, ALU.mult).then_inc(s_xn, 1)

            link(dve.memset(best[:], LOWEST))
            dve.wait_ge(s_x, 16)
            dve.wait_ge(s_const, 1)
            for i in range(NT):
                n[0] += 1
                dve.bn_stats(stats[:, i, :], x_sb[:, i, :]).then_inc(s_dve, 1)
            dve.wait_ge(s_dve, n[0])
            for i in range(NT):
                n[0] += 1
                dve.bn_aggr(mv[:, i, :], stats[:, i, :]).then_inc(s_dve, 1)
            dve.wait_ge(s_dve, n[0])
            dve.tensor_scalar(var_eps[:], mv[:, :, 1], EPS, None, ALU.add).then_inc(s_ve, 1)
            normalise(x_sb, range(NT), 1)
            def kvt_lows(jobs):
                for k in jobs:
                    g, part = divmod(k, 2)
                    dve.wait_ge(s_khi, k + 1)
                    cols = slice(g * HALF, min((g + 1) * HALF, PAIRS))
                    dve.tensor_tensor(kvt_lo[part][:, cols], ps[:, (6 + part) * HALF:(6 + part) * HALF + cols.stop - cols.start],
                                      kvt_hi[part][:, cols], ALU.subtract).then_inc(s_klo, 1)

            kvt_lows(turns(-1))
            for h in range(NL):
                dve.wait_ge(s_qhi, h + 1)
                dve.tensor_tensor(q_lo[:, h * HALF:(h + 1) * HALF], bank(4 + h), q_hi[:, h * HALF:(h + 1) * HALF],
                                  ALU.subtract).then_inc(s_qlo, 1)

            def dot_of(i):
                dve.wait_ge(s_dots, i + 1)
                dve.tensor_reduce(dot[:, i % 2:i % 2 + 1], pair[:, i % 2, 0:D], AX.X, ALU.add).then_inc(s_dot, 1)

            def hits_of(i):
                if i:
                    dve.wait_ge(s_diag, i + 1)
                    dve.wait_ge(s_rowc, i)
                    dve.wait_ge(s_hits, i)
                    dve.tensor_scalar(junk[:, P:P + i * P], id_row[:, 0:i * P], idxf[:, i:i + 1], 0.0, ALU.is_equal,
                                      ALU.add, accum_out=hits_a[:, i:i + 1])
                dve.wait_ge(s_own, i + 1)
                dve.tensor_scalar(junk[:, 0:P], own[:], idxf[:, i:i + 1], 0.0, ALU.is_equal, ALU.add,
                                  accum_out=hits_b[:, i:i + 1]).then_inc(s_hits, 1)

            kvt_lows(turns(0))
            for i in range(NT):
                b2 = i % 2
                for c, (start, end) in enumerate(CHUNKS):
                    if i == 0 and c:
                        kvt_lows(turns(c))
                    m = i * NCH + c
                    if c == 0 and i >= 2:
                        dve.wait_ge(s_idx, 2 * i - 2)
                    dve.wait_ge(s_sc, m + 1)
                    dve.wait_ge(s_rl, m + 1)
                    b = 2 * (m % 3) * HALF
                    dve.tensor_tensor_reduce(out=m_all[b2][:, start:end], in0=ps[:, b:b + end - start],
                                             in1=gain[:, m % 3, 0:end - start], scale=1.0, scalar=LOWEST,
                                             op0=ALU.add, op1=ALU.max, accum_out=best[:, b2, c // 4, c % 4:c % 4 + 1]).then_inc(s_scu, 1)
                    if c % 4 == 3:
                        half = slice(0, MID) if c == 3 else slice(MID, PAIRS)
                        if i >= 2 and c == 3:
                            dve.wait_ge(s_at, i - 1)
                        dve.wait_ge(s_scu, m + 1)
                        link(dve.max(best8[:, b2, c // 4, :], best[:, b2, c // 4, :]))
                        dve.max_index(at8[:, b2, c // 4, :], best8[:, b2, c // 4, :], m_all[b2][:, half]).then_inc(s_idx, 1)
                    if c == NCH - 1:
                        n[0] += 1
                        dve.tensor_tensor(later[:], best8[:, b2, 1, 0:1], best8[:, b2, 0, 0:1], ALU.is_gt).then_inc(s_dve, 1)
                        dve.wait_ge(s_idx, 2 * i + 2)
                        link(dve.scalar_tensor_tensor(out=apart[:], in0=at8[:, b2, 1, 0:1], scalar=float(MID),
                                                      in1=at8[:, b2, 0, 0:1], op0=ALU.add, op1=ALU.subtract))
                        dve.scalar_tensor_tensor(out=at[:, b2:b2 + 1], in0=apart[:], scalar=later[:, 0:1],
                                                 in1=at8[:, b2, 0, 0:1], op0=ALU.mult, op1=ALU.add).then_inc(s_at, 1)
                    if c == 5 and i >= 1:
                        dot_of(i - 1)
                    if c == 6 and i >= 2:
                        hits_of(i - 2)
            hits_of(NT - 2)
            i, b2 = NT - 1, (NT - 1) % 2
            dve.wait_ge(s_pair[b2], 16 * NT // 2)
            link(dve.tensor_tensor(pair[:, b2, D:], pair[:, b2, D:], pair[:, b2, 0:D], ALU.subtract))
            link(dve.tensor_tensor(pair[:, b2, 0:D], pair[:, b2, D:], q_nat[:, i, :], ALU.mult))
            link(dve.tensor_reduce(dot[:, b2:b2 + 1], pair[:, b2, 0:D], AX.X, ALU.add))
            dve.wait_ge(s_first, NT - 1)
            link(dve.tensor_scalar(odd[:], dot[:, b2:b2 + 1], 0.0, None, ALU.is_gt))
            link(dve.scalar_tensor_tensor(out=idxf[:, i:i + 1], in0=at[:, b2:b2 + 1], scalar=2.0, in1=odd[:],
                                          op0=ALU.mult, op1=ALU.add))
            dve.wait_ge(s_row, i)
            dve.tensor_scalar(diag[:], ident[:], idxf[:, i:i + 1], None, ALU.mult).then_inc(s_diag, 1)
            link(dve.tensor_scalar(junk[:, P:P + i * P], id_row[:, 0:i * P], idxf[:, i:i + 1], 0.0, ALU.is_equal,
                                   ALU.add, accum_out=hits_a[:, i:i + 1]))
            dve.wait_ge(s_rowc, NT)
            link(dve.tensor_tensor(own[:], id_row[:, i * P:(i + 1) * P], not_earlier[:], ALU.add))
            link(dve.tensor_scalar(junk[:, 0:P], own[:], idxf[:, i:i + 1], 0.0, ALU.is_equal, ALU.add,
                                   accum_out=hits_b[:, i:i + 1]))
            link(dve.tensor_scalar(first[:, i:i + 1], hits_b[:, i:i + 1], hits_a[:, i:i + 1], 0.0, ALU.add,
                                   ALU.is_equal))
            dve.tensor_tensor(seen_f[:, i + 1:i + 2], seen_f[:, i:i + 1], first[:, i:i + 1], ALU.add).then_inc(s_first, 1)
            link(dve.tensor_copy(idx_b[:, 0, :], idxf[:]))
            link(dve.tensor_tensor(idx_b[:, 1, :], idxf[:], idx_b[:, 0, :], ALU.subtract))
            dve.wait_ge(s_slot, 1)
            sl = ps[:, 6 * HALF + P:6 * HALF + P + NT + 1]
            dve.tensor_copy(n_rows[:], sl[0:1, NT:NT + 1]).then_inc(s_count, 1)
            link(dve.scalar_tensor_tensor(out=slot[:], in0=sl[:, 0:NT], scalar=1.0, in1=first[:, 0:NT],
                                          op0=ALU.add, op1=ALU.mult))
            link(dve.tensor_tensor(above[:], thr[:, 0:NT].unsqueeze(1).broadcast_to([P, NT, NT]),
                                   slot[:].unsqueeze(2).broadcast_to([P, NT, NT]), ALU.is_lt))
            link(dve.tensor_reduce(slot_t[:], above[:], AX.X, ALU.add))
            link(dve.scalar_tensor_tensor(out=slot_p[:], in0=slot_t[:], scalar=-float(P), in1=slot[:],
                                          op0=ALU.mult, op1=ALU.add))
            link(dve.tensor_scalar(slot_p[:], slot_p[:], float(P), None, ALU.add))
            link(dve.tensor_tensor(pick_t[:, :, 2, :], iota1[:, 0:NT].unsqueeze(1).broadcast_to([P, NT, NT]),
                                   slot_t[:].unsqueeze(2).broadcast_to([P, NT, NT]), ALU.is_equal))
            for k in range(2):
                dve.tensor_tensor(pick_t[:, :, k, :], pick_t[:, :, 2, :],
                                  idx_b[:, k, :].unsqueeze(2).broadcast_to([P, NT, NT]), ALU.mult)
            for i in range(NT):
                dve.tensor_scalar(pick_p[:, i, :], iota1[:], slot_p[:, i:i + 1], None, ALU.is_equal).then_inc(s_pk, 1)
            dve.wait_ge(s_rows, 1)
            link(dve.tensor_copy(row_c[:].rearrange("p k t -> p (k t)"), ps[:, 5 * HALF:5 * HALF + 3 * NT]))
            n[0] += 1
            dve.tensor_scalar(pad[:], row_c[:, 2, :], -1.0, 1.0, ALU.mult, ALU.add).then_inc(s_dve, 1)
            link(dve.tensor_tensor(row_s[:], row_c[:, 0, :], row_c[:, 1, :], ALU.add))
            link(dve.scalar_tensor_tensor(out=row_f[:], in0=pad[:], scalar=id_row[:, 0:1], in1=row_s[:],
                                          op0=ALU.mult, op1=ALU.add))
            link(dve.tensor_copy(row_u[:], row_f[:]))
            dve.sem_inc(s_idxc, 1)

            def attention_dve(T):
                n = [0]

                def link(ins):
                    n[0] += 1
                    ins.then_inc(s_dveb, 1)
                    dve.wait_ge(s_dveb, n[0])

                for t in range(T):
                    n[0] += 1
                    if t:
                        dve.wait_ge(s_dveb, n[0] - 1)
                    dve.tensor_scalar(junk[:], id_row[:], row_f[:, t:t + 1], 0.0, ALU.is_equal, ALU.add,
                                      accum_out=uses[:, t:t + 1]).then_inc(s_dveb, 1)
                dve.wait_ge(s_dveb, n[0])
                link(dve.tensor_tensor(weight_v[:, 0:T], uses[:, 0:T], row_c[:, 2, 0:T], ALU.mult))
                dve.wait_ge(s_kz, 1)
                hk = T * P // 2
                for t in range(T):
                    if t == T - 1:
                        dve.wait_ge(s_mTs, T)
                        dve.tensor_tensor(memT_d[:, 0:hk], memT[:, hk:2 * hk], memT[:, 0:hk], ALU.subtract
                                          ).then_inc(s_md, 1)
                    dve.wait_ge(s_ka, t + 1)
                    c, b, bv = slice(t * P, (t + 1) * P), (2 + t % 2) * HALF, (4 + t % 2) * HALF
                    for j in range(GH):
                        r = slice(RS * j, RS * (j + 1))
                        dve.scalar_tensor_tensor(out=k_blk[r, j, c], in0=ps[r, b:b + P], scalar=k_low[r, 0:1],
                                                 in1=k_a[r, t % 2, :].bitcast(F32), op0=ALU.mult, op1=ALU.add)
                    dve.tensor_copy(v_ext[:, t, DH:DH + 1], weight_v[:, t:t + 1])
                    dve.tensor_scalar(v_ext[:, t, 0:DH], ps[:, bv:bv + DH], weight_v[:, t:t + 1], None, ALU.mult
                                      ).then_inc(s_kb, 1)
                dve.wait_ge(s_kdp, 1)
                dve.wait_ge(s_kda, 1)
                for j in range(GH):
                    r = slice(RS * j, RS * (j + 1))
                    last = dve.scalar_tensor_tensor(out=kd_blk[r, j, 0:hk], in0=ps[r, 0:hk], scalar=k_low[r, 0:1],
                                                    in1=kd_a[r, 0:hk].bitcast(F32), op0=ALU.mult, op1=ALU.add)
                last.then_inc(s_kdb, 1)
                jobs, steps = max_jobs(T), NG * T
                hu = 2 if T <= 4 else 1

                def max_job(m):
                    i, unit = jobs[m]
                    dve.wait_ge(s_p1, m + 1)
                    if unit is not None and by_rise(T, m):
                        dve.wait_ge(s_p1r, rises_before(T, m) + 1)
                        g, j0, j1 = heads_of(T, unit)
                        for j in range(j0, j1):
                            b, k = 2 * place_of(T, m) * HALF + (j - j0) * hk, slice((j - j0) * hk, (j - j0 + 1) * hk)
                            last = dve.tensor_tensor_reduce(out=rise[:, place_of(T, m), k], in0=ps[:, b:b + hk],
                                                            in1=rise[:, place_of(T, m), k], scale=1.0, scalar=LOWEST,
                                                            op0=ALU.add, op1=ALU.max,
                                                            accum_out=mx[:, i, NG * j + g:NG * j + g + 1])
                        last.then_inc(s_p1u, 1)
                    elif unit is not None:
                        g, j0, j1 = heads_of(T, unit)
                        if hu == 2:
                            sc = bank(2 * place_of(T, m), 2).rearrange("p (h k) -> p h k", h=2)[:, :, 0:T * P]
                            to = mx[:, i, :].rearrange("p (j g) -> p j g", j=GH)[:, j0:j1, g]
                        else:
                            sc, to = bank(2 * place_of(T, m), 2), mx[:, i, NG * j0 + g:NG * j0 + g + 1]
                        dve.tensor_reduce(to, sc, AX.X, ALU.max).then_inc(s_p1u, 1)
                    else:
                        c = slice(i * P, (i + 1) * P)
                        mt = ps[0:H, 2 * place_of(T, m) * HALF:2 * place_of(T, m) * HALF + P]
                        link(dve.tensor_scalar(nm_hi[:, c], mt, -1.0, None, ALU.mult))
                        dve.scalar_tensor_tensor(out=nm_lo[:, c], in0=mt, scalar=-1.0, in1=nm_hi[:, c].bitcast(F32),
                                                 op0=ALU.mult, op1=ALU.subtract).then_inc(s_p1u, 1)

                for m in jobs_at(T, -1):
                    max_job(m)
                for period in range(1, NQ + 2):
                    for s in range(steps):
                        if period >= 2 and s >= 2 and s % 2 == 0 and (s - 2) // 4 < TQ:
                            i = TQ * (period - 2) + (s - 2) // 4
                            if (s - 2) % 4 == 0:
                                dve.wait_ge(s_avT, i + 1)
                                a = bank(7).rearrange("p (h d) -> p h d", h=H)
                                link(dve.reciprocal(rden[:], a[:, :, DH]))
                                dve.tensor_tensor(att[:].rearrange("p (h d) -> p h d", h=H), a[:, :, 0:DH],
                                                  rden[:].unsqueeze(2).broadcast_to([P, H, DH]), ALU.mult
                                                  ).then_inc(s_att, 1)
                            else:
                                dve.wait_ge(s_wc, i + 1)
                                dve.scalar_tensor_tensor(out=x1[:, i, :], in0=ps[:, 7 * HALF:7 * HALF + D],
                                                         scalar=gates[:, 0:1], in1=x_sb[:, i, :],
                                                         op0=ALU.mult, op1=ALU.add).then_inc(s_x1, 1)
                                dve.wait_ge(s_x1, i + 1)
                                link(dve.bn_stats(stats[:, i, :], x1[:, i, :]))
                                link(dve.bn_aggr(mv[:, i, :], stats[:, i, :]))
                                if i % 4 == 3:
                                    t = slice(i - 3, i + 1)
                                    dve.tensor_scalar(var_eps[:, t], mv[:, t, 1], EPS, None, ALU.add).then_inc(s_ve, 1)
                        if period == NQ and s == 1:
                            normalise(x1, range(4), 2)
                        for m in (jobs_at(T, (period - 1) * steps + s) if period <= NQ else ()):
                            max_job(m)

            by_count(dve, attention_dve)
            normalise(x1, range(4, NT), 3)
            for half in range(NL):
                t = slice(4 * half, 4 * half + 4)
                dve.wait_ge(s_r, 4 * half + 4)
                logits = ps[:, (6 + half) * HALF:(6 + half) * HALF + 4 * E].rearrange("p (t e) -> p t e", t=4)
                link(dve.tensor_tensor(r8[:, t, :], logits,
                                       consts[:, C_ROW:C_ROW + E].unsqueeze(1).broadcast_to([P, 4, E]), ALU.add))
                for i in range(4 * half, 4 * half + 4):
                    n[0] += 1
                    dve.max(m8[:, i, :], r8[:, i, :]).then_inc(s_dve, 1)
                dve.wait_ge(s_dve, n[0])
                dve.tensor_tensor(below_top[:, t, :], m8[:, t, :], m8[:, t, 0:1].broadcast_to([P, 4, 8]), ALU.subtract
                                  ).then_inc(s_m8, 1)
                for i in range(4 * half, 4 * half + 4):
                    n[0] += 1
                    dve.max_index(i8[:, i, :], m8[:, i, :], r8[:, i, :]).then_inc(s_dve, 1)
            dve.wait_ge(s_dve, n[0])
            link(dve.tensor_copy(i8f[:], i8[:, :, 0:TOPK].rearrange("p t k -> p k t")))
            for k in range(TOPK):
                link(dve.tensor_tensor(pick[:, k], iota8[:].unsqueeze(1).broadcast_to([P, NT, E]),
                                       i8f[:, k, :].unsqueeze(2).broadcast_to([P, NT, E]), ALU.is_equal))
            dve.wait_ge(s_tok, 1)
            link(dve.tensor_tensor(counts[0][:, 4:, :], pick[:, 0], pick[:, 1], ALU.add))
            for k in range(3):
                link(dve.tensor_tensor(counts[k + 1][:, 4:, :], counts[k][:, 4:, :],
                                       counts[k][:, 4 - 2 ** k:4 - 2 ** k + NT, :], ALU.add))
            dve.sem_inc(s_mask, 1)
            dve.wait_ge(s_e8, 1)
            link(dve.tensor_reduce(sum8[:], e8[:], AX.X, ALU.add))
            link(dve.reciprocal(rs8[:], sum8[:]))
            link(dve.tensor_scalar(rs8[:], rs8[:], gates[:, 1:2], None, ALU.mult))
            for k in range(TOPK):
                n[0] += 1
                dve.tensor_tensor(tmpw[:, k, :], e8[:, :, k], rs8[:], ALU.mult).then_inc(s_dve, 1)
            dve.wait_ge(s_pos, 1)
            pos = ps[:, 5 * HALF:5 * HALF + NT * E].rearrange("p (t e) -> p t e", t=NT)
            for k in range(TOPK):
                n[0] += 1
                dve.tensor_tensor(scr[:, k], pick[:, k], pos, ALU.mult).then_inc(s_dve, 1)
            dve.wait_ge(s_dve, n[0])
            link(dve.tensor_reduce(place[:], scr[:].rearrange("p k t e -> p (k t) e"), AX.X, ALU.add))
            n[0] += 1
            dve.tensor_scalar(keep[:], place[:], float(CAP), None, ALU.is_lt).then_inc(s_dve, 1)
            link(dve.scalar_tensor_tensor(out=dest[:], in0=i8f[:].rearrange("p k t -> p (k t)"), scalar=float(CAP),
                                          in1=place[:], op0=ALU.mult, op1=ALU.add))
            n[0] += 1
            dve.tensor_tensor(weight[:], tmpw[:].rearrange("p k t -> p (k t)"), keep[:], ALU.mult).then_inc(s_dve, 1)
            link(dve.scalar_tensor_tensor(out=slot1[:], in0=dest[:], scalar=1.0, in1=keep[:],
                                          op0=ALU.add, op1=ALU.mult))
            kt = TOPK * NT
            link(dve.tensor_tensor(above_s[:], thr[:].unsqueeze(1).broadcast_to([P, kt, NS]),
                                   slot1[:].unsqueeze(2).broadcast_to([P, kt, NS]), ALU.is_lt))
            link(dve.tensor_reduce(slot_a[:], above_s[:], AX.X, ALU.add))
            n[0] += 1
            dve.tensor_tensor(pick_a[:], iota1[:, 0:NS].unsqueeze(1).broadcast_to([P, kt, NS]),
                              slot_a[:].unsqueeze(2).broadcast_to([P, kt, NS]), ALU.is_equal).then_inc(s_dve, 1)
            link(dve.scalar_tensor_tensor(out=slot_b[:], in0=slot_a[:], scalar=-float(P), in1=slot1[:],
                                          op0=ALU.mult, op1=ALU.add))
            n[0] += 1
            dve.tensor_scalar(slot_b[:], slot_b[:], float(P), None, ALU.add).then_inc(s_dve, 1)
            dve.tensor_scalar(pick_id[:, :, 0, :], pick_a[:], tok1[:, 0:1], None, ALU.mult)
            dve.tensor_tensor(pick_id[:, :, 1, :], pick_a[:], tile_of[:].unsqueeze(2).broadcast_to([P, kt, NS]), ALU.mult)
            dve.wait_ge(s_dve, n[0])
            for i in range(kt):
                dve.tensor_scalar(pick_b[:, i, :], iota1_b[:], slot_b[:, i:i + 1], None, ALU.is_equal).then_inc(s_pb, 1)
            dve.wait_ge(s_in, 1)
            link(dve.tensor_copy(info_id[:].rearrange("p k s -> p (k s)"), ps[:, 5 * HALF:5 * HALF + 2 * NS]))
            for t in range(NS):
                for k in range(2):
                    last = dve.tensor_scalar(info_diag[:, k, t, :], ident_b[:], info_id[:, k, t:t + 1], None, ALU.mult)
                last.then_inc(s_idg, 1)
            n[0] += 1
            dve.scalar_tensor_tensor(out=info[:, 0, :], in0=info_id[:, 1, :], scalar=float(P), in1=info_id[:, 0, :],
                                     op0=ALU.mult, op1=ALU.add).then_inc(s_dve, 1)
            for b in range(0, SLOTS, HALF):
                dve.wait_ge(s_trc, b // HALF + 1)
                w = min(HALF, SLOTS - b)
                for i in range(NT):
                    if b:
                        dve.wait_ge(s_putu, (b // HALF - 1) * NT + i + 1)
                    dve.tensor_scalar(put[:, i, 0:w], tok_of[:, b:b + w], tok1[:, i:i + 1], None, ALU.is_equal
                                      ).then_inc(s_put, 1)
            link(dve.tensor_copy(weight_b[:, 0], weight[:]))
            link(dve.tensor_tensor(weight_r[:, 0], weight[:], weight_b[:, 0], ALU.subtract))
            link(dve.tensor_copy(weight_b[:, 1], weight_r[:, 0]))
            link(dve.tensor_tensor(weight_r[:, 1], weight_r[:, 0], weight_b[:, 1], ALU.subtract))
            link(dve.tensor_copy(weight_b[:, 2], weight_r[:, 1]))
            for k in range(3):
                last = dve.tensor_tensor(pick_w[:, :, k, :], pick_a[:],
                                         weight_b[:, k, :].unsqueeze(2).broadcast_to([P, kt, NS]), ALU.mult)
            last.then_inc(s_pw, 1)
            dve.wait_ge(s_inw, 1)
            link(dve.tensor_copy(info_w[:].rearrange("p k s -> p (k s)"), ps[:, 6 * HALF:6 * HALF + 3 * NS]))
            link(dve.tensor_tensor(info_s[:], info_w[:, 0, :], info_w[:, 1, :], ALU.add))
            link(dve.tensor_tensor(info[:, 1, :], info_s[:], info_w[:, 2, :], ALU.add))
            dve.sem_inc(s_iw, 1)
            dve.wait_ge(s_tok, 2)
            rows_done = 0
            for e in range(E + 2):
                for t in (done_with[e] if e < E else ()):
                    dve.tensor_scalar(get[:, t, :], tok1_row[:], info[:, 0, t:t + 1], None, ALU.is_equal)
                if 1 <= e <= E:
                    dve.wait_ge(s_e2, e)
                    dve.tensor_scalar(eoT[:, (e - 1) * CAP:e * CAP], ps[:, 5 * HALF:5 * HALF + CAP],
                                      consts[:, C_B + (E + 2) * KH + e - 1:C_B + (E + 2) * KH + e], None, ALU.add
                                      ).then_inc(s_e2s, 1)
                if e >= 2 and e - 2 in groups:
                    rows_done += len(done_with[e - 2])
                    dve.wait_ge(s_eh, rows_done)
                    for k, t in enumerate(done_with[e - 2]):
                        dve.scalar_tensor_tensor(out=eo[:, t, 1, :], in0=ps[:, 6 * HALF + k * P:6 * HALF + (k + 1) * P],
                                                 scalar=info[:, 1, t:t + 1], in1=eo[:, t, 0, :].bitcast(F32),
                                                 op0=ALU.mult, op1=ALU.subtract).then_inc(s_eo, 1)
            def out_rows(c):
                t, b = slice(2 * c, 2 * c + 2), combine_at(2 * c)
                low = ps[:, b:b + HALF].rearrange("p (t k d) -> p t k d", t=2, k=2)[:, :, 1, :]
                dve.wait_ge(s_acc, c + 1)
                dve.tensor_tensor(fin[:, t, :], low, acc[:, t, :], ALU.add).then_inc(s_fin, 2)

            for c in range(NT // 2):
                t, b = slice(2 * c, 2 * c + 2), combine_at(2 * c)
                high = ps[:, b:b + HALF].rearrange("p (t k d) -> p t k d", t=2, k=2)[:, :, 0, :]
                dve.wait_ge(s_cmb, c + 1)
                dve.tensor_tensor(acc[:, t, :], high, x1[:, t, :], ALU.add).then_inc(s_acc, 1)
                if c:
                    out_rows(c - 1)
            out_rows(NT // 2 - 1)

        @block.tensor
        def _(pe):
            b5, b7 = 5 * HALF, 7 * HALF
            pe.wait_ge(s_const, 1)
            pe.wait_ge(s_wql, 16)
            pe.transpose(ps[:, 3 * HALF + C_WQ:3 * HALF + C_WQ + D], wq_nat[:], ident[:]).then_inc(s_cT, 1)
            def turn_kv(jobs):
                for k in jobs:
                    g, part = divmod(k, 2)
                    if k >= 2:
                        pe.wait_ge(s_klo, k - 1)
                    for t in range(4 * g, min(4 * g + 4, NKV)):
                        pe.wait_ge(s_kd, t // KV_PIECE + 1)
                        r = P if t < NKV - 1 else TAIL
                        col = (6 + part) * HALF + (t - 4 * g) * P
                        last = pe.transpose(ps[:, col:col + r], kv_nat[0:r, t, part, :], ident[0:r, 0:r])
                    last.then_inc(s_kvT, 1)

            turn_kv(turns(-1))
            for half in range(NL):
                pe.wait_ge(s_xn, 4 * (half + 1))
                for t in range(4):
                    last = pe.transpose(ps[:, (4 + half) * HALF + t * P:(4 + half) * HALF + (t + 1) * P],
                                        xn[:, 4 * half + t, :], ident[:])
                last.then_inc(s_xT, 1)
            pe.wait_ge(s_cs, 1)
            for half in range(NL):
                pe.wait_ge(s_xTs, half + 1)
                pe.matmul(bank(4 + half), consts[:, C_WQ:C_WQ + D], xnT[:, half * HALF:(half + 1) * HALF],
                          start=True, stop=True).then_inc(s_qp, 1)
            turn_kv(turns(0))
            for half in range(NL):
                pe.wait_ge(s_qlo, half + 1)
                for t in range(4):
                    last = pe.matmul(ps[:, (4 + half) * HALF + t * P:(4 + half) * HALF + (t + 1) * P],
                                     xnT[:, half * HALF + t * P:half * HALF + (t + 1) * P], consts[:, C_WQ:C_WQ + D],
                                     start=True, stop=True)
                last.then_inc(s_qnp, 1)

            def small_operands():
                pe.wait_ge(s_const, 2)
                pe.wait_ge(s_small, 16 * 9)
                pe.wait_ge(s_klo, 2 * NKG)
                pe.transpose(ps[:, b7 + C_WC:b7 + C_WC + D], wc_nat[:], ident[:])
                pe.transpose(ps[:, b7 + C_WKV:b7 + C_WKV + 2 * DH], wkv_nat[:], ident[0:2 * DH, 0:2 * DH])
                nb = E * KH + 2 * KH + E
                pe.transpose(ps[:, b7 + C_B:b7 + C_B + nb], bias_nat[:], ident[0:nb, 0:nb])
                pe.matmul(ps[:, b7 + C_ROW:b7 + C_ROW + 10], ones[0:1, :], row10[:], start=True, stop=True
                          ).then_inc(s_cT, 1)

            def index_row(i):
                pe.wait_ge(s_diag, i + 1)
                if i:
                    pe.wait_ge(s_rowc, i)
                pe.matmul(ps[:, 6 * HALF:6 * HALF + P], ones[:], diag[:], start=True, stop=True).then_inc(s_row, 1)

            def side_jobs(i):
                if i >= 2:
                    index_row(i - 2)
                g, half = (i - 1) // NL, (i - 1) % NL
                pe.wait_ge(s_cs, 5)
                if i >= 2:
                    pe.wait_ge(s_qa, i - 1)
                pe.matmul(bank(7), wq_rep[:, GH * g:GH * (g + 1), :].rearrange("p j r -> p (j r)"),
                          xnT[:, half * HALF:(half + 1) * HALF], start=True, stop=True).then_inc(s_q4, 1)

            for i in range(NT):
                q_h, q_l = q_hi[:, i * P:(i + 1) * P], q_lo[:, i * P:(i + 1) * P]
                for c, (start, end) in enumerate(CHUNKS):
                    if i == 0:
                        if c:
                            turn_kv(turns(c))
                        pe.wait_ge(s_klo, turns(c).start)
                    m = i * NCH + c
                    if m == 0:
                        pe.wait_ge(s_qn, NL)
                    if m >= 3:
                        pe.wait_ge(s_scu, m - 2)
                    for part, done in ((1, s_scd), (0, s_sc)):
                        b = (2 * (m % 3) + part) * HALF
                        o = ps[:, b:b + end - start]
                        hi, lo = kvt_hi[part][:, start:end], kvt_lo[part][:, start:end]
                        pe.matmul(o, q_h, hi, start=True, stop=False)
                        pe.matmul(o, q_h, lo, start=False, stop=False)
                        pe.matmul(o, q_l, hi, start=False, stop=True).then_inc(done, 1)
                    if c == 2 and i >= 1:
                        side_jobs(i)
                if i == 0:
                    small_operands()
            side_jobs(NT)
            index_row(NT - 1)

            pe.wait_ge(s_first, NT)
            pe.wait_ge(s_rowc, NT)
            sl = ps[:, 6 * HALF + P:6 * HALF + P + NT + 1]
            pe.matmul(sl, below_b[:], first[:], start=True, stop=False)
            pe.matmul(sl, all_b[:], seen_f[:], start=False, stop=True).then_inc(s_slot, 1)
            pe.wait_ge(s_scu, NT * NCH)
            for i in range(NT):
                pe.wait_ge(s_pk, i + 1)
                last = pe.matmul(ps[:, 5 * HALF:5 * HALF + 3 * NT], pick_p[:, i, :],
                                 pick_t[:, i].rearrange("p k t -> p (k t)"), start=(i == 0), stop=(i == NT - 1))
            last.then_inc(s_rows, 1)

            def hidden_products(layer, half, k):
                n = KH * half + k
                cols = slice(half * HALF, (half + 1) * HALF)
                if layer == 1:
                    if half:
                        pe.wait_ge(s_h2s, n - 3)
                    pe.matmul(bank(n % 4), rw1_sb[:, k * P:(k + 1) * P], xnT[:, cols], start=True, stop=True
                              ).then_inc(s_h1, 1)
                    return
                pe.wait_ge(s_h1s, KH * (half + 1))
                for c in range(KH):
                    last = pe.matmul(bank(n % 4), rw2_sb[:, c, k * P:(k + 1) * P], h1[:, c, cols],
                                     start=(c == 0), stop=(c == KH - 1))
                last.then_inc(s_h2, 1)

            def turn_xn(half):
                pe.wait_ge(s_xn, NT + 4 * (half + 1))
                for t in range(4):
                    last = pe.transpose(ps[:, (4 + half) * HALF + t * P:(4 + half) * HALF + (t + 1) * P],
                                        xn[:, 4 * half + t, :], ident[:])
                last.then_inc(s_xT, 1)

            def attention_pe(T):
                for t in range(T + 1):
                    if t < T:
                        pe.wait_ge(s_mem[t % 4], 16 * (t // 4 + 1))
                        if t >= 2:
                            pe.wait_ge(s_mTs, t - 1)
                        pe.transpose(ps[:, (t % 2) * HALF:(t % 2) * HALF + P], mem[:, t, :], ident[:]).then_inc(s_mT, 1)
                    if t:
                        k = t - 1
                        pe.wait_ge(s_mTs, t)
                        if k >= 2:
                            pe.wait_ge(s_kb, k - 1)
                        else:
                            pe.wait_ge(s_idxc, 1)
                        b, bv = (2 + k % 2) * HALF, (4 + k % 2) * HALF
                        pe.matmul(ps[:, b:b + P], wk_rep[:].rearrange("p j r -> p (j r)"), memT[:, k * P:(k + 1) * P],
                                  start=True, stop=True)
                        pe.matmul(ps[:, bv:bv + DH], memT[:, k * P:(k + 1) * P], consts[:, C_WKV + DH:C_WKV + 2 * DH],
                                  start=True, stop=True).then_inc(s_mkv, 1)
                hk = T * P // 2
                pe.wait_ge(s_md, 1)
                pe.matmul(ps[:, 0:hk], wk_rep[:].rearrange("p j r -> p (j r)"), memT_d[:, 0:hk], start=True, stop=True
                          ).then_inc(s_kdp, 1)
                pe.wait_ge(s_kb, T)
                pe.wait_ge(s_kdb, 1)
                pe.wait_ge(s_q4u, NT)
                jobs, steps, n = max_jobs(T), NG * T, 0
                hu = 2 if T <= 4 else 1

                def weigh(u):
                    group, t = divmod(u, T)
                    pe.wait_ge(s_ex, (GH // HB) * (u + 1))
                    if t == 0 and group:
                        pe.wait_ge(s_avc, group)
                    for j in range(GH):
                        last = pe.matmul(ps[RS * j:RS * (j + 1), 6 * HALF:6 * HALF + W], v_ext[:, t, :],
                                         probs[:, u % 2, j, :], start=(t == 0), stop=(t == T - 1),
                                         skip_group_check=True)
                    last.then_inc(s_avd, 1)

                def max_job(m):
                    i, unit = jobs[m]
                    opening = len(jobs_at(T, -1))
                    if m < opening:
                        if m >= 4:
                            pe.wait_ge(s_p1u, m - 3)
                    else:
                        pe.wait_ge(s_p1u, max(opening, m - 1))
                    if unit is None:
                        pe.wait_ge(s_p1u, m if m == len(jobs) - 1 else m - 1)
                        pe.transpose(ps[0:H, 2 * place_of(T, m) * HALF:2 * place_of(T, m) * HALF + P], mx[:, i, :], ident[:]
                                     ).then_inc(s_p1, 1)
                        return
                    g, j0, j1 = heads_of(T, unit)
                    if by_rise(T, m):
                        for b, keys, done in ((2 * place_of(T, m) + 1, kd_blk, s_p1d), (2 * place_of(T, m), k_blk, s_p1)):
                            o = ps[:, b * HALF:b * HALF + hu * hk].rearrange("p (j k) -> p j k", j=hu)
                            pe.matmul(o, q_rows[:, g, i * P:(i + 1) * P], keys[:, j0:j1, 0:hk], start=True, stop=True
                                      ).then_inc(done, 1)
                        return
                    for j in range(j0, j1):
                        for c in range(0, T * P, HALF):
                            w = min(HALF, T * P - c)
                            b = 2 * place_of(T, m) + j - j0 + c // HALF
                            last = pe.matmul(ps[:, b * HALF:b * HALF + w], q_rows[:, g, i * P:(i + 1) * P],
                                             k_blk[:, j, c:c + w], start=True, stop=True)
                    last.then_inc(s_p1, 1)

                for m in jobs_at(T, -1):
                    max_job(m)
                for period in range(1, NQ + 2):
                    for s in range(steps):
                        take = jobs_at(T, (period - 1) * steps + s) if period <= NQ else ()
                        for m in take[:1]:
                            max_job(m)
                        if period <= NQ:
                            q = period - 1
                            g, t = divmod(s, T)
                            if s == 0:
                                pe.wait_ge(s_nmrow[q], 32)
                            if period == 1 and s == 0:
                                pe.wait_ge(s_p1u, len(jobs_at(T, -1)))
                            for b in range(GH // HB):
                                if n >= 2:
                                    pe.wait_ge(s_ex, n - 1)
                                for j in range(b * HB, (b + 1) * HB):
                                    col = (4 + n % 2) * HALF + (j - b * HB) * W
                                    last = pe.matmul(ps[:, col:col + W], k_blk[:, j, t * P:(t + 1) * P],
                                                     q_rows[:, g, q * W:(q + 1) * W], start=True, stop=True)
                                last.then_inc(s_lg, 1)
                                n += 1
                        for m in take[1:]:
                            max_job(m)
                        u = (period - 1) * steps + s
                        if 1 <= u <= NQ * steps:
                            weigh(u - 1)
                        if period == NQ + 1 and s == 0:
                            turn_xn(0)
                            pe.wait_ge(s_w, 16 * 5)
                            pe.wait_ge(s_p1u, len(jobs))
                            pe.wait_ge(s_nmrow[NQ - 1], 32)
                            pe.wait_ge(s_xTs, NL + 1)
                        if period >= 2 and s >= 1 and (s - 1) // 4 < TQ:
                            i = TQ * (period - 2) + (s - 1) // 4
                            part = (s - 1) % 4
                            if part == 0:
                                pe.wait_ge(s_avc, NG * (period - 1))
                                if i:
                                    pe.wait_ge(s_x1, i)
                                for g in range(NG):
                                    last = pe.transpose(ps[:, b7 + g * P:b7 + (g + 1) * P],
                                                        av[:, period % 2, g, (i % TQ) * P:(i % TQ + 1) * P], ident[:])
                                last.then_inc(s_avT, 1)
                            elif part == 1:
                                pe.wait_ge(s_att, i + 1)
                                pe.transpose(ps[:, b7:b7 + P], att[:], ident[:]).then_inc(s_attT, 1)
                            elif part == 2:
                                pe.wait_ge(s_attTs, i + 1)
                                pe.matmul(ps[:, b7:b7 + D], attT[:], consts[:, C_WC:C_WC + D], start=True, stop=True
                                          ).then_inc(s_wc, 1)
                        if period == NQ + 1:
                            for layer, k in HIDDEN_AT.get(s, ()):
                                hidden_products(layer, 0, k)

            by_count(pe, attention_pe)
            hidden_products(2, 0, 3)
            turn_xn(1)
            pe.wait_ge(s_xTs, NL + 2)
            for k in range(KH):
                hidden_products(1, 1, k)
            def router_products(tiles):
                for i in tiles:
                    pe.wait_ge(s_h2s, KH * (i // 4 + 1))
                    for c in range(KH):
                        o = (6 + i // 4) * HALF + (i % 4) * E
                        last = pe.matmul(ps[:, o:o + E], h2[:, c, i * P:(i + 1) * P],
                                         rw3_sb[:, c, :], start=(c == 0), stop=(c == KH - 1))
                    last.then_inc(s_r, 1)

            router_products(range(4))
            for k in range(KH):
                hidden_products(2, 1, k)
            router_products(range(4, NT))
            pe.wait_ge(s_mask, 1)
            pe.matmul(ps[:, 5 * HALF:5 * HALF + NT * E], below[:], counts[0][:, 4:, :].rearrange("p t e -> p (t e)"),
                      start=True, stop=False)
            pe.matmul(ps[:, 5 * HALF:5 * HALF + NT * E], ones[:],
                      counts[3][:, 3:3 + NT, :].rearrange("p t e -> p (t e)"), start=False, stop=True).then_inc(s_pos, 1)
            for i in range(TOPK * NT):
                pe.wait_ge(s_pb, i + 1)
                last = pe.matmul(ps[:, 5 * HALF:5 * HALF + 2 * NS], pick_b[:, i, :],
                                 pick_id[:, i].rearrange("p k s -> p (k s)"), start=(i == 0),
                                 stop=(i == TOPK * NT - 1))
            last.then_inc(s_in, 1)
            for b in range(3):
                for t in range(4 * b, min(4 * b + 4, NS)):
                    pe.wait_ge(s_idg, t + 1)
                    for k in range(2):
                        last = pe.matmul(ps[:, t * P:(t + 1) * P], ones_b[:, k, :], info_diag[:, k, t, :],
                                         start=(k == 0), stop=(k == 1))
                last.then_inc(s_tr, 1)
            pe.wait_ge(s_xl, 1)
            for b in range(0, SLOTS, HALF):
                pe.wait_ge(s_trc, b // HALF + 1)
                w = min(HALF, SLOTS - b)
                for i in range(NT):
                    pe.wait_ge(s_put, (b // HALF) * NT + i + 1)
                    for part in (xn_hi, xn_lo):
                        last = pe.matmul(ps[:, b:b + w], part[:, i, :], put[:, i, 0:w],
                                         start=(i == 0 and part is xn_hi), stop=(i == NT - 1 and part is xn_lo))
                    last.then_inc(s_putu, 1)
            rows_done = 0
            for e in range(E + 3):
                if e == 1:
                    pe.wait_ge(s_pw, 1)
                    for i in range(TOPK * NT):
                        last = pe.matmul(ps[:, 6 * HALF:6 * HALF + 3 * NS], pick_b[:, i, :],
                                         pick_w[:, i].rearrange("p k s -> p (k s)"), start=(i == 0), stop=(i == TOPK * NT - 1))
                    last.then_inc(s_inw, 1)
                for k in range(KH):
                    if e < E:
                        m = KH * e + k
                        pe.wait_ge(s_dTs, -(-(e + 1) * CAP // HALF))
                        if m >= 2:
                            pe.wait_ge(s_e1s, m - 1)
                        b = 3 + m % 2
                        pe.matmul(ps[:, b * HALF:b * HALF + CAP], ew1_sb[:, e, k * P:(k + 1) * P],
                                  dT[:, e * CAP:(e + 1) * CAP], start=True, stop=True).then_inc(s_e1, 1)
                    if 1 <= e <= E:
                        pe.wait_ge(s_e1s, KH * (e - 1) + k + 1)
                        if e >= 2 and k == 0:
                            pe.wait_ge(s_e2s, e - 1)
                        last = pe.matmul(ps[:, 5 * HALF:5 * HALF + CAP], ew2_sb[:, e - 1, k, :], hh[:, (e - 1) % 2, k, :],
                                         start=(k == 0), stop=(k == KH - 1))
                        if k == KH - 1:
                            last.then_inc(s_e2, 1)
                if e >= 3 and e - 3 in groups:
                    rows_done += len(done_with[e - 3])
                if e >= 2 and e - 2 in groups:
                    pe.wait_ge(s_e2s, e - 1)
                    if rows_done:
                        pe.wait_ge(s_eo, rows_done)
                    else:
                        pe.wait_ge(s_iw, 1)
                    for n, t in enumerate(done_with[e - 2]):
                        last = pe.transpose(ps[:, 6 * HALF + n * P:6 * HALF + (n + 1) * P], eoT[:, t * P:(t + 1) * P], ident[:])
                    last.then_inc(s_eT, 1)
                if e >= 3 and e - 3 in groups:
                    pe.wait_ge(s_eo, rows_done)
                    for t in done_with[e - 3]:
                        for i in range(NT):
                            c = combine_at(i)
                            last = pe.matmul(ps[:, c:c + 2 * D], get[:, t, i * P:(i + 1) * P],
                                             eo[:, t].rearrange("p k d -> p (k d)"), start=(t == 0 and i % 2 == 0),
                                             stop=(t == NS - 1 and i % 2 == 1), skip_group_check=True)
                            if t == NS - 1 and i % 2 == 1:
                                last.then_inc(s_cmb, 1)


_INS = ['x', 'ctx_1024', 'g_xattn', 'g_ffn', 'L0_xattn_Wq', 'L0_xattn_Wkv', 'L0_xattn_Wc', 'L0_ffn_rW1', 'L0_ffn_rb1',
        'L0_ffn_rW2', 'L0_ffn_rb2', 'L0_ffn_rW3', 'L0_ffn_rb3', 'L0_ffn_eW1', 'L0_ffn_eb1', 'L0_ffn_eW2', 'L0_ffn_eb2']


def kernel(**inputs):
    import numpy as _np
    import concourse.bacc as _bacc
    from concourse import mybir as _mybir
    from concourse.bass_utils import run_bass_kernel_spmd as _run

    nc = _bacc.Bacc("TRN2", target_bir_lowering=False, num_devices=1)
    arrays, args = {}, []
    for name in _INS:
        a = _np.ascontiguousarray(inputs[name])
        arrays[f"in_{name}_dram"] = a
        args.append(nc.dram_tensor(f"in_{name}_dram", a.shape, _mybir.dt.from_np(a.dtype), kind="ExternalInput").ap())
    args.append(nc.dram_tensor("out_0_dram", (1, TOK, D), _mybir.dt.float32, kind="ExternalOutput").ap())
    program(nc, *args)
    r = _run(nc, [arrays], core_ids=[0])
    return r.results[0]["out_0_dram"]
```
